# Optimizing a Trainium2 kernel written in Bass

```python
import numpy as np
import jax
import jax.numpy as jnp

def _softmax(x, axis=-1):
    return jax.nn.softmax(x, axis=axis)

def _gelu(x):
    return jax.nn.gelu(x, approximate=True)

def _silu(x):
    return jax.nn.silu(x)

def _sigmoid(x):
    return jax.nn.sigmoid(x)

def _layernorm(x, axis=-1, eps=1e-05):
    m = jnp.mean(x, axis=axis, keepdims=True)
    v = jnp.var(x, axis=axis, keepdims=True)
    return (x - m) / jnp.sqrt(v + eps)

def _scatter_add(tgt, idx, src, axis=0):
    return tgt.at[idx].add(src)

def _segment_sum(src, seg, n):
    return jax.ops.segment_sum(src, seg, n)
kernel_name = 'mk_seq_postln_d2_jaxref_r8_4cc7a8'

def setup_inputs(seed: int=0):
    np.random.seed(seed)
    _w = jnp.asarray

    def _L0_attn_setup():
        import jax, jax.numpy as jnp
        import numpy as np
        B, S, D = (2, 1024, 128)
        NH = 4
        DH = D // NH
        DHID = 2 * DH
        CHUNK = 256
        BASE_LR_INV = float(np.log(np.expm1(0.001)))
        NS_COEFFS = ((4.0848, -6.8946, 2.927), (3.9505, -6.3029, 2.6377), (3.7418, -5.5913, 2.3037), (2.8769, -3.1427, 1.2046), (2.8366, -3.0525, 1.2012))

        def rms_norm(x, w, eps=1e-06):
            return x * jax.lax.rsqrt(jnp.mean(x * x, axis=-1, keepdims=True) + eps) * w

        def l2_normalize(x):
            return x / (jnp.linalg.norm(x, axis=-1, keepdims=True) + 1e-05)

        def silu(x):
            return x * jax.nn.sigmoid(x)

        def newton_schulz5(G):
            trans = G.shape[1] > G.shape[2]
            X = jnp.swapaxes(G, 1, 2) if trans else G
            X = X / (jnp.linalg.norm(X, axis=(1, 2), keepdims=True) + 1e-07)
            for a, b, c in NS_COEFFS:
                A = X @ jnp.swapaxes(X, 1, 2)
                Bm = b * A + c * (A @ A)
                X = a * X + Bm @ X
            return jnp.swapaxes(X, 1, 2) if trans else X
        ks = jax.random.split(jax.random.key(seed), 8)
        f32 = jnp.float32
        return {'hidden_states': jax.random.normal(ks[0], (B, S, D), f32), 'qkv_w': jax.random.normal(ks[1], (3 * D, D), f32) / np.sqrt(D), 'q_norm_w': jnp.ones((D,), f32), 'k_norm_w': jnp.ones((D,), f32), 'lr_proj_w': jax.random.normal(ks[2], (3 * NH, D), f32) / np.sqrt(D), 'lr_proj_b': jnp.zeros((3 * NH,), f32), 'w0': jax.random.normal(ks[3], (NH, DHID, DH), f32) / np.sqrt(DH), 'w1': jax.random.normal(ks[4], (NH, DH, DHID), f32) / np.sqrt(DHID), 'w2': jax.random.normal(ks[5], (NH, DHID, DH), f32) / np.sqrt(DH)}
    _L0_attn_in = _L0_attn_setup()

    def _L0_ffn_setup():
        import math
        import jax, jax.numpy as jnp
        import numpy as np
        D_MODEL = 128
        D_FF = 512
        N_EXPERTS = 8
        CAPACITY_FACTOR = 1.25
        L, B = (64, 8)

        def _route(tokens, router_w):
            T = tokens.shape[0]
            E = router_w.shape[0]
            capacity = int(math.ceil(T / E * CAPACITY_FACTOR))
            logits = tokens @ router_w.T
            probs = jax.nn.softmax(logits, axis=-1)
            top1_idx = jnp.argmax(probs, axis=-1)
            top1_prob = jnp.max(probs, axis=-1)
            order = jnp.lexsort((-top1_prob, top1_idx))
            sorted_e = top1_idx[order]
            counts = jnp.bincount(top1_idx, length=E)
            start = jnp.cumsum(counts) - counts
            pos_in_group = jnp.arange(T) - start[sorted_e]
            keep_sorted = pos_in_group < capacity
            keep = jnp.zeros((T,), bool).at[order].set(keep_sorted)
            return jnp.where(keep, top1_idx, 0).astype(jnp.int32)
        key = jax.random.key(seed)
        ks = jax.random.split(key, 6)
        s_in = 1.0 / math.sqrt(D_MODEL)
        s_ff = 1.0 / math.sqrt(D_FF)
        return {'x': jax.random.normal(ks[0], (L, B, D_MODEL), dtype=jnp.float32), 'router_w': jax.random.uniform(ks[1], (N_EXPERTS, D_MODEL), minval=-s_in, maxval=s_in), 'W1': jax.random.uniform(ks[2], (N_EXPERTS, D_MODEL, D_FF), minval=-s_in, maxval=s_in), 'b1': jax.random.uniform(ks[3], (N_EXPERTS, D_FF), minval=-s_in, maxval=s_in), 'W2': jax.random.uniform(ks[4], (N_EXPERTS, D_FF, D_MODEL), minval=-s_ff, maxval=s_ff), 'b2': jax.random.uniform(ks[5], (N_EXPERTS, D_MODEL), minval=-s_ff, maxval=s_ff)}
    _L0_ffn_in = _L0_ffn_setup()

    def _L1_attn_setup():
        import jax, jax.numpy as jnp
        import numpy as np
        N_HEADS = 16
        HEAD_DIM = 64
        DIM = 128
        BATCH = 2
        SEQ = 256
        key = jax.random.key(seed)
        ks = jax.random.split(key, 6)
        hd = N_HEADS * HEAD_DIM
        scale_in = 1.0 / np.sqrt(DIM)
        scale_out = 1.0 / np.sqrt(hd)
        return {'x': jax.random.normal(ks[0], (BATCH, SEQ, DIM), dtype=jnp.float32), 'Wq': jax.random.normal(ks[1], (DIM, hd), dtype=jnp.float32) * scale_in, 'Wk': jax.random.normal(ks[2], (DIM, hd), dtype=jnp.float32) * scale_in, 'Wv': jax.random.normal(ks[3], (DIM, hd), dtype=jnp.float32) * scale_in, 'Wo': jax.random.normal(ks[4], (hd, DIM), dtype=jnp.float32) * scale_out, 'bo': jnp.zeros((DIM,), dtype=jnp.float32)}
    _L1_attn_in = _L1_attn_setup()

    def _L1_ffn_setup():
        import jax, jax.numpy as jnp
        import numpy as np
        B, S, D, E, F, K = (4, 128, 128, 8, 352, 1)
        key = jax.random.key(seed)
        ks = jax.random.split(key, 8)
        sc = 0.02
        return {'x_bsD': jax.random.normal(ks[0], (B, S, D), jnp.float32), 'router_DE': jax.random.normal(ks[1], (D, E), jnp.float32) * sc, 'w1_eDF': jax.random.normal(ks[2], (E, D, F), jnp.float32) * sc, 'w3_eDF': jax.random.normal(ks[3], (E, D, F), jnp.float32) * sc, 'w2_eFD': jax.random.normal(ks[4], (E, F, D), jnp.float32) * sc, 'ws1_DF': jax.random.normal(ks[5], (D, F), jnp.float32) * sc, 'ws3_DF': jax.random.normal(ks[6], (D, F), jnp.float32) * sc, 'ws2_FD': jax.random.normal(ks[7], (F, D), jnp.float32) * sc}
    _L1_ffn_in = _L1_ffn_setup()
    _d = {'L0_attn_hidden_states': _L0_attn_in['hidden_states'], 'L0_attn_qkv_w': _L0_attn_in['qkv_w'], 'L0_attn_q_norm_w': _L0_attn_in['q_norm_w'], 'L0_attn_k_norm_w': _L0_attn_in['k_norm_w'], 'L0_attn_lr_proj_w': _L0_attn_in['lr_proj_w'], 'L0_attn_lr_proj_b': _L0_attn_in['lr_proj_b'], 'L0_attn_w0': _L0_attn_in['w0'], 'L0_attn_w1': _L0_attn_in['w1'], 'L0_attn_w2': _L0_attn_in['w2'], 'L0_ffn_router_w': _L0_ffn_in['router_w'], 'L0_ffn_W1': _L0_ffn_in['W1'], 'L0_ffn_b1': _L0_ffn_in['b1'], 'L0_ffn_W2': _L0_ffn_in['W2'], 'L0_ffn_b2': _L0_ffn_in['b2'], 'L1_attn_Wq': _L1_attn_in['Wq'], 'L1_attn_Wk': _L1_attn_in['Wk'], 'L1_attn_Wv': _L1_attn_in['Wv'], 'L1_attn_Wo': _L1_attn_in['Wo'], 'L1_attn_bo': _L1_attn_in['bo'], 'L1_ffn_router_DE': _L1_ffn_in['router_DE'], 'L1_ffn_w1_eDF': _L1_ffn_in['w1_eDF'], 'L1_ffn_w3_eDF': _L1_ffn_in['w3_eDF'], 'L1_ffn_w2_eFD': _L1_ffn_in['w2_eFD'], 'L1_ffn_ws1_DF': _L1_ffn_in['ws1_DF'], 'L1_ffn_ws3_DF': _L1_ffn_in['ws3_DF'], 'L1_ffn_ws2_FD': _L1_ffn_in['ws2_FD']}
    _x0 = _d['L0_attn_hidden_states']
    _d['L0_attn_hidden_states'] = jax.random.normal(jax.random.fold_in(jax.random.key(seed), 1), (1, 2048, 128), dtype=_x0.dtype)
    del _x0
    return _d

def reference(L0_attn_hidden_states, L0_attn_qkv_w, L0_attn_q_norm_w, L0_attn_k_norm_w, L0_attn_lr_proj_w, L0_attn_lr_proj_b, L0_attn_w0, L0_attn_w1, L0_attn_w2, L0_ffn_router_w, L0_ffn_W1, L0_ffn_b1, L0_ffn_W2, L0_ffn_b2, L1_attn_Wq, L1_attn_Wk, L1_attn_Wv, L1_attn_Wo, L1_attn_bo, L1_ffn_router_DE, L1_ffn_w1_eDF, L1_ffn_w3_eDF, L1_ffn_w2_eFD, L1_ffn_ws1_DF, L1_ffn_ws3_DF, L1_ffn_ws2_FD):

    def _L0_attn_ref(hidden_states, qkv_w, q_norm_w, k_norm_w, lr_proj_w, lr_proj_b, w0, w1, w2):
        import jax, jax.numpy as jnp
        import numpy as np
        B, S, D = (2, 1024, 128)
        NH = 4
        DH = D // NH
        DHID = 2 * DH
        CHUNK = 256
        BASE_LR_INV = float(np.log(np.expm1(0.001)))
        NS_COEFFS = ((4.0848, -6.8946, 2.927), (3.9505, -6.3029, 2.6377), (3.7418, -5.5913, 2.3037), (2.8769, -3.1427, 1.2046), (2.8366, -3.0525, 1.2012))

        def rms_norm(x, w, eps=1e-06):
            return x * jax.lax.rsqrt(jnp.mean(x * x, axis=-1, keepdims=True) + eps) * w

        def l2_normalize(x):
            return x / (jnp.linalg.norm(x, axis=-1, keepdims=True) + 1e-05)

        def silu(x):
            return x * jax.nn.sigmoid(x)

        def newton_schulz5(G):
            trans = G.shape[1] > G.shape[2]
            X = jnp.swapaxes(G, 1, 2) if trans else G
            X = X / (jnp.linalg.norm(X, axis=(1, 2), keepdims=True) + 1e-07)
            for a, b, c in NS_COEFFS:
                A = X @ jnp.swapaxes(X, 1, 2)
                Bm = b * A + c * (A @ A)
                X = a * X + Bm @ X
            return jnp.swapaxes(X, 1, 2) if trans else X
        b, s, d = hidden_states.shape
        qkv = hidden_states @ qkv_w.T
        q, k, v = jnp.split(qkv, 3, axis=-1)
        q = rms_norm(q, q_norm_w)
        k = rms_norm(k, k_norm_w)

        def to_heads(x):
            return x.reshape(b, s, NH, DH).transpose(0, 2, 1, 3).reshape(b * NH, s, DH)
        q = l2_normalize(to_heads(q))
        k = l2_normalize(to_heads(k))
        v = to_heads(v)
        lr = jax.nn.softplus(hidden_states @ lr_proj_w.T + lr_proj_b + BASE_LR_INV)
        lr = lr.reshape(b, s, NH, 3).transpose(0, 2, 1, 3).reshape(b * NH, s, 3)
        W0 = jnp.tile(w0, (b, 1, 1))
        W1 = jnp.tile(w1, (b, 1, 1))
        W2 = jnp.tile(w2, (b, 1, 1))
        n0 = jnp.linalg.norm(W0, axis=2, keepdims=True)
        n1 = jnp.linalg.norm(W1, axis=2, keepdims=True)
        n2 = jnp.linalg.norm(W2, axis=2, keepdims=True)
        nc = s // CHUNK

        def chunked(x):
            return x.reshape(b * NH, nc, CHUNK, -1).transpose(1, 0, 2, 3)
        qc, kc, vc, lrc = (chunked(q), chunked(k), chunked(v), chunked(lr))

        def renorm(w, n):
            return w / (jnp.linalg.norm(w, axis=2, keepdims=True) + 1e-05) * n

        def step(carry, xs):
            W0, W1, W2 = carry
            qi, ki, vi, li = xs
            l0, l1, l2 = (li[..., 0], li[..., 1], li[..., 2])
            gq = silu(jnp.einsum('bhd,bcd->bhc', W0, qi))
            hq = jnp.einsum('bhd,bcd->bhc', W2, qi)
            o = jnp.einsum('boh,bhc->bco', W1, gq * hq)
            gba = jnp.einsum('bhd,bcd->bhc', W0, ki)
            hbm = jnp.einsum('bhd,bcd->bhc', W2, ki)
            sg = silu(gba)
            hidden = sg * hbm
            dhid = jnp.einsum('boh,bco->bhc', W1, vi)
            dhbm = dhid * sg
            dgate = dhid * hbm
            sig = jax.nn.sigmoid(gba)
            dgba = dgate * sig * (1 + gba * (1 - sig))
            dw1 = jnp.einsum('bco,bhc,bc->boh', vi, hidden, l1)
            dw0 = jnp.einsum('bhc,bcd,bc->bhd', dgba, ki, l0)
            dw2 = jnp.einsum('bhc,bcd,bc->bhd', dhbm, ki, l2)
            dw0, dw1, dw2 = (newton_schulz5(dw0), newton_schulz5(dw1), newton_schulz5(dw2))
            W0 = renorm(W0 + dw0, n0)
            W1 = renorm(W1 + dw1, n1)
            W2 = renorm(W2 + dw2, n2)
            return ((W0, W1, W2), o)
        _, os_ = jax.lax.scan(step, (W0, W1, W2), (qc, kc, vc, lrc))
        out = os_.transpose(1, 0, 2, 3).reshape(b * NH, s, DH)
        return out.reshape(b, NH, s, DH).transpose(0, 2, 1, 3).reshape(b, s, d)

    def _L0_ffn_ref(x, router_w, W1, b1, W2, b2):
        import math
        import jax, jax.numpy as jnp
        import numpy as np
        D_MODEL = 128
        D_FF = 512
        N_EXPERTS = 8
        CAPACITY_FACTOR = 1.25
        L, B = (64, 8)

        def _route(tokens, router_w):
            T = tokens.shape[0]
            E = router_w.shape[0]
            capacity = int(math.ceil(T / E * CAPACITY_FACTOR))
            logits = tokens @ router_w.T
            probs = jax.nn.softmax(logits, axis=-1)
            top1_idx = jnp.argmax(probs, axis=-1)
            top1_prob = jnp.max(probs, axis=-1)
            order = jnp.lexsort((-top1_prob, top1_idx))
            sorted_e = top1_idx[order]
            counts = jnp.bincount(top1_idx, length=E)
            start = jnp.cumsum(counts) - counts
            pos_in_group = jnp.arange(T) - start[sorted_e]
            keep_sorted = pos_in_group < capacity
            keep = jnp.zeros((T,), bool).at[order].set(keep_sorted)
            return jnp.where(keep, top1_idx, 0).astype(jnp.int32)
        Lx, Bx, D = x.shape
        T = Lx * Bx
        E = router_w.shape[0]
        tokens = x.reshape(T, D)
        final_e = _route(tokens, router_w)
        out = jnp.zeros_like(tokens)
        for e in range(E):
            h = jax.nn.relu(tokens @ W1[e] + b1[e])
            y = h @ W2[e] + b2[e]
            out = out + jnp.where((final_e == e)[:, None], y, 0.0)
        return out.reshape(Lx, Bx, D)

    def _L1_attn_ref(x, Wq, Wk, Wv, Wo, bo):
        import jax, jax.numpy as jnp
        import numpy as np
        N_HEADS = 16
        HEAD_DIM = 64
        DIM = 128
        BATCH = 2
        SEQ = 256
        b, s, _ = x.shape
        q = (x @ Wq).reshape(b, s, N_HEADS, HEAD_DIM)
        k = (x @ Wk).reshape(b, s, N_HEADS, HEAD_DIM)
        v = (x @ Wv).reshape(b, s, N_HEADS, HEAD_DIM)
        dot = jnp.einsum('bihd,bkhd->bhik', q, k)
        w = jax.nn.softmax(dot / jnp.sqrt(jnp.float32(HEAD_DIM)), axis=-1)
        a = jnp.einsum('bhij,bjhd->bihd', w, v)
        a = a.reshape(b, s, N_HEADS * HEAD_DIM)
        return a @ Wo + bo

    def _L1_ffn_ref(x_bsD, router_DE, w1_eDF, w3_eDF, w2_eFD, ws1_DF, ws3_DF, ws2_FD):
        import jax, jax.numpy as jnp
        import numpy as np
        B, S, D, E, F, K = (4, 128, 128, 8, 352, 1)
        b, s, d = x_bsD.shape
        a = b * s
        x_aD = x_bsD.reshape(a, d)
        scores_aE = x_aD @ router_DE
        vals_aK, idx_aK = jax.lax.top_k(scores_aE, K)
        masked_aE = jnp.full_like(scores_aE, -jnp.inf).at[jnp.arange(a)[:, None], idx_aK].set(vals_aK)
        gates_Ea = jax.nn.sigmoid(masked_aE).T
        routed_in_EaD = jax.lax.stop_gradient(gates_Ea[:, :, None] * x_aD[None, :, :])
        mid_EaF = jax.nn.silu(jnp.einsum('ead,edf->eaf', routed_in_EaD, w1_eDF)) * jnp.einsum('ead,edf->eaf', routed_in_EaD, w3_eDF)
        routed_out_EaD = jnp.einsum('eaf,efd->ead', mid_EaF, w2_eFD)
        shared_aD = jax.nn.silu(x_aD @ ws1_DF) * (x_aD @ ws3_DF) @ ws2_FD
        out_aD = shared_aD + routed_out_EaD.sum(axis=0)
        return out_aD.reshape(b, s, d)
    x = L0_attn_hidden_states
    x = _layernorm(x + _L0_attn_ref(x, L0_attn_qkv_w, L0_attn_q_norm_w, L0_attn_k_norm_w, L0_attn_lr_proj_w, L0_attn_lr_proj_b, L0_attn_w0, L0_attn_w1, L0_attn_w2), axis=-1)
    x = _layernorm(x + _L0_ffn_ref(x, L0_ffn_router_w, L0_ffn_W1, L0_ffn_b1, L0_ffn_W2, L0_ffn_b2), axis=-1)
    x = _layernorm(x + _L1_attn_ref(x, L1_attn_Wq, L1_attn_Wk, L1_attn_Wv, L1_attn_Wo, L1_attn_bo), axis=-1)
    x = _layernorm(x + _L1_ffn_ref(x, L1_ffn_router_DE, L1_ffn_w1_eDF, L1_ffn_w3_eDF, L1_ffn_w2_eFD, L1_ffn_ws1_DF, L1_ffn_ws3_DF, L1_ffn_ws2_FD), axis=-1)
    return x

_drawn_inputs = setup_inputs


def setup_inputs(seed=0):
    import zlib

    import numpy as np

    out = dict(_drawn_inputs(seed))
    spreads = {'L0_attn_q_norm_w': (1.0, 0.6),
     'L0_attn_k_norm_w': (1.0, 0.2),
     'L0_attn_lr_proj_b': (0.0, 2.0),
     'L1_attn_bo': (0.0, 0.1)}
    factors = {'L0_ffn_b1': 2.685,
     'L1_ffn_router_DE': 8.0,
     'L1_ffn_w1_eDF': 8.0,
     'L1_ffn_w3_eDF': 8.0,
     'L1_ffn_w2_eFD': 8.0,
     'L1_ffn_ws1_DF': 5.895,
     'L1_ffn_ws3_DF': 5.893,
     'L1_ffn_ws2_FD': 5.892}
    for name, (base, spread) in spreads.items():
        noise = np.random.default_rng([zlib.crc32(name.encode()), seed]).standard_normal(out[name].shape)
        drawn = base * np.exp(spread * noise) if base else spread * noise
        out[name] = jnp.asarray(drawn.astype(out[name].dtype))
    for name, factor in factors.items():
        out[name] = (out[name] * factor).astype(out[name].dtype)
    return out
```

```python
from contextlib import ExitStack

import numpy as np

import concourse.bass as bass
import concourse.mybir as mybir

F32 = mybir.dt.float32
F32R = mybir.dt.float32r
BF16 = mybir.dt.bfloat16
I32 = mybir.dt.int32
U32 = mybir.dt.uint32
ALU = mybir.AluOpType
ACT = mybir.ActivationFunctionType
AX = mybir.AxisListType

P = 128
LN_EPS = 1e-5
CREDIT = 1000


class Tick:

    def __init__(self, counter, value, loop=None):
        self.counter, self.value, self.loop = counter, value, loop

    def back(self, n=1):
        t = Tick(self.counter, self.value, self.loop)
        t.value -= n * self.loop.per(self.counter)
        return t


class Loop:

    def __init__(self, book, name, n):
        self.book, self.name, self.n = book, name, n
        self.open = True
        self.start = {c: c.count for c in book.counters}
        self.index = None

    def per(self, counter):
        return self.book.known.get((self.name, counter.name), 0)

    def close(self):
        self.open = False
        for c in self.book.counters:
            raised = c.count - self.start[c]
            self.book.found[(self.name, c.name)] = raised
            c.count = self.start[c] + self.n * raised


class Counter:

    def __init__(self, book, name, step, credit=CREDIT):
        self.book, self.name, self.step = book, name, step
        self.sem = book.ctx.enter_context(book.nc.semaphore(name))
        self.count = credit
        book.counters.append(self)
        if credit:
            book.nc.sync.sem_inc(self.sem, credit)

    def mark(self, instruction):
        instruction.then_inc(self.sem, self.step)
        self.count += self.step
        return Tick(self, self.count, self.book.loop)


class Queue:

    def __init__(self, book, name, engine):
        self.book, self.name, self.engine = book, name, engine
        self.counter = Counter(book, f"done_{name}", 1)
        self.seen = {}

    def wait(self, *ticks):
        for t in ticks:
            if t is None:
                continue
            loop, value = t.loop, t.value
            if loop is not None and not loop.open:
                value += (loop.n - 1) * loop.per(t.counter)
                loop = None
            key = (t.counter, loop)
            if self.seen.get(key, -1) >= value:
                continue
            self.seen[key] = value
            if loop is None:
                self.engine.wait_ge(t.counter.sem, value)
            else:
                self.engine.wait_ge(t.counter.sem, loop.index * loop.per(t.counter) + value)

    def done(self, instruction):
        return self.counter.mark(instruction)


class Book:

    def __init__(self, nc, ctx, known):
        self.nc, self.ctx, self.known, self.found = nc, ctx, known, {}
        self.counters, self.loop, self.events = [], None, {}
        self.queues = [Queue(self, n, e) for n, e in (
            ("pe", nc.tensor), ("act", nc.scalar), ("dve", nc.vector), ("pool", nc.gpsimd), ("sp", nc.sync))]
        self.names = 0

    def dma(self, name, credit=CREDIT):
        return Counter(self, name, 16, credit)

    def run(self, name, n, body):
        loop = Loop(self, name, n)
        for q in self.queues:
            q.seen = {k: v for k, v in q.seen.items() if k[1] is None}
        with self.nc.Fori(0, n, 1) as i:
            loop.index, self.loop = i, loop
            self.events[name] = {}
            body(i)
        self.loop = None
        loop.close()
        for q in self.queues:
            q.seen = {k: v for k, v in q.seen.items() if k[1] is None}


def bcast(ap, shape):
    return ap.to_broadcast(list(shape))


class Net:

    def __init__(self, nc, ctx, known, io):
        self.nc, self.ctx, self.io = nc, ctx, io
        self.book = Book(nc, ctx, known)
        self.PE, self.A, self.V, self.G, self.S = self.book.queues
        self.psum = ctx.enter_context(nc.psum_tensor("psum", [P, 8, 512], F32))
        self.scratch = None

    def note(self, key, tick):
        book = self.book
        book.events[book.loop.name][key] = tick
        book.found[("event", book.loop.name, key)] = (tick.counter.name, tick.value - tick.loop.start[tick.counter])

    def prev(self, key):
        book, loop = self.book, self.book.loop
        if ("event", loop.name, key) not in book.known:
            return None
        name, offset = book.known[("event", loop.name, key)]
        counter = next(c for c in book.counters if c.name == name)
        return Tick(counter, loop.start[counter] + offset - loop.per(counter), loop)

    def settle(self, *queues):
        ticks = [Tick(q.counter, q.counter.count) for q in self.book.queues]
        for q in queues or self.book.queues:
            q.wait(*ticks)

    def sb(self, name, shape, dt=F32, ctx=None):
        return (ctx or self.ctx).enter_context(self.nc.sbuf_tensor(name, shape, dt))


def constants(n):
    nc, G = n.nc, n.G
    n.ident = n.sb("ident", [P, P])
    n.ones = n.sb("ones", [P, P])
    n.blocks = n.sb("blocks", [P, P])
    n.mask4 = n.sb("mask4", [P, 4, 64])
    n.before = n.sb("before", [P, P])
    n.eps = n.sb("eps", [P, 4])
    ts = [G.done(nc.gpsimd.memset(t, v)) for t, v in (
        (n.ident[:, :], 0.0), (n.ones[:, :], 1.0), (n.blocks[:, :], 1.0), (n.mask4[:, :, :], 1.0),
        (n.before[:, :], 1.0), (n.eps[:, 0:1], 1e-6), (n.eps[:, 1:2], LN_EPS), (n.eps[:, 2:3], 1e-7),
        (n.eps[:, 3:4], 0.0))]
    G.wait(ts[-1])

    def keep(t, pattern, base, mult, op=ALU.is_ge, fill=0.0):
        k = G.done(nc.gpsimd.affine_select(out=t, in_=t, pattern=pattern, compare_op=op, fill=fill, base=base,
                                           channel_multiplier=mult))
        G.wait(k)
        return k

    keep(n.ident[:, :], [[-1, P]], 0, 1, ALU.not_equal, 1.0)
    b = n.blocks[:, :].rearrange("p (h x) -> p h x", h=4)
    keep(b, [[-32, 4], [0, 32]], 0, 1)
    keep(b, [[32, 4], [0, 32]], 31, -1)
    keep(n.mask4[:, :, :], [[-32, 4], [0, 64]], 0, 1)
    keep(n.mask4[:, :, :], [[32, 4], [0, 64]], 31, -1)
    keep(n.before[:, :], [[1, P]], -1, -1)
    n.e_less = n.sb("e_less", [P, 8])
    n.steps = n.sb("steps", [P, 16])
    n.count = n.sb("count", [P, 24])
    for t, step, base in ((n.e_less, 1, -8), (n.steps, P, 0), (n.count, 1, 0)):
        i32 = n.sb(f"i32_{base}_{step}", [P, t.shape[1]], I32)
        k = G.done(nc.gpsimd.iota(i32[:, :], pattern=[[step, t.shape[1]]], base=base, channel_multiplier=0))
        G.wait(k)
        n.t_const = G.done(nc.gpsimd.tensor_copy(t[:, :], i32[:, :]))



HEADS, DH, HID, CHUNK = 4, 32, 64, 256
TPC = CHUNK // P
BASE_LR_INV = float(np.log(np.expm1(0.001)))
NS = ((4.0848, -6.8946, 2.927), (3.9505, -6.3029, 2.6377), (3.7418, -5.5913, 2.3037),
      (2.8769, -3.1427, 1.2046), (2.8366, -3.0525, 1.2012))


def ttt_attention(n, x_all, y_all, stats):
    nc, io, PE, A, V, G, S, ps = n.nc, n.io, n.PE, n.A, n.V, n.G, n.S, n.psum
    NT = x_all.shape[1]
    NC = NT // TPC
    with ExitStack() as mem:
        sb = lambda name, shape, dt=F32: n.sb("t_" + name, shape, dt, mem)
        qT = sb("qT", [P, NT * P])
        kT = sb("kT", [P, NT * P])
        vT = sb("vT", [P, NT * P])
        kl0 = sb("kl0", [P, NT, P])
        kl2 = sb("kl2", [P, NT, P])
        vl1 = sb("vl1", [P, NT, P])
        wT = sb("wT", [P, 384])
        lwT = sb("lwT", [P, 12])
        lr = sb("lr", [P, NT * 12])
        Wc = sb("Wc", [P, 3, HID])
        WB = sb("WB", [P, 3, HEADS, HID])
        W1T = sb("W1T", [P, 2, P])
        N0 = sb("N0", [P, 129])
        aI = sb("aI", [P, len(NS), P])

        wraw = sb("wraw", [P, 3, P])
        lraw = sb("lraw", [12, P])
        w02 = sb("w02", [HID, 2, HEADS, DH])
        nw = sb("nw", [P, 2, P])
        lb = sb("lb", [P, 12])
        d_w = n.book.dma("ttt_weights")
        for dst, src in (
            (wraw[:, :, :], io["L0_attn_qkv_w"].rearrange("(a p) d -> p a d", p=P)),
            (lraw[:, :], io["L0_attn_lr_proj_w"]),
            (w02[:, 0], io["L0_attn_w0"].rearrange("h i d -> i h d")),
            (w02[:, 1], io["L0_attn_w2"].rearrange("h i d -> i h d")),
            (Wc[:, 2, :], io["L0_attn_w1"].rearrange("h o i -> (h o) i")),
            (nw[:, 0, :], io["L0_attn_q_norm_w"].rearrange("(a d) -> a d", a=1).to_broadcast([P, P])),
            (nw[:, 1, :], io["L0_attn_k_norm_w"].rearrange("(a d) -> a d", a=1).to_broadcast([P, P])),
            (lb[:, :], io["L0_attn_lr_proj_b"].rearrange("(a d) -> a d", a=1).to_broadcast([P, 12])),
        ):
            t_w = d_w.mark(nc.sync.dma_start(dst, src))
        PE.wait(t_w, n.t_const)
        for a in range(3):
            nc.tensor.transpose(ps[:, 0, a * P:(a + 1) * P], wraw[:, a, :], n.ident[:, :])
        nc.tensor.transpose(ps[:, 0, 384:396], lraw[:, :], n.ident[0:12, 0:12])
        for a in range(2):
            t = PE.done(nc.tensor.transpose(ps[:, 1, a * HID:(a + 1) * HID],
                                            w02[:, a].rearrange("i h d -> i (h d)"), n.ident[0:HID, 0:HID]))
        A.wait(t)
        A.done(nc.scalar.activation(wT[:, :], ps[:, 0, 0:384], ACT.Copy))
        t_wT = A.done(nc.scalar.activation(lwT[:, :], ps[:, 0, 384:396], ACT.Copy))
        V.wait(t, n.t_const)
        t_Wc = V.done(nc.vector.tensor_copy(Wc[:, 0:2, :], ps[:, 1, 0:2 * HID].rearrange("p (a i) -> p a i", a=2)))
        for k, (a, _, _) in enumerate(NS):
            t_aI = V.done(nc.vector.tensor_scalar(aI[:, k, :], n.ident[:, :], a, None, ALU.mult))
        V.wait(t_w)
        t_lb = V.done(nc.vector.tensor_scalar(lb[:, :], lb[:, :], BASE_LR_INV, None, ALU.add))

        sqw = sb("sqw", [P, 3, HID])
        rs = sb("rs", [P, 129])
        NR = sb("NR", [P, 129])
        Wn = sb("Wn", [P, 3, HID])

        def row_norms(w, t_in, out, t_free):
            A.wait(t_in, t_free)
            t_sq = A.done(nc.scalar.activation(sqw[:, :, :], w[:, :, :], ACT.Square))
            PE.wait(t_sq, n.t_b3)
            t_s = PE.done(nc.tensor.matmul(ps[:, 3, 0:2 * HID], n.blocks[:, :], sqw[:, 0:2, :], start=True, stop=True))
            V.wait(t_sq)
            t_r = V.done(nc.vector.tensor_reduce(rs[:, 0:1], sqw[:, 2, :], AX.X, ALU.add))
            A.wait(t_s, t_r)
            t1 = A.done(nc.scalar.activation(out[:, 0:2 * HID], ps[:, 3, 0:2 * HID], ACT.Sqrt))
            return A.done(nc.scalar.activation(out[:, 128:129], rs[:, 0:1], ACT.Sqrt)), t1

        def blocks_of(t_w, t_free):
            V.wait(t_w, t_free)
            t_wb = V.done(nc.vector.tensor_tensor(
                WB[:, :, :, :], bcast(Wc[:, :, :].unsqueeze(2), [P, 3, HEADS, HID]),
                bcast(n.mask4[:, :, :].unsqueeze(1), [P, 3, HEADS, HID]), ALU.mult))
            PE.wait(t_wb)
            for g in range(2):
                t = PE.done(nc.tensor.transpose(ps[:, 7, g * P:(g + 1) * P],
                                                WB[:, 2, 2 * g:2 * g + 2, :].rearrange("p a b -> p (a b)"), n.ident[:, :]))
            A.wait(t, t_free)
            return t_wb, A.done(nc.scalar.activation(W1T[:, :, :].rearrange("p a b -> p (a b)"), ps[:, 7, 0:256], ACT.Copy))

        n.t_b3 = None
        V.wait(t_Wc)
        A.wait(t_w)
        t_N0, _ = row_norms(Wc, t_Wc, N0, None)
        t_WB, t_W1T = blocks_of(t_Wc, None)

        xs = sb("xs", [P, TPC, P])
        xT = sb("xT", [P, TPC * P])
        sq = sb("sq", [P, TPC, 256])
        qw = sb("qw", [P, TPC, 256])
        vv = sb("vv", [P, TPC, P])
        ss = sb("ss", [P, 4])
        s2 = sb("s2", [P, 16])
        z = sb("z", [P, 24])
        s_ = sb("s_", [P, 24])
        w_ = sb("w_", [P, 24])
        w2_ = sb("w2_", [P, 24])
        ac = sb("ac", [P, 24])
        d_x = n.book.dma("ttt_x")
        x_rows = io["L0_attn_hidden_states"].rearrange("b (t p) d -> p (b t) d", p=P)

        def project(c):
            S.wait(n.prev("x"))
            t_x = d_x.mark(nc.sync.dma_start(xs[:, :, :], x_rows[:, bass.ds(c * TPC, TPC), :]))
            PE.wait(t_x, n.prev("xT"))
            for t in range(TPC):
                k = PE.done(nc.tensor.transpose(ps[:, 0, t * P:(t + 1) * P], xs[:, t, :], n.ident[:, :]))
            n.note("x", k)
            A.wait(k, n.prev("xT_sb"))
            k = A.done(nc.scalar.activation(xT[:, :], ps[:, 0, 0:256], ACT.Copy))
            n.note("xT", k)
            PE.wait(k, n.prev("qk"), n.prev("v"), n.prev("lr"), t_wT)
            for t in range(TPC):
                lhs = xT[:, t * P:(t + 1) * P]
                nc.tensor.matmul(ps[:, 1, t * 256:(t + 1) * 256], lhs, wT[:, 0:256], start=True, stop=True)
                nc.tensor.matmul(ps[:, 2, t * P:(t + 1) * P], lhs, wT[:, 256:384], start=True, stop=True)
                k = PE.done(nc.tensor.matmul(ps[:, 3, t * 12:(t + 1) * 12], lhs, lwT[:, :], start=True, stop=True))
            n.note("xT_sb", k)
            qk = ps[:, 1, :]
            A.wait(k, n.prev("sq2"))
            t_sq = A.done(nc.scalar.activation(sq[:, :, :].rearrange("p a b -> p (a b)"), qk, ACT.Square))
            V.wait(t_sq, n.prev("qkv_t"), n.prev("lrs"))
            t_qw = V.done(nc.vector.tensor_tensor(qw[:, :, :].rearrange("p a (m d) -> p a m d", m=2),
                                                  qk.rearrange("p (a m d) -> p a m d", a=TPC, m=2),
                                                  bcast(nw[:, :, :].unsqueeze(1), [P, TPC, 2, P]), ALU.mult))
            n.note("qk", t_qw)
            t_ss = V.done(nc.vector.tensor_reduce(ss[:, :], sq[:, :, :].rearrange("p a (m d) -> p (a m) d", m=2),
                                                  AX.X, ALU.add))
            A.wait(t_qw, t_ss)
            t_sq2 = A.done(nc.scalar.activation(sq[:, :, :], qw[:, :, :], ACT.Square))
            V.wait(t_sq2)
            t_s2 = V.done(nc.vector.tensor_reduce(s2[:, :], sq[:, :, :].rearrange("p a (h d) -> p (a h) d", d=DH),
                                                  AX.X, ALU.add))
            n.note("sq2", t_s2)
            A.wait(t_s2)
            A.done(nc.scalar.activation(ss[:, :], ss[:, :], ACT.Sqrt, bias=n.eps[:, 0:1], scale=1.0 / P))
            t_n2 = A.done(nc.scalar.activation(s2[:, :], s2[:, :], ACT.Sqrt))
            V.wait(t_n2)
            t = V.done(nc.vector.reciprocal(ss[:, :], ss[:, :]))
            V.wait(t)
            rb = bcast(ss[:, :].unsqueeze(2), [P, 4, 4])
            s2v = s2[:, :].rearrange("p (g h) -> p g h", h=4)
            t = V.done(nc.vector.tensor_tensor(s2v, s2v, rb, ALU.mult))
            V.wait(t)
            t = V.done(nc.vector.tensor_scalar(s2[:, :], s2[:, :], 1e-5, None, ALU.add))
            V.wait(t)
            t = V.done(nc.vector.reciprocal(s2[:, :], s2[:, :]))
            V.wait(t)
            t = V.done(nc.vector.tensor_tensor(s2v, s2v, rb, ALU.mult))
            V.wait(t)
            qwh = qw[:, :, :].rearrange("p a (h d) -> p (a h) d", d=DH)
            t_qk = V.done(nc.vector.tensor_tensor(qwh, qwh, bcast(s2[:, :].unsqueeze(2), [P, 16, DH]), ALU.mult))
            t_z = V.done(nc.vector.tensor_tensor(z[:, :].rearrange("p (a b) -> p a b", a=TPC),
                                                 ps[:, 3, 0:24].rearrange("p (a b) -> p a b", a=TPC),
                                                 bcast(lb[:, :].unsqueeze(1), [P, TPC, 12]), ALU.add))
            n.note("lr", t_z)
            V.wait(t_z)
            t = V.done(nc.vector.scalar_tensor_tensor(s_[:, :], z[:, :], -1.0, z[:, :], ALU.mult, ALU.min))
            A.wait(t)
            t = A.done(nc.scalar.activation(s_[:, :], s_[:, :], ACT.Sigmoid))
            V.wait(t)
            t = V.done(nc.vector.tensor_scalar(w_[:, :], s_[:, :], -1.0, 2.0, ALU.mult, ALU.add))
            V.wait(t)
            t = V.done(nc.vector.reciprocal(w_[:, :], w_[:, :]))
            V.wait(t)
            t = V.done(nc.vector.tensor_tensor(w_[:, :], w_[:, :], s_[:, :], ALU.mult))
            V.wait(t)
            t = V.done(nc.vector.tensor_tensor(w2_[:, :], w_[:, :], w_[:, :], ALU.mult))
            V.wait(t)
            t = V.done(nc.vector.tensor_scalar(ac[:, :], w2_[:, :], 1.0 / 17, None, ALU.mult))
            for k in (15, 13, 11, 9, 7, 5, 3):
                V.wait(t)
                t = V.done(nc.vector.scalar_tensor_tensor(ac[:, :], ac[:, :], 1.0 / k, w2_[:, :], ALU.add, ALU.mult))
            V.wait(t)
            t = V.done(nc.vector.scalar_tensor_tensor(ac[:, :], ac[:, :], 1.0, w_[:, :], ALU.add, ALU.mult))
            V.wait(t)
            t = V.done(nc.vector.tensor_scalar(ac[:, :], ac[:, :], 2.0, None, ALU.mult))
            V.wait(t, n.prev("lrs"))
            lrc = ac[:, :]
            t_lr = V.done(nc.vector.scalar_tensor_tensor(w_[:, :], z[:, :], 0.0, lrc, ALU.max, ALU.add))
            A.wait(n.prev("qkv_t"), n.prev("lrs"))
            t_v = A.done(nc.scalar.activation(vv[:, :, :].rearrange("p a b -> p (a b)"), ps[:, 2, 0:256], ACT.Copy))
            n.note("v", t_v)
            l4 = w_[:, :].rearrange("p (a h j) -> p a h j", a=TPC, j=3)
            G.wait(t_lr, t_qk, t_v)
            for j, src, dst in ((0, qw[:, :, P:256], kl0), (2, qw[:, :, P:256], kl2), (1, vv[:, :, :], vl1)):
                t_g = G.done(nc.gpsimd.tensor_tensor(
                    dst[:, bass.ds(c * TPC, TPC), :].rearrange("p a (h d) -> p a h d", d=DH),
                    src.rearrange("p a (h d) -> p a h d", d=DH),
                    bcast(l4[:, :, :, j:j + 1], [P, TPC, HEADS, DH]), ALU.mult))
            n.note("lrs", t_g)
            PE.wait(t_qk, t_v, n.prev("tr"))
            for m in range(3):
                for t in range(TPC):
                    src = vv[:, t, :] if m == 2 else qw[:, t, m * P:(m + 1) * P]
                    at = (m * TPC + t) * P
                    k = PE.done(nc.tensor.transpose(ps[:, 4 + at // 512, at % 512:at % 512 + P], src, n.ident[:, :]))
            n.note("qkv_t", k)
            A.wait(k)
            A.done(nc.scalar.activation(qT[:, bass.ds(c * CHUNK, CHUNK)], ps[:, 4, 0:256], ACT.Copy))
            A.done(nc.scalar.activation(kT[:, bass.ds(c * CHUNK, CHUNK)], ps[:, 4, 256:512], ACT.Copy))
            n.note("tr", A.done(nc.scalar.activation(vT[:, bass.ds(c * CHUNK, CHUNK)], ps[:, 5, 0:256], ACT.Copy)))

        V.wait(t_lb)
        n.book.run("project", NC, project)

        kTs, vTs = sb("kTs", [P, CHUNK]), sb("vTs", [P, CHUNK])
        k0s, k2s, v1s = (sb(f"{a}s", [P, TPC, P]) for a in ("k0", "k2", "v1"))
        sig, hb, sg, hd, dg, dh, v1, u = (sb(a, [P, 512]) for a in ("sig", "hb", "sg", "hd", "dg", "dh", "v1", "u"))
        sigq, tq, hq = (sb(a, [P, 512]) for a in ("sigq", "tq", "hq"))
        X = sb("X", [P, 3, HID])
        XT = sb("XT", [P, 3, P])
        Ab, T1, Gm = (sb(a, [P, 3, P]) for a in ("Ab", "T1", "Gm"))
        fn = sb("fn", [P, 3])
        d_s = n.book.dma("ttt_stage")
        t_xt0 = V.done(nc.vector.memset(XT[:, :, :], 0.0))

        def stage(c):
            for dst, src in ((kTs[:, :], kT[:, bass.ds(c * CHUNK, CHUNK)]), (vTs[:, :], vT[:, bass.ds(c * CHUNK, CHUNK)]),
                             (k0s[:, :, :], kl0[:, bass.ds(c * TPC, TPC), :]), (k2s[:, :, :], kl2[:, bass.ds(c * TPC, TPC), :]),
                             (v1s[:, :, :], vl1[:, bass.ds(c * TPC, TPC), :])):
                t = d_s.mark(nc.sync.dma_start(dst, src))
            return t

        def forward(c, b, t_free0, t_free1, t_free2):
            PE.wait(t_free0, t_free1, b["WB"])
            for m in range(2):
                for g in range(2):
                    t = PE.done(nc.tensor.matmul(ps[:, m, g * 256:(g + 1) * 256],
                                                 WB[:, m, 2 * g:2 * g + 2, :].rearrange("p a b -> p (a b)"),
                                                 qT[:, bass.ds(c * CHUNK, CHUNK)], start=True, stop=True))
            A.wait(t, b["sigq"])
            t_sq = A.done(nc.scalar.activation(sigq[:, :], ps[:, 0, :], ACT.Sigmoid))
            V.wait(t_sq, b["tq"])
            t_t = V.done(nc.vector.tensor_tensor(tq[:, :], ps[:, 0, :], sigq[:, :], ALU.mult))
            V.wait(t_t, b["hq"])
            t_h = V.done(nc.vector.tensor_tensor(hq[:, :], ps[:, 1, :], tq[:, :], ALU.mult))
            PE.wait(t_h, t_free2, b["W1T"])
            for t in range(TPC):
                for g in range(2):
                    k = PE.done(nc.tensor.matmul(ps[:, 2, t * P:(t + 1) * P], hq[:, g * 256 + t * P:g * 256 + (t + 1) * P],
                                                 W1T[:, g, :], start=(g == 0), stop=(g == 1)))
            V.wait(k)
            yc = y_all[:, bass.ds(c * TPC, TPC), :]
            t_y = V.done(nc.vector.tensor_tensor(yc, ps[:, 2, 0:256].rearrange("p (a b) -> p a b", a=TPC),
                                                 x_all[:, bass.ds(c * TPC, TPC), :], ALU.add))
            V.wait(t_y)
            for t in range(TPC):
                t_st = V.done(nc.vector.bn_stats(stats[:, bass.ds(c * TPC + t, 1), :].rearrange("p a s -> p (a s)"),
                                                 y_all[:, bass.ds(c * TPC + t, 1), :].rearrange("p a d -> p (a d)")))
            return t_h, k, t_st

        def update(c):
            PE.wait(n.prev("stage"), n.prev("hq"), n.prev("y"), n.prev("WB"))
            for m, lhs in ((0, kTs), (1, kTs), (2, vTs)):
                for t in range(TPC):
                    k = nc.tensor.matmul(ps[:, m, t * 256:(t + 1) * 256], lhs[:, t * P:(t + 1) * P],
                                         WB[:, m].rearrange("p h i -> p (h i)"), start=True, stop=True)
                tk = PE.done(k)
                if m == 0:
                    A.wait(tk)
                    t_sig = A.done(nc.scalar.activation(sig[:, :], ps[:, 0, :], ACT.Sigmoid))
                if m == 1:
                    A.wait(tk)
                    t_hb = A.done(nc.scalar.activation(hb[:, :], ps[:, 1, :], ACT.Copy))
            V.wait(t_sig)
            t_sg = V.done(nc.vector.tensor_tensor(sg[:, :], ps[:, 0, :], sig[:, :], ALU.mult))
            G.wait(t_sg, t_hb)
            t_hid = G.done(nc.gpsimd.tensor_tensor(hd[:, :], sg[:, :], hb[:, :], ALU.mult))
            V.wait(t_sg)
            t_v1 = V.done(nc.vector.scalar_tensor_tensor(v1[:, :], sg[:, :], -1.0, sig[:, :], ALU.add, ALU.mult))
            V.wait(tk, t_hb)
            t_dh = V.done(nc.vector.tensor_tensor(dh[:, :], ps[:, 2, :], sg[:, :], ALU.mult))
            t_dg = V.done(nc.vector.tensor_tensor(dg[:, :], ps[:, 2, :], hb[:, :], ALU.mult))
            V.wait(t_v1)
            t_u = V.done(nc.vector.tensor_tensor(u[:, :], sg[:, :], v1[:, :], ALU.subtract))
            V.wait(t_u)
            t_dga = V.done(nc.vector.tensor_tensor(dg[:, :], dg[:, :], u[:, :], ALU.mult))
            fb = {"WB": None, "W1T": n.prev("W1T"), "sigq": n.prev("hq"), "tq": n.prev("hq"), "hq": n.prev("y")}
            t_h, t_o, t_st = forward(c, fb, t_sg, t_hb, t_dg)
            PE.wait(n.prev("X5"))
            for m, lhs, rhs, tr in ((1, k2s, dh, t_dh), (2, v1s, hd, t_hid), (0, k0s, dg, t_dga)):
                PE.wait(tr)
                for h in range(HEADS):
                    for t in range(TPC):
                        k = nc.tensor.matmul(ps[h * DH:(h + 1) * DH, 3, m * HID:(m + 1) * HID],
                                             lhs[:, t, h * DH:(h + 1) * DH], rhs[:, t * 256 + h * HID:t * 256 + (h + 1) * HID],
                                             start=(t == 0), stop=(t == 1), tile_position=(0, h * DH))
            t_gr = PE.done(k)
            grads = ps[:, 3, 0:192].rearrange("p (m i) -> p m i", m=3)
            S.wait(t_gr)
            n.note("stage", stage(c + 1))
            A.wait(t_gr)
            t = A.done(nc.scalar.activation(sqw[:, :, :], grads, ACT.Square))
            V.wait(t)
            t = V.done(nc.vector.tensor_reduce(fn[:, :], sqw[:, :, :], AX.X, ALU.add))
            PE.wait(t)
            t = PE.done(nc.tensor.matmul(ps[:, 3, 256:259], n.blocks[:, :], fn[:, :], start=True, stop=True))
            A.wait(t)
            t = A.done(nc.scalar.activation(fn[:, :], ps[:, 3, 256:259], ACT.Sqrt))
            V.wait(t)
            t = V.done(nc.vector.tensor_scalar(fn[:, :], fn[:, :], 1e-7, None, ALU.add))
            V.wait(t)
            t = V.done(nc.vector.reciprocal(fn[:, :], fn[:, :]))
            V.wait(t)
            t_X = V.done(nc.vector.tensor_tensor(X[:, :, :], grads, bcast(fn[:, :].unsqueeze(2), [P, 3, HID]), ALU.mult))
            n.t_b3 = t_X
            PE.wait(t_X)
            tX, tXT = [t_X] * 3, [None] * 3
            k01 = PE.done(nc.tensor.transpose(ps[:, 4, 0:P], X[:, 0:2, :].rearrange("p a b -> p (a b)"), n.ident[:, :]))
            k2 = PE.done(nc.tensor.transpose(ps[0:HID, 6, 0:P], X[:, 2, :], n.ident[:, :]))
            A.wait(k01)
            for m, rows in ((0, ps[0:HID, 4, 0:P]), (1, ps[HID:P, 4, 0:P]), (2, ps[0:HID, 6, 0:P])):
                if m == 2:
                    A.wait(k2)
                tXT[m] = A.done(nc.scalar.activation(XT[0:HID, m, :], rows, ACT.Copy))
            tXT[0] = tXT[1]
            for it, (_, cb, cc) in enumerate(NS):
                last = it == len(NS) - 1
                tA, tAb, tT, tAA, tG = ([None] * 3 for _ in range(5))
                for m in range(3):
                    PE.wait(tXT[m])
                    tA[m] = PE.done(nc.tensor.matmul(ps[:, 4 + m, 0:P], XT[:, m, :], XT[:, m, :], start=True, stop=True))
                for m in range(3):
                    V.wait(tA[m])
                    tAb[m] = V.done(nc.vector.tensor_tensor(Ab[:, m, :], ps[:, 4 + m, 0:P], n.blocks[:, :], ALU.mult))
                for m in range(3):
                    PE.wait(tAb[m])
                    tAA[m] = PE.done(nc.tensor.matmul(ps[:, 4 + m, P:2 * P], Ab[:, m, :], Ab[:, m, :], start=True, stop=True))
                    V.wait(tAb[m])
                    tT[m] = V.done(nc.vector.scalar_tensor_tensor(T1[:, m, :], Ab[:, m, :], cb, aI[:, it, :], ALU.mult, ALU.add))
                for m in range(3):
                    V.wait(tAA[m], tT[m])
                    tG[m] = V.done(nc.vector.scalar_tensor_tensor(Gm[:, m, :], ps[:, 4 + m, P:2 * P], cc, T1[:, m, :], ALU.mult, ALU.add))
                for m in range(3):
                    PE.wait(tG[m], tX[m])
                    k = nc.tensor.matmul(ps[:, 4 + m, 256:256 + HID], Gm[:, m, :], X[:, m, :], start=True, stop=True)
                    if not last:
                        k = nc.tensor.matmul(ps[0:HID, 4 + m, 384:512], X[:, m, :], Gm[:, m, :], start=True, stop=True)
                    k = PE.done(k)
                    if not last:
                        A.wait(k)
                        tX[m] = A.done(nc.scalar.activation(X[:, m, :], ps[:, 4 + m, 256:256 + HID], ACT.Copy))
                        tXT[m] = A.done(nc.scalar.activation(XT[0:HID, m, :], ps[0:HID, 4 + m, 384:512], ACT.Copy))
            V.wait(k)
            t_Wn = V.done(nc.vector.tensor_tensor(Wn[:, :, :], ps[:, 4:7, 256:256 + HID], Wc[:, :, :], ALU.add))
            n.note("X5", t_Wn)
            t_r, _ = row_norms(Wn, t_Wn, NR, None)
            V.wait(t_r, t_N0)
            t = V.done(nc.vector.tensor_scalar(NR[:, :], NR[:, :], 1e-5, None, ALU.add))
            V.wait(t)
            t = V.done(nc.vector.reciprocal(NR[:, :], NR[:, :]))
            V.wait(t)
            t = V.done(nc.vector.tensor_tensor(NR[:, :], NR[:, :], N0[:, :], ALU.mult))
            V.wait(t)
            V.done(nc.vector.tensor_tensor(Wc[:, 0:2, :], Wn[:, 0:2, :], NR[:, 0:128].rearrange("p (a b) -> p a b", a=2), ALU.mult))
            t = V.done(nc.vector.tensor_scalar(Wc[:, 2, :], Wn[:, 2, :], NR[:, 128:129], None, ALU.mult))
            t_wb, t_w1t = blocks_of(t, t_o)
            for key, tick in (("WB", t_wb), ("W1T", t_w1t), ("hq", t_h), ("y", t_st)):
                n.note(key, tick)

        n.settle()
        t_s0 = stage(0)
        PE.wait(t_s0)
        n.book.run("scan", NC - 1, update)
        last = n.book.events["scan"]
        return forward(NC - 1, {"WB": last["WB"], "W1T": last["W1T"], "sigq": last["hq"], "tq": last["hq"], "hq": last["y"]},
                       last["y"], last["stage"], last["hq"])[2]



def row_stats(n, y_all, stats, t, eng_wait=True):
    n.V.wait(t)
    for i in range(y_all.shape[1]):
        t = n.V.done(n.nc.vector.bn_stats(stats[:, i, :], y_all[:, i, :]))
    return t


def layer_norm(n, y_all, stats, t_stats, out):
    nc, V, A = n.nc, n.V, n.A
    NT = y_all.shape[1]
    mv, sd = n.mv, n.sd
    V.wait(t_stats)
    for i in range(NT):
        t = V.done(nc.vector.bn_aggr(mv[:, i, :], stats[:, i, :]))
    A.wait(t)
    t = A.done(nc.scalar.activation(sd[:, :], mv[:, :, 1:2].rearrange("p a b -> p (a b)"), ACT.Sqrt, bias=n.eps[:, 1:2]))
    V.wait(t)
    t = V.done(nc.vector.reciprocal(sd[:, :], sd[:, :]))
    V.wait(t)
    for i in range(NT):
        t = V.done(nc.vector.tensor_scalar(out[:, i, :], y_all[:, i, :], mv[:, i, 0:1], sd[:, i:i + 1],
                                           ALU.subtract, ALU.mult))
    return t


def transpose_all(n, x_all, xT, t_x, banks=(0, 1)):
    nc, PE, A = n.nc, n.PE, n.A
    PE.wait(t_x)
    free = [None] * len(banks)
    for g in range(x_all.shape[1] // 4):
        k = g % len(banks)
        PE.wait(free[k])
        for i in range(4):
            t = PE.done(nc.tensor.transpose(n.psum[:, banks[k], i * P:(i + 1) * P], x_all[:, 4 * g + i, :], n.ident[:, :]))
        A.wait(t)
        free[k] = A.done(nc.scalar.activation(xT[:, g * 512:(g + 1) * 512], n.psum[:, banks[k], :], ACT.Copy))
    return free[k]


def router(n, xT, rT, t_in, bank):
    nc, PE = n.nc, n.PE
    E = rT.shape[1]
    PE.wait(t_in)
    NT = xT.shape[1] // P
    for i in range(NT):
        t = PE.done(nc.tensor.matmul(n.psum[:, bank, i * E:(i + 1) * E], xT[:, i * P:(i + 1) * P], rT, start=True, stop=True))
    return t, n.psum[:, bank, 0:NT * E].rearrange("p (t e) -> p t e", e=E)


def top_one(n, sb, logits, t_logits):
    nc, V, G = n.nc, n.V, n.G
    NT, E = logits.shape[1:]
    mx = sb("mx", [P, NT])
    hot = sb("hot", [P, NT, E])
    cand = sb("cand", [P, NT, E])
    idx = sb("idx", [P, NT])
    V.wait(t_logits)
    t_mx = V.done(nc.vector.tensor_reduce(mx[:, :], logits, AX.X, ALU.max))
    V.wait(t_mx)
    t = V.done(nc.vector.tensor_tensor(cand[:, :, :], logits, bcast(mx[:, :].unsqueeze(2), [P, NT, E]), ALU.is_ge))
    V.wait(t)
    t = V.done(nc.vector.tensor_tensor(cand[:, :, :], cand[:, :, :], bcast(n.e_less[:, :].unsqueeze(1), [P, NT, E]), ALU.mult))
    V.wait(t)
    t = V.done(nc.vector.tensor_reduce(idx[:, :], cand[:, :, :], AX.X, ALU.min))
    V.wait(t)
    t = V.done(nc.vector.tensor_tensor(hot[:, :, :], bcast(n.e_less[:, :].unsqueeze(1), [P, NT, E]),
                                       bcast(idx[:, :].unsqueeze(2), [P, NT, E]), ALU.is_equal))
    return mx, hot, t_mx, t


def capacity(n, sb, logits, mx, hot, t_mx, t_hot, cap):
    nc, V, A, PE = n.nc, n.V, n.A, n.PE
    NT, E = hot.shape[1:]
    ps = n.psum
    ex = sb("ex", [P, NT, E])
    pr = sb("pr", [P, NT])
    prow = sb("prow", [P, NT * P])
    gt = sb("gt", [P, 2, NT * P], BF16)
    eq = sb("eq", [P, P], BF16)
    tri = sb("tri", [P, P], BF16)
    hotb = sb("hotb", [P, NT, E], BF16)
    rank = sb("rank", [P, NT, E])
    rk = sb("rk", [P, NT])
    V.wait(t_mx)
    t = V.done(nc.vector.tensor_tensor(ex[:, :, :], logits, bcast(mx[:, :].unsqueeze(2), [P, NT, E]), ALU.subtract))
    A.wait(t)
    t = A.done(nc.scalar.activation(ex[:, :, :], ex[:, :, :], ACT.Exp))
    V.wait(t)
    t = V.done(nc.vector.tensor_reduce(pr[:, :], ex[:, :, :], AX.X, ALU.add))
    V.wait(t)
    t_pr = V.done(nc.vector.reciprocal(pr[:, :], pr[:, :]))
    V.wait(t_hot)
    t_hb = V.done(nc.vector.tensor_copy(hotb[:, :, :], hot[:, :, :]))
    V.done(nc.vector.tensor_copy(tri[:, :], n.before[:, :]))
    PE.wait(t_pr)
    for g in range(NT // 4):
        for i in range(4):
            t = PE.done(nc.tensor.transpose(ps[:, 4 + g % 4, i * P:(i + 1) * P],
                                            bcast(pr[:, 4 * g + i:4 * g + i + 1], [P, P]), n.ident[:, :]))
        A.wait(t)
        t_row = A.done(nc.scalar.activation(prow[:, g * 512:(g + 1) * 512], ps[:, 4 + g % 4, :], ACT.Copy))
    V.wait(t_row)
    free = [None, None]
    for i in range(NT):
        s = i % 2
        V.wait(free[s])
        me = slice(i * P, (i + 1) * P)
        if i:
            t = V.done(nc.vector.tensor_scalar(gt[:, s, 0:i * P], prow[:, 0:i * P], pr[:, i:i + 1], None, ALU.is_lt))
        if i < NT - 1:
            t = V.done(nc.vector.tensor_scalar(gt[:, s, (i + 1) * P:], prow[:, (i + 1) * P:], pr[:, i:i + 1], None, ALU.is_le))
        V.wait(t)
        t = V.done(nc.vector.scalar_tensor_tensor(eq[:, :], prow[:, me], pr[:, i:i + 1], tri[:, :], ALU.is_equal, ALU.mult))
        V.wait(t)
        t = V.done(nc.vector.scalar_tensor_tensor(gt[:, s, me], prow[:, me], pr[:, i:i + 1], eq[:, :], ALU.is_lt, ALU.add))
        PE.wait(t, t_hb)
        for j in range(NT):
            k = nc.tensor.matmul(ps[:, 3, j * E:(j + 1) * E], gt[:, s, j * P:(j + 1) * P], hotb[:, i, :],
                                 start=(i == 0 and j == 0), stop=(i == NT - 1), skip_group_check=True)
        free[s] = PE.done(k)
    V.wait(free[s], t_hot)
    t = V.done(nc.vector.tensor_tensor(rank[:, :, :], ps[:, 3, 0:NT * E].rearrange("p (t e) -> p t e", e=E),
                                       hot[:, :, :], ALU.mult))
    V.wait(t)
    t = V.done(nc.vector.tensor_reduce(rk[:, :], rank[:, :, :], AX.X, ALU.add))
    V.wait(t)
    t = V.done(nc.vector.tensor_scalar(rk[:, :], rk[:, :], float(cap), None, ALU.is_lt))
    V.wait(t)
    t = V.done(nc.vector.tensor_tensor(hot[:, :, 1:E], hot[:, :, 1:E], bcast(rk[:, :].unsqueeze(2), [P, NT, E - 1]), ALU.mult))
    V.wait(t)
    t = V.done(nc.vector.tensor_reduce(rk[:, :], hot[:, :, 1:E], AX.X, ALU.add))
    V.wait(t)
    return V.done(nc.vector.tensor_scalar(hot[:, :, 0:1], rk[:, :].unsqueeze(2), -1.0, 1.0, ALU.mult, ALU.add))


def dispatch(n, sb, hot, t_hot, tiles, bank, slots, experts):
    nc, V, PE = n.nc, n.V, n.PE
    NT, E = hot.shape[1:]
    ps = n.psum
    tot = sb("tot", [P, 2, NT + 1, E])
    cnt = sb("cnt", [P, E, NT])
    nt = sb("nt", [P, 2, E + 1])
    te = sb("te", [P, tiles, E])
    tef = sb("tef", [P, tiles])
    pos = sb("pos", [P, NT, E])
    sl = sb("sl", [P, NT])
    hv = hot[:, :, :].rearrange("p t e -> p (t e)")
    PE.wait(t_hot)
    w = NT * E
    nc.tensor.matmul(ps[:, bank, 0:w], n.before[:, :], hv, start=True, stop=True)
    t = PE.done(nc.tensor.matmul(ps[:, bank, w:2 * w], n.ones[:, :], hv, start=True, stop=True))
    within = ps[:, bank, 0:w].rearrange("p (t e) -> p t e", e=E)
    V.wait(t)
    t = V.done(nc.vector.memset(tot[:, :, 0, :], 0.0))
    a = V.done(nc.vector.tensor_copy(tot[:, 0, 1:NT + 1, :], ps[:, bank, w:2 * w].rearrange("p (t e) -> p t e", e=E)))
    src, d = 0, 1
    while d < NT:
        V.wait(a)
        V.done(nc.vector.tensor_copy(tot[:, 1 - src, 1:d + 1, :], tot[:, src, 1:d + 1, :]))
        a = V.done(nc.vector.tensor_tensor(tot[:, 1 - src, d + 1:NT + 1, :], tot[:, src, d + 1:NT + 1, :],
                                           tot[:, src, 1:NT + 1 - d, :], ALU.add))
        src, d = 1 - src, 2 * d
    V.wait(a)
    a = V.done(nc.vector.tensor_tensor(cnt[:, :, :], bcast(tot[:, src, NT, :].unsqueeze(2), [P, E, NT]),
                                       bcast(n.steps[:, :].unsqueeze(1), [P, E, NT]), ALU.is_gt))
    V.wait(a)
    V.done(nc.vector.memset(nt[:, :, 0:1], 0.0))
    a = V.done(nc.vector.tensor_reduce(nt[:, 0, 1:E + 1], cnt[:, :, :], AX.X, ALU.add))
    cur, d = 0, 1
    while d < E:
        V.wait(a)
        V.done(nc.vector.tensor_copy(nt[:, 1 - cur, 1:d + 1], nt[:, cur, 1:d + 1]))
        a = V.done(nc.vector.tensor_tensor(nt[:, 1 - cur, d + 1:E + 1], nt[:, cur, d + 1:E + 1], nt[:, cur, 1:E + 1 - d], ALU.add))
        cur, d = 1 - cur, 2 * d
    V.wait(a)
    a = V.done(nc.vector.tensor_tensor(te[:, :, :], bcast(nt[:, cur, 1:E + 1].unsqueeze(1), [P, tiles, E]),
                                       bcast(n.count[:, 0:tiles].unsqueeze(2), [P, tiles, E]), ALU.is_le))
    V.wait(a)
    a = V.done(nc.vector.tensor_reduce(tef[:, :], te[:, :, :], AX.X, ALU.add))
    V.wait(a)
    t_te = V.done(nc.vector.tensor_scalar(experts[:, :], tef[0:1, :], float(E - 1), None, ALU.min))
    a = V.done(nc.vector.scalar_tensor_tensor(pos[:, :, :], bcast(nt[:, cur, 0:E].unsqueeze(1), [P, NT, E]), float(P),
                                              tot[:, src, 0:NT, :], ALU.mult, ALU.add))
    V.wait(a)
    a = V.done(nc.vector.tensor_tensor(pos[:, :, :], within, pos[:, :, :], ALU.add))
    V.wait(a)
    a = V.done(nc.vector.tensor_tensor(pos[:, :, :], pos[:, :, :], hot[:, :, :], ALU.mult))
    V.wait(a)
    a = V.done(nc.vector.tensor_reduce(sl[:, :], pos[:, :, :], AX.X, ALU.add))
    V.wait(a)
    return V.done(nc.vector.tensor_copy(slots[:, :], sl[:, :])), t_te


def scatter(n, rows, x_all, slots, t_in, name):
    n.G.wait(*t_in)
    d = n.book.dma(name, 0)
    for i in range(x_all.shape[1]):
        t = d.mark(n.nc.gpsimd.indirect_dma_start(rows, bass.IndirectOffsetOnAxis(slots[:, i:i + 1], 0), x_all[:, i, :], None))
    return t


def gather(n, rows, out, slots, t_in, name):
    n.G.wait(*t_in)
    d = n.book.dma(name, 0)
    for i in range(out.shape[1]):
        t = d.mark(n.nc.gpsimd.indirect_dma_start(out[:, i, :], None, rows, bass.IndirectOffsetOnAxis(slots[:, i:i + 1], 0)))
    return t



def relu_experts(n, x_all, y_all, stats, t_x):
    nc, io, PE, A, V, G, S, ps = n.nc, n.io, n.PE, n.A, n.V, n.G, n.S, n.psum
    E, _, F = io["L0_ffn_W1"].shape
    FC = F // P
    NT = x_all.shape[1]
    cap = -(-NT * P * 5 // (4 * E))
    tiles = n.tiles
    with ExitStack() as mem:
        sb = lambda name, shape, dt=F32: n.sb("r_" + name, shape, dt, mem)
        W1 = sb("W1", [P, E * F])
        W2 = sb("W2", [P, E * FC * P])
        b1 = sb("b1", [P, E * FC])
        b1raw = sb("b1raw", [E, F])
        b2 = sb("b2", [P, E * P])
        rraw = sb("rraw", [E, P])
        rT = sb("rT", [P, E])
        d_w = n.book.dma("relu_weights")
        for dst, src in ((rraw[:, :], io["L0_ffn_router_w"]), (b1raw[:, :], io["L0_ffn_b1"]),
                         (b2[:, :], io["L0_ffn_b2"].rearrange("(a e) d -> a (e d)", a=1).to_broadcast([P, E * P])),
                         (W1[:, :].rearrange("p (e f) -> p e f", e=E), io["L0_ffn_W1"].rearrange("e p f -> p e f")),
                         (W2[:, :].rearrange("p (g d) -> p g d", d=P), io["L0_ffn_W2"].rearrange("e (c p) d -> p (e c) d", p=P))):
            t_w = d_w.mark(nc.sync.dma_start(dst, src))
        PE.wait(t_w)
        nc.tensor.transpose(ps[:, 2, 0:E], rraw[:, :], n.ident[0:E, 0:E])
        for c in range(FC):
            t = PE.done(nc.tensor.transpose(ps[:, 2, (c + 1) * E:(c + 2) * E], b1raw[:, c * P:(c + 1) * P], n.ident[0:E, 0:E]))
        V.wait(t)
        t_rT = V.done(nc.vector.tensor_copy(rT[:, :], ps[:, 2, 0:E]))
        t_b1 = V.done(nc.vector.tensor_copy(b1[:, :].rearrange("p (e c) -> p c e", c=FC),
                                            ps[:, 2, E:E + FC * E].rearrange("p (c e) -> p c e", c=FC)))
        slots, experts = sb("slots", [P, NT], U32), sb("experts", [1, tiles], I32)
        with ExitStack() as tmp:
            tb = lambda name, shape, dt=F32: n.sb("rr_" + name, shape, dt, tmp)
            xT = tb("xT", [P, NT * P])
            t_xT = transpose_all(n, x_all, xT, t_x)
            PE.wait(t_b1)
            t_lg, logits = router(n, xT, rT[:, :], t_xT, 2)
            mx, hot, t_mx, t_hot = top_one(n, tb, logits, t_lg)
            t_hot = capacity(n, tb, logits, mx, hot, t_mx, t_hot, cap)
            t_slots, t_te = dispatch(n, tb, hot, t_hot, tiles, 4, slots, experts)
            n.settle()
        t_sc = scatter(n, n.x_rows[0], x_all, slots, (t_slots, t_x, n.t_zero), "relu_scatter")

        xt = sb("xt", [P, 2, P])
        xT2 = sb("xT2", [P, 2, P])
        W1s = sb("W1s", [P, 2, F])
        b1s = sb("b1s", [P, 2, FC])
        h = sb("h", [P, 2, F])
        yt = sb("yt", [P, 2, P])
        d_x = [n.book.dma(f"relu_x{u}") for u in range(2)]
        d_y = [n.book.dma(f"relu_y{u}") for u in range(2)]
        S.wait(t_sc)
        for q in (PE, V):
            q.wait(t_te, t_w, t_b1)

        def pair(j):
            t_ev, t_ws, t_h = [None] * 2, [None] * 2, [None] * 2
            ev, ep = [None] * 2, [None] * 2
            for u in range(2):
                S.wait(n.prev(f"xt{u}"))
                t_l = d_x[u].mark(nc.sync.dma_start(xt[:, u, :], n.x_rows[0][bass.ds((2 * j + u) * P, P), :]))
                PE.wait(t_l, n.prev(f"xT{u}"))
                k = PE.done(nc.tensor.transpose(ps[:, u, 0:P], xt[:, u, :], n.ident[:, :]))
                n.note(f"xt{u}", k)
                A.wait(k, n.prev(f"up{u}"))
                t_ev[u] = A.done(nc.scalar.activation(xT2[:, u, :], ps[:, u, 0:P], ACT.Copy))
                n.note(f"xT{u}", t_ev[u])
                ev[u] = nc.vector.value_load(experts[0:1, bass.ds(2 * j + u, 1)], min_val=0, max_val=E - 1)
                ep[u] = nc.tensor.value_load(experts[0:1, bass.ds(2 * j + u, 1)], min_val=0, max_val=E - 1)
                V.wait(n.prev(f"up{u}"))
                V.done(nc.vector.tensor_copy(W1s[:, u, :], W1[:, bass.ds(ev[u] * F, F)]))
                V.wait(n.prev(f"h{u}"))
                t_ws[u] = V.done(nc.vector.tensor_copy(b1s[:, u, :], b1[:, bass.ds(ev[u] * FC, FC)]))
            for u in range(2):
                PE.wait(t_ev[u], t_ws[u], n.prev(f"hb{u}"))
                for c in range(FC):
                    k = nc.tensor.matmul(ps[:, 2 + u, c * P:(c + 1) * P], W1s[:, u, c * P:(c + 1) * P], xT2[:, u, :], start=True, stop=True)
                k = PE.done(k)
                n.note(f"up{u}", k)
                V.wait(k, t_ws[u], n.prev(f"dn{u}"))
                k = V.done(nc.vector.tensor_tensor(h[:, u, :].rearrange("p (c t) -> p c t", c=FC),
                                                   ps[:, 2 + u, :].rearrange("p (c t) -> p c t", c=FC),
                                                   bcast(b1s[:, u, :].unsqueeze(2), [P, FC, P]), ALU.add))
                n.note(f"hb{u}", k)
                n.note(f"h{u}", k)
                A.wait(k)
                t_h[u] = A.done(nc.scalar.activation(h[:, u, :], h[:, u, :], ACT.Relu))
            for u in range(2):
                PE.wait(t_h[u], n.prev(f"y{u}"))
                for c in range(FC):
                    k = nc.tensor.matmul(ps[:, 4 + u, 0:P], h[:, u, c * P:(c + 1) * P],
                                         W2[:, bass.ds(ep[u] * (FC * P) + c * P, P)], start=(c == 0), stop=(c == FC - 1))
                k = PE.done(k)
                n.note(f"dn{u}", k)
                V.wait(k, n.prev(f"st{u}"))
                k = V.done(nc.vector.tensor_tensor(yt[:, u, :], ps[:, 4 + u, 0:P], b2[:, bass.ds(ev[u] * P, P)], ALU.add))
                n.note(f"y{u}", k)
                S.wait(k)
                n.note(f"st{u}", d_y[u].mark(nc.sync.dma_start(n.y_rows[0][bass.ds((2 * j + u) * P, P), :], yt[:, u, :])))

        n.book.run("relu_tiles", tiles // 2, pair)
        ev = n.book.events["relu_tiles"]
        got = sb("got", [P, NT, P])
        t_g = gather(n, n.y_rows[0], got, slots, (ev["st0"], ev["st1"]), "relu_gather")
        V.wait(t_g)
        t = V.done(nc.vector.tensor_tensor(y_all[:, :, :], x_all[:, :, :], got[:, :, :], ALU.add))
        t = row_stats(n, y_all, stats, t)
        n.settle()
        return t



def softmax_attention(n, x_all, y_all, stats, t_x):
    nc, io, PE, A, V, G, S, ps = n.nc, n.io, n.PE, n.A, n.V, n.G, n.S, n.psum
    NT = x_all.shape[1]
    T = NT * P
    D = 64
    QT = 512
    NU = T // QT
    pairs = io["L1_attn_Wq"].shape[1] // (2 * D)
    scale = 1.0 / float(np.sqrt(D))
    POOL = 704
    SLOT = ((0, 1), (2, 3))
    B_O, B_P, B_M = 4, 5, 6
    with ExitStack() as mem:
        sb = lambda name, shape, dt=F32: n.sb("a_" + name, shape, dt, mem)
        xT = sb("xT", [P, T])
        Wq, Wk = (sb(a, [P, 2, 2, 2, D]) for a in ("Wq", "Wk"))
        Wv, Wo = (sb(a, [P, 2, P]) for a in ("Wv", "Wo"))
        K1, K2 = (sb(a, [P, 2, 2, T], F32R) for a in ("K1", "K2"))
        M1, M2 = (sb(a, [P, 2, 2, QT], F32R) for a in ("M1", "M2"))
        Vb = sb("Vb", [P, 2, NT, P])
        Pb = sb("Pb", [P, 4, 2 * QT])
        acc = sb("acc", [P, 2, 2 * QT])
        Or = sb("Or", [P, 2, QT])
        On = sb("On", [P, QT])
        mx = sb("mx", [P, 2, 4, NU])
        nm = sb("nm", [P, 2, 4])
        rr = sb("rr", [P, 8])
        bo = sb("bo", [P, P])
        d_q = [n.book.dma(f"att_w{u}") for u in range(2)]
        d_o = [n.book.dma(f"att_wo{u}") for u in range(2)]
        d_b = n.book.dma("att_bo")
        state = {}

        def get(key):
            if key in state:
                return state[key]
            if n.book.loop is not None:
                return n.prev(key)
            return n.book.events.get("heads", {}).get(key)

        def put(key, tick):
            state[key] = tick
            if n.book.loop is not None:
                n.note(key, tick)

        def load_qkv(pair, par):
            cols = slice(pair * P, (pair + 1) * P) if isinstance(pair, int) else bass.ds(pair * P, P)
            S.wait(get(f"Wq{par}"), get(f"Wk{par}"), get(f"Wv{par}"))
            for dst, name in ((Wq, "L1_attn_Wq"), (Wk, "L1_attn_Wk")):
                for twice in range(2):
                    d_q[par].mark(nc.sync.dma_start(dst[:, par, :, twice, :],
                                                    io[name][:, cols].rearrange("p (h d) -> p h d", h=2)))
            put(f"dq{par}", d_q[par].mark(nc.sync.dma_start(Wv[:, par, :], io["L1_attn_Wv"][:, cols])))

        def load_o(pair, par):
            rows = slice(pair * P, (pair + 1) * P) if isinstance(pair, int) else bass.ds(pair * P, P)
            S.wait(get(f"Wo{par}"))
            put(f"do{par}", d_o[par].mark(nc.sync.dma_start(Wo[:, par, :], io["L1_attn_Wo"][rows, :])))

        def keys_job(par, qt, h):
            at = slice(qt * QT, (qt + 1) * QT)
            PE.wait(get(f"dq{par}"), get("B_P"))
            k = PE.done(nc.tensor.matmul(ps[:, B_P, :], Wk[:, par, h].rearrange("p a d -> p (a d)"), xT[:, at], start=True, stop=True))
            put(f"Wk{par}", k)
            A.wait(k, get(f"K{par}"))
            k = A.done(nc.scalar.activation(K1[:, par, h, at], ps[:, B_P, :], ACT.Copy))
            V.wait(k, get(f"K{par}"))
            k = V.done(nc.vector.tensor_tensor(K2[0:D, par, h, at], ps[0:D, B_P, :], K1[0:D, par, h, at].bitcast(F32), ALU.subtract))
            put("B_P", k)
            put(f"Kready{par}{h}", k)

        def values_job(par, qt):
            PE.wait(get(f"dq{par}"), get("B_P"))
            for i in range(4):
                k = nc.tensor.matmul(ps[:, B_P, i * P:(i + 1) * P], xT[:, (4 * qt + i) * P:(4 * qt + i + 1) * P], Wv[:, par, :], start=True, stop=True)
            k = PE.done(k)
            put(f"Wv{par}", k)
            A.wait(k, get(f"K{par}"))
            k = A.done(nc.scalar.activation(Vb[:, par, 4 * qt:4 * qt + 4, :].rearrange("p a d -> p (a d)"), ps[:, B_P, :], ACT.Copy))
            put("B_P", k)
            put(f"Vready{par}", k)

        def queries_job(par, u, qt, h):
            PE.wait(get(f"dq{par}"), get("B_P"))
            k = PE.done(nc.tensor.matmul(ps[:, B_P, :], Wq[:, par, h].rearrange("p a d -> p (a d)"), xT[:, qt * QT:(qt + 1) * QT], start=True, stop=True))
            put(f"Wq{par}", k)
            A.wait(k, get(f"M{u}"))
            k1 = A.done(nc.scalar.activation(M1[:, u, h, :], ps[:, B_P, :], ACT.Copy))
            k = A.done(nc.scalar.activation(M2[0:D, u, h, :], ps[0:D, B_P, :], ACT.Copy))
            V.wait(k)
            k = V.done(nc.vector.tensor_tensor(M1[D:P, u, h, :], ps[D:P, B_P, :], M1[D:P, u, h, :].bitcast(F32), ALU.subtract))
            put("B_P", k)
            put(f"Q{u}{h}", k)

        def max_job(par, u, k):
            h, qc, quarter, bank = k // 16, (k % 16) // 4, k % 4, B_M + k % 2
            PE.wait(get(f"Q{u}{h}"), get(f"Kready{par}{h}"), get(f"B{bank}"))
            t = PE.done(nc.tensor.matmul(ps[:, bank, :], M1[:, u, h, qc * P:(qc + 1) * P],
                                         K1[:, par, h, quarter * QT:(quarter + 1) * QT], start=True, stop=True))
            V.wait(t)
            put(f"B{bank}", V.done(nc.vector.tensor_reduce(mx[:, h, qc, quarter:quarter + 1], ps[:, bank, :], AX.X, ALU.max)))

        def max_row_job(u, h):
            V.wait(get(f"B{B_M}"), get(f"B{B_M + 1}"), get(f"nm{h}"))
            k = V.done(nc.vector.tensor_reduce(nm[:, h, :], mx[:, h, :, :], AX.X, ALU.max, negate=True))
            PE.wait(k, get("B_P"))
            for qc in range(4):
                k = nc.tensor.matmul(ps[D:D + 1, B_P, qc * P:(qc + 1) * P], nm[:, h, qc:qc + 1], n.ident[:, :], start=True, stop=True)
            k = PE.done(k)
            put(f"nm{h}", k)
            A.wait(k)
            k = A.done(nc.scalar.activation(M2[D:D + 1, u, h, :], ps[D:D + 1, B_P, :], ACT.Copy))
            put("B_P", k)
            put(f"M2ready{u}{h}", k)

        def scores(step, par, u, kc):
            b = SLOT[step % 2]
            PE.wait(get(f"slot{step % 2}"), get(f"M2ready{u}0"), get(f"M2ready{u}1"), get(f"Kready{par}1"))
            for h in range(2):
                at = slice(kc * P, (kc + 1) * P)
                nc.tensor.matmul(ps[:, b[h], :], K1[:, par, h, at], M1[:, u, h, :], start=True, stop=False)
                k = nc.tensor.matmul(ps[:, b[h], :], K2[0:D + 1, par, h, at], M2[0:D + 1, u, h, :], start=False, stop=True)
            k = PE.done(k)
            put(f"M{u}", k)
            put(f"Klast{par}", k)
            buf = step % 4
            A.wait(k, get(f"pv{buf}"), get(f"addv{buf}"), get(f"addg{buf}"))
            k = A.done(nc.scalar.activation(Pb[:, buf, :], ps[:, b[0]:b[0] + 2, :].rearrange("p a b -> p (a b)"), ACT.Exp, scale=scale))
            put(f"slot{step % 2}", k)
            put(f"exp{buf}", k)

        def weigh(step, par, u, kc):
            buf = step % 4
            PE.wait(get(f"exp{buf}"), get(f"Vready{par}"))
            if kc == 0:
                PE.wait(get("B_O"))
            for h in range(2):
                k = nc.tensor.matmul(ps[h * D:(h + 1) * D, B_O, :], Vb[:, par, kc, h * D:(h + 1) * D], Pb[:, buf, h * QT:(h + 1) * QT],
                                     start=(kc == 0), stop=(kc == NT - 1))
            k = PE.done(k)
            put(f"pv{buf}", k)
            if kc == NT - 1:
                A.wait(k, get(f"Or{u}"))
                k = A.done(nc.scalar.activation(Or[:, u, :], ps[:, B_O, :], ACT.Copy))
                put("B_O", k)
                put(f"Oraw{u}", k)
            if kc == 0:
                return
            for q, at, key, op in ((V, slice(POOL, 2 * QT), "addv", nc.vector.tensor_tensor),
                                   (G, slice(0, POOL), "addg", nc.gpsimd.tensor_tensor)):
                q.wait(get(f"exp{buf}"), get(f"{key}"), get(f"sums{u}") if kc == 1 else None)
                first = Pb[:, (step - 1) % 4, at] if kc == 1 else acc[:, u, at]
                k = q.done(op(acc[:, u, at], first, Pb[:, buf, at], ALU.add))
                put(key, k)
                put(f"{key}{buf}", k)
                if kc == 1:
                    put(f"{key}{(step - 1) % 4}", k)

        def sums_job(u):
            PE.wait(get("addv"), get("addg"), get("B_P"))
            for i in range(8):
                k = nc.tensor.matmul(ps[:, B_P, i:i + 1], acc[:, u, i * P:(i + 1) * P], n.ones[:, 0:1], start=True, stop=True)
            k = PE.done(k)
            put(f"sums{u}", k)
            V.wait(k, get("rr_free"))
            k = V.done(nc.vector.reciprocal(rr[:, :], ps[:, B_P, 0:8]))
            put("B_P", k)
            put("rr", k)

        def normalise_job(u):
            PE.wait(get("rr"), get("B_P"))
            for i in range(8):
                h, qc = i // 4, i % 4
                k = nc.tensor.matmul(ps[h * D:(h + 1) * D, B_P, qc * P:(qc + 1) * P], bcast(rr[:, i:i + 1], [P, D]), n.ident[:, :], start=True, stop=True)
            k = PE.done(k)
            put("rr_free", k)
            V.wait(k, get(f"Oraw{u}"), get("On_free"))
            k = V.done(nc.vector.tensor_tensor(On[:, :], ps[:, B_P, :], Or[:, u, :], ALU.mult))
            put("B_P", k)
            put(f"Or{u}", k)
            put("On", k)

        def output_job(par, qt):
            PE.wait(get("On"), get("B_P"), get(f"do{par}"))
            for i in range(4):
                k = nc.tensor.matmul(ps[:, B_P, i * P:(i + 1) * P], On[:, i * P:(i + 1) * P], Wo[:, par, :], start=True, stop=True)
            k = PE.done(k)
            put("On_free", k)
            put(f"Wo{par}", k)
            yq = y_all[:, 4 * qt:4 * qt + 4, :]
            V.wait(k, get(f"y{qt}"))
            k = V.done(nc.vector.tensor_tensor(yq, ps[:, B_P, :].rearrange("p (a d) -> p a d", a=4), yq, ALU.add))
            put("B_P", k)
            put(f"y{qt}", k)

        t_b = d_b.mark(nc.sync.dma_start(bo[:, :], io["L1_attn_bo"].rearrange("(a d) -> a d", a=1).to_broadcast([P, P])))
        load_qkv(0, 0)
        load_qkv(1, 1)
        load_o(0, 0)
        t_one = V.done(nc.vector.memset(K2[D:D + 1, :, :, :].bitcast(F32), 1.0))
        t_xT = transpose_all(n, x_all, xT, t_x, (0, 1, 2, 3))
        G.wait(t_b, t_x)
        G.done(nc.gpsimd.tensor_tensor(y_all[:, :, :], x_all[:, :, :], bcast(bo[:, :].unsqueeze(1), [P, NT, P]), ALU.add))
        PE.wait(t_xT, t_one)
        for qt in range(NU):
            for h in range(2):
                keys_job(0, qt, h)
            values_job(0, qt)
        for h in range(2):
            queries_job(0, 0, 0, h)
        for k in range(8 * NU):
            max_job(0, 0, k)
        for h in range(2):
            max_row_job(0, h)
        n.settle()
        ready = dict(state)
        state.clear()

        STEPS = NT
        MAX_AT = [(kc, point) for kc in range(3, 14) for point in range(3)]

        def body(i, last):
            units = 2 * NU
            if last or True:
                pass
            for g in range(units):
                a, qt, u = g // NU, g % NU, g % 2
                more_q = not (last and g == units - 1)
                more_k = not (last and a == 1)
                ga, gq = ((g + 1) // NU) % 2, (g + 1) % NU
                pu, pqt, pa = 1 - u, (g - 1) % NU, ((g - 1) % units) // NU
                for kc in range(STEPS):
                    step = g * STEPS + kc
                    def maxima(point):
                        if more_q and (kc, point) in MAX_AT and MAX_AT.index((kc, point)) < 8 * NU:
                            max_job(ga, 1 - u, MAX_AT.index((kc, point)))

                    maxima(0)
                    if kc < STEPS - 1:
                        scores(step + 1, a, u, kc + 1)
                    elif more_q:
                        scores(step + 1, ga, 1 - u, 0)
                    if more_k and kc in (0, 1):
                        keys_job(1 - a, qt, kc)
                    if more_q and kc in (2, 3):
                        queries_job(ga, 1 - u, gq, kc - 2)
                    if more_k and kc == 4:
                        values_job(1 - a, qt)
                    if kc == 5:
                        sums_job(pu)
                    if kc == 7:
                        normalise_job(pu)
                    if kc == 8:
                        output_job(pa, pqt)
                    maxima(1)
                    if more_q and kc == 12:
                        max_row_job(1 - u, 0)
                    if more_q and kc == 14:
                        max_row_job(1 - u, 1)
                    weigh(step, a, u, kc)
                    maxima(2)
                if qt == NU - 1:
                    put(f"K{a}", get(f"Klast{a}"))
                    if not last:
                        load_qkv(2 * i + a + 2, a)
                if qt == 0:
                    if not (last and a == 1):
                        load_o(2 * i + a + 1, 1 - a)

        V.done(nc.vector.memset(acc[:, 1, :], 1.0))
        V.done(nc.vector.memset(Or[:, 1, :], 0.0))
        S.wait(ready["dq0"])
        k = d_o[1].mark(nc.sync.dma_start(Wo[:, 1, :], io["L1_attn_Wo"][0:P, :]))
        PE.wait(k)
        n.settle()
        scores(0, 0, 0, 0)
        n.settle()
        state.clear()
        n.book.run("heads", pairs // 2 - 1, lambda i: (state.clear(), body(i, False)))
        state.clear()
        body(pairs // 2 - 1, True)
        sums_job(1)
        normalise_job(1)
        output_job(1, NU - 1)
        t = row_stats(n, y_all, stats, get(f"y{NU - 1}"))
        n.settle()
        return t



def gated_experts(n, x_all, y_all, stats, t_x):
    nc, io, PE, A, V, G, S, ps = n.nc, n.io, n.PE, n.A, n.V, n.G, n.S, n.psum
    E, _, F = io["L1_ffn_w1_eDF"].shape
    FC = -(-F // P)
    FP, FL = FC * P, F - (FC - 1) * P
    NT = x_all.shape[1]
    tiles = n.tiles
    QT = 512
    with ExitStack() as mem:
        sb = lambda name, shape, dt=F32: n.sb("g_" + name, shape, dt, mem)
        w13 = sb("w13", [P, E, 2, F])
        w2 = sb("w2", [P, E * FC * P])
        w2v = w2[:, :].rearrange("p (e c d) -> p e c d", e=E, c=FC)
        ws13 = sb("ws13", [P, 2, FP])
        ws2 = sb("ws2", [P, FC, P])
        rT = sb("rT", [P, E])
        w13s = sb("w13s", [P, 2, 2, FP])
        lo = FL // 32 * 32
        for part in (w2v[lo:P, :, FC - 1, :], ws2[lo:P, FC - 1, :], ws13[:, :, F:FP], w13s[:, :, :, F:FP]):
            t_pad = V.done(nc.vector.memset(part, 0.0))
        d_w = n.book.dma("gated_weights")
        S.wait(t_pad)
        full = (FC - 1) * P
        for dst, src in (
            (rT[:, :], io["L1_ffn_router_DE"]),
            (ws13[:, 0, 0:F], io["L1_ffn_ws1_DF"]), (ws13[:, 1, 0:F], io["L1_ffn_ws3_DF"]),
            (ws2[:, 0:FC - 1, :], io["L1_ffn_ws2_FD"][0:full, :].rearrange("(c p) d -> p c d", p=P)),
            (ws2[0:FL, FC - 1, :], io["L1_ffn_ws2_FD"][full:F, :]),
            (w13[:, :, 0, :], io["L1_ffn_w1_eDF"].rearrange("e p f -> p e f")),
            (w13[:, :, 1, :], io["L1_ffn_w3_eDF"].rearrange("e p f -> p e f")),
            (w2v[0:FL, :, FC - 1, :], io["L1_ffn_w2_eFD"][:, full:F, :].rearrange("e p d -> p e d")),
            *((w2v[:, :, c, :], io["L1_ffn_w2_eFD"][:, c * P:(c + 1) * P, :].rearrange("e p d -> p e d")) for c in range(FC - 1)),
        ):
            t_w = d_w.mark(nc.sync.dma_start(dst, src))
        slots, experts = sb("slots", [P, NT], U32), sb("experts", [1, tiles], I32)
        xT = sb("xT", [P, NT * P])
        xg = sb("xg", [P, NT, P])
        with ExitStack() as tmp:
            tb = lambda name, shape, dt=F32: n.sb("gr_" + name, shape, dt, tmp)
            gate = tb("gate", [P, NT])
            t_xT = transpose_all(n, x_all, xT, t_x)
            PE.wait(t_w)
            t_lg, logits = router(n, xT, rT[:, :], t_xT, 2)
            mx, hot, t_mx, t_hot = top_one(n, tb, logits, t_lg)
            A.wait(t_mx)
            t = A.done(nc.scalar.activation(gate[:, :], mx[:, :], ACT.Sigmoid))
            G.wait(t)
            t_xg = G.done(nc.gpsimd.tensor_tensor(xg[:, :, :], x_all[:, :, :], bcast(gate[:, :].unsqueeze(2), [P, NT, P]), ALU.mult))
            t_slots, t_te = dispatch(n, tb, hot, t_hot, tiles, 3, slots, experts)
            n.settle()
        t_sc = scatter(n, n.x_rows[1], xg, slots, (t_slots, t_xg, n.t_zero), "gated_scatter")

        sg = sb("sg", [P, FC, QT])
        hh = sb("hh", [P, FC, QT])

        def shared(i):
            PE.wait(n.prev("t"), n.prev("h"))
            ks = []
            for m in range(2):
                for c in range(FC):
                    k = PE.done(nc.tensor.matmul(ps[:, 3 * m + c, :], ws13[:, m, c * P:(c + 1) * P], xT[:, bass.ds(i * QT, QT)], start=True, stop=True))
                    ks.append(k)
            for c in range(FC):
                A.wait(ks[c], n.prev("h"))
                k = A.done(nc.scalar.activation(sg[:, c, :], ps[:, c, :], ACT.Sigmoid))
                V.wait(k)
                k = V.done(nc.vector.tensor_tensor(sg[:, c, :], ps[:, c, :], sg[:, c, :], ALU.mult))
                n.note("t", k)
                V.wait(k, ks[FC + c], n.prev("down"))
                k = V.done(nc.vector.tensor_tensor(hh[:, c, :], ps[:, 3 + c, :], sg[:, c, :], ALU.mult))
            n.note("h", k)
            PE.wait(k, n.prev("y"))
            for t in range(4):
                for c in range(FC):
                    k = nc.tensor.matmul(ps[:, 6, t * P:(t + 1) * P], hh[:, c, t * P:(t + 1) * P], ws2[:, c, :], start=(c == 0), stop=(c == FC - 1))
            k = PE.done(k)
            n.note("down", k)
            V.wait(k)
            at = bass.ds(i * 4, 4)
            n.note("y", V.done(nc.vector.tensor_tensor(y_all[:, at, :], ps[:, 6, :].rearrange("p (a d) -> p a d", a=4),
                                                       x_all[:, at, :], ALU.add)))

        PE.wait(t_w)
        n.book.run("shared", NT * P // QT, shared)

        xt = sb("xt", [P, 2, P])
        xT2 = sb("xT2", [P, 2, P])
        sig = sb("sig", [P, 2, FP])
        h = sb("h", [P, 2, FP])
        yt = sb("yt", [P, 2, P])
        d_x = [n.book.dma(f"gated_x{u}") for u in range(2)]
        d_y = [n.book.dma(f"gated_y{u}") for u in range(2)]
        S.wait(t_sc)
        n.settle()

        def pair(j):
            t_ev, t_ws, t_h, ep = ([None] * 2 for _ in range(4))
            for u in range(2):
                S.wait(n.prev(f"xt{u}"))
                t_l = d_x[u].mark(nc.sync.dma_start(xt[:, u, :], n.x_rows[1][bass.ds((2 * j + u) * P, P), :]))
                PE.wait(t_l, n.prev(f"y{u}"))
                k = PE.done(nc.tensor.transpose(ps[:, 6 + u, 0:P], xt[:, u, :], n.ident[:, :]))
                n.note(f"xt{u}", k)
                A.wait(k, n.prev(f"up{u}"))
                t_ev[u] = A.done(nc.scalar.activation(xT2[:, u, :], ps[:, 6 + u, 0:P], ACT.Copy))
                ev = nc.vector.value_load(experts[0:1, bass.ds(2 * j + u, 1)], min_val=0, max_val=E - 1)
                ep[u] = nc.tensor.value_load(experts[0:1, bass.ds(2 * j + u, 1)], min_val=0, max_val=E - 1)
                V.wait(n.prev(f"up{u}"))
                t_ws[u] = V.done(nc.vector.tensor_copy(w13s[:, u, :, 0:F], w13[:, bass.ds(ev, 1), :, :].rearrange("p a b f -> p (a b) f")))
            for u in range(2):
                PE.wait(t_ev[u], t_ws[u], n.prev(f"h{u}"))
                for m in range(2):
                    for c in range(FC):
                        k = nc.tensor.matmul(ps[:, 2 + 2 * u + m, c * P:(c + 1) * P], w13s[:, u, m, c * P:(c + 1) * P], xT2[:, u, :], start=True, stop=True)
                k = PE.done(k)
                n.note(f"up{u}", k)
                A.wait(k, n.prev(f"h{u}"))
                k = A.done(nc.scalar.activation(sig[:, u, :], ps[:, 2 + 2 * u, 0:FP], ACT.Sigmoid))
                V.wait(k)
                k = V.done(nc.vector.tensor_tensor(sig[:, u, :], ps[:, 2 + 2 * u, 0:FP], sig[:, u, :], ALU.mult))
                V.wait(k, n.prev(f"dn{u}"))
                t_h[u] = V.done(nc.vector.tensor_tensor(h[:, u, :], ps[:, 3 + 2 * u, 0:FP], sig[:, u, :], ALU.mult))
                n.note(f"h{u}", t_h[u])
            for u in range(2):
                PE.wait(t_h[u], t_ev[u])
                for c in range(FC):
                    k = nc.tensor.matmul(ps[:, 6 + u, P:2 * P], h[:, u, c * P:(c + 1) * P],
                                         w2[:, bass.ds(ep[u] * (FC * P) + c * P, P)], start=(c == 0), stop=(c == FC - 1))
                k = PE.done(k)
                n.note(f"dn{u}", k)
                A.wait(k, n.prev(f"st{u}"))
                k = A.done(nc.scalar.activation(yt[:, u, :], ps[:, 6 + u, P:2 * P], ACT.Copy))
                n.note(f"y{u}", k)
                S.wait(k)
                n.note(f"st{u}", d_y[u].mark(nc.sync.dma_start(n.y_rows[1][bass.ds((2 * j + u) * P, P), :], yt[:, u, :])))

        n.book.run("gated_tiles", tiles // 2, pair)
        ev = n.book.events["gated_tiles"]
        t_g = gather(n, n.y_rows[1], xg, slots, (ev["st0"], ev["st1"], t_sc), "gated_gather")
        V.wait(t_g)
        t = V.done(nc.vector.tensor_tensor(y_all[:, :, :], y_all[:, :, :], xg[:, :, :], ALU.add))
        t = row_stats(n, y_all, stats, t)
        n.settle()
        return t


def program(nc, known, io, out, debug=None, start=0):
    with ExitStack() as ctx:
        n = Net(nc, ctx, known, io)
        NT = io["L0_attn_hidden_states"].shape[1] // P
        E = io["L0_ffn_W1"].shape[0]
        n.tiles = NT + E
        constants(n)
        x_all = n.sb("x_all", [P, NT, P])
        y_all = n.sb("y_all", [P, NT, P])
        stats = n.sb("stats", [P, NT, 6])
        n.mv = n.sb("mv", [P, NT, 2])
        n.sd = n.sb("sd", [P, NT])
        n.x_rows = [nc.dram_tensor(f"x_rows{i}", (n.tiles * P, P), F32, kind="Internal").ap() for i in range(2)]
        n.y_rows = [nc.dram_tensor(f"y_rows{i}", (n.tiles * P, P), F32, kind="Internal").ap() for i in range(2)]
        n.G.wait(n.t_const)
        zero = n.sb("zero", [P, P])
        t = n.G.done(nc.gpsimd.memset(zero[:, :], 0.0))
        d_z = n.book.dma("zero_rows")
        n.A.wait(t)
        for i in range(2):
            n.t_zero = d_z.mark(nc.scalar.dma_start(n.x_rows[i].rearrange("(t p) d -> p t d", p=P),
                                                    bcast(zero[:, :].unsqueeze(1), [P, n.tiles, P])))
        d_in = n.book.dma("x_in")
        src = io["L0_attn_hidden_states"] if not start else debug["x"]
        t_in = d_in.mark(nc.sync.dma_start(x_all[:, :, :], src.rearrange("b (t p) d -> p (b t) d", p=P)))
        n.V.wait(t_in)
        d = n.book.dma("dbg")

        def dump(name, src, t):
            if debug and name in debug:
                n.S.wait(t)
                n.S.wait(d.mark(nc.sync.dma_start(debug[name].rearrange("(t p) d -> p t d", p=P), src[:, :, :])))
        if start < 1:
            t = ttt_attention(n, x_all, y_all, stats)
            dump("y1", y_all, t)
            t_in = layer_norm(n, y_all, stats, t, x_all)
            dump("x1", x_all, t_in)
        n.settle()
        if start < 2:
            t = relu_experts(n, x_all, y_all, stats, t_in)
            t_in = layer_norm(n, y_all, stats, t, x_all)
            dump("x2", x_all, t_in)
        if start < 3:
            t = softmax_attention(n, x_all, y_all, stats, t_in)
            t_in = layer_norm(n, y_all, stats, t, x_all)
            dump("x3", x_all, t_in)
        t = gated_experts(n, x_all, y_all, stats, t_in)
        t_in = layer_norm(n, y_all, stats, t, x_all)
        n.S.wait(t_in, n.t_zero)
        n.S.wait(d.mark(nc.sync.dma_start(out.rearrange("b (t p) d -> p (b t) d", p=P), x_all[:, :, :])))
        return n.book.found


_INS = ['L0_attn_hidden_states', 'L0_attn_qkv_w', 'L0_attn_q_norm_w', 'L0_attn_k_norm_w', 'L0_attn_lr_proj_w',
        'L0_attn_lr_proj_b', 'L0_attn_w0', 'L0_attn_w1', 'L0_attn_w2', 'L0_ffn_router_w', 'L0_ffn_W1', 'L0_ffn_b1',
        'L0_ffn_W2', 'L0_ffn_b2', 'L1_attn_Wq', 'L1_attn_Wk', 'L1_attn_Wv', 'L1_attn_Wo', 'L1_attn_bo',
        'L1_ffn_router_DE', 'L1_ffn_w1_eDF', 'L1_ffn_w3_eDF', 'L1_ffn_w2_eFD', 'L1_ffn_ws1_DF', 'L1_ffn_ws3_DF',
        'L1_ffn_ws2_FD']


def kernel(**inputs):
    import concourse.bacc as _bacc
    from concourse.bass_utils import run_bass_kernel_spmd as _run

    arrays = {f"in_{name}_dram": np.ascontiguousarray(inputs[name]) for name in _INS}
    known = {}
    for _ in range(2):
        nc = _bacc.Bacc("TRN2", target_bir_lowering=False, num_devices=1)
        io = {name: nc.dram_tensor(f"in_{name}_dram", arrays[f"in_{name}_dram"].shape, F32, kind="ExternalInput").ap()
              for name in _INS}
        out = nc.dram_tensor("out_0_dram", (1, 2048, 128), F32, kind="ExternalOutput").ap()
        known = program(nc, known, io, out)
    r = _run(nc, [arrays], core_ids=[0])
    return r.results[0]["out_0_dram"]
```

```python
from contextlib import ExitStack

import numpy as np

import concourse.bass as bass
import concourse.mybir as mybir

F32 = mybir.dt.float32
F32R = mybir.dt.float32r
BF16 = mybir.dt.bfloat16
I32 = mybir.dt.int32
U32 = mybir.dt.uint32
ALU = mybir.AluOpType
ACT = mybir.ActivationFunctionType
AX = mybir.AxisListType

P = 128
LN_EPS = 1e-5
TILE = 256
TP = TILE // P
CREDIT = 1000


class Tick:

    def __init__(self, counter, value, loop=None):
        self.counter, self.value, self.loop = counter, value, loop

    def back(self, n=1):
        t = Tick(self.counter, self.value, self.loop)
        t.value -= n * self.loop.per(self.counter)
        return t


class Loop:

    def __init__(self, book, name, n):
        self.book, self.name, self.n = book, name, n
        self.open = True
        self.start = {c: c.count for c in book.counters}
        self.index = None

    def per(self, counter):
        return self.book.known.get((self.name, counter.name), 0)

    def close(self):
        self.open = False
        for c in self.book.counters:
            raised = c.count - self.start[c]
            self.book.found[(self.name, c.name)] = raised
            c.count = self.start[c] + self.n * raised


class Counter:

    def __init__(self, book, name, step, credit=CREDIT):
        self.book, self.name, self.step = book, name, step
        self.sem = book.ctx.enter_context(book.nc.semaphore(name))
        self.count = credit
        book.counters.append(self)
        if credit:
            book.nc.sync.sem_inc(self.sem, credit)

    def mark(self, instruction):
        instruction.then_inc(self.sem, self.step)
        self.count += self.step
        return Tick(self, self.count, self.book.loop)


class Queue:

    def __init__(self, book, name, engine):
        self.book, self.name, self.engine = book, name, engine
        self.counter = Counter(book, f"done_{name}", 1)
        self.seen = {}

    def wait(self, *ticks):
        for t in ticks:
            if t is None:
                continue
            loop, value = t.loop, t.value
            if loop is not None and not loop.open:
                value += (loop.n - 1) * loop.per(t.counter)
                loop = None
            key = (t.counter, loop)
            if self.seen.get(key, -1) >= value:
                continue
            self.seen[key] = value
            if loop is None:
                self.engine.wait_ge(t.counter.sem, value)
            else:
                self.engine.wait_ge(t.counter.sem, loop.index * loop.per(t.counter) + value)

    def done(self, instruction):
        return self.counter.mark(instruction)


class Book:

    def __init__(self, nc, ctx, known):
        self.nc, self.ctx, self.known, self.found = nc, ctx, known, {}
        self.counters, self.loop, self.events = [], None, {}
        self.queues = [Queue(self, n, e) for n, e in (
            ("pe", nc.tensor), ("act", nc.scalar), ("dve", nc.vector), ("pool", nc.gpsimd), ("sp", nc.sync))]
        self.names = 0

    def dma(self, name, credit=CREDIT):
        return Counter(self, name, 16, credit)

    def run(self, name, n, body):
        loop = Loop(self, name, n)
        for q in self.queues:
            q.seen = {k: v for k, v in q.seen.items() if k[1] is None}
        with self.nc.Fori(0, n, 1) as i:
            loop.index, self.loop = i, loop
            self.events[name] = {}
            body(i)
        self.loop = None
        loop.close()
        for q in self.queues:
            q.seen = {k: v for k, v in q.seen.items() if k[1] is None}


def bcast(ap, shape):
    return ap.to_broadcast(list(shape))


class Net:

    def __init__(self, nc, ctx, known, io):
        self.nc, self.ctx, self.io = nc, ctx, io
        self.book = Book(nc, ctx, known)
        self.PE, self.A, self.V, self.G, self.S = self.book.queues
        self.psum = ctx.enter_context(nc.psum_tensor("psum", [P, 8, 512], F32))
        self.scratch = None

    def note(self, key, tick):
        book = self.book
        book.events[book.loop.name][key] = tick
        book.found[("event", book.loop.name, key)] = (tick.counter.name, tick.value - tick.loop.start[tick.counter])

    def prev(self, key):
        book, loop = self.book, self.book.loop
        if ("event", loop.name, key) not in book.known:
            return None
        name, offset = book.known[("event", loop.name, key)]
        counter = next(c for c in book.counters if c.name == name)
        return Tick(counter, loop.start[counter] + offset - loop.per(counter), loop)

    def settle(self, *queues):
        ticks = [Tick(q.counter, q.counter.count) for q in self.book.queues]
        for q in queues or self.book.queues:
            q.wait(*ticks)

    def sb(self, name, shape, dt=F32, ctx=None):
        return (ctx or self.ctx).enter_context(self.nc.sbuf_tensor(name, shape, dt))


class Carry:

    def __init__(self, n, name):
        self.n, self.name, self.now = n, name, {}

    def get(self, key):
        if key in self.now:
            return self.now[key]
        if self.n.book.loop is not None:
            return self.n.prev(key)
        return self.n.book.events.get(self.name, {}).get(key)

    def put(self, key, tick):
        self.now[key] = tick
        if self.n.book.loop is not None:
            self.n.note(key, tick)
        return tick

    def loop(self, count, body):
        self.n.settle()
        self.now = {}

        def fresh(i):
            self.now = {}
            body(i)

        self.n.book.run(self.name, count, fresh)
        self.now = {}


def constants(n):
    nc, G = n.nc, n.G
    n.ident = n.sb("ident", [P, P])
    n.ones = n.sb("ones", [P, P])
    n.blocks = n.sb("blocks", [P, P])
    n.mask4 = n.sb("mask4", [P, 4, 64])
    n.before = n.sb("before", [P, P])
    n.eps = n.sb("eps", [P, 4])
    ts = [G.done(nc.gpsimd.memset(t, v)) for t, v in (
        (n.ident[:, :], 0.0), (n.ones[:, :], 1.0), (n.blocks[:, :], 1.0), (n.mask4[:, :, :], 1.0),
        (n.before[:, :], 1.0), (n.eps[:, 0:1], 1e-6), (n.eps[:, 1:2], LN_EPS), (n.eps[:, 2:3], 1e-7),
        (n.eps[:, 3:4], 0.0))]
    G.wait(ts[-1])

    def keep(t, pattern, base, mult, op=ALU.is_ge, fill=0.0):
        k = G.done(nc.gpsimd.affine_select(out=t, in_=t, pattern=pattern, compare_op=op, fill=fill, base=base,
                                           channel_multiplier=mult))
        G.wait(k)
        return k

    keep(n.ident[:, :], [[-1, P]], 0, 1, ALU.not_equal, 1.0)
    b = n.blocks[:, :].rearrange("p (h x) -> p h x", h=4)
    keep(b, [[-32, 4], [0, 32]], 0, 1)
    keep(b, [[32, 4], [0, 32]], 31, -1)
    keep(n.mask4[:, :, :], [[-32, 4], [0, 64]], 0, 1)
    keep(n.mask4[:, :, :], [[32, 4], [0, 64]], 31, -1)
    keep(n.before[:, :], [[1, P]], -1, -1)
    n.e_less = n.sb("e_less", [P, 8])
    n.steps = n.sb("steps", [P, 16])
    n.count = n.sb("count", [P, 24])
    for t, step, base in ((n.e_less, 1, -8), (n.steps, TILE, 0), (n.count, 1, 0)):
        i32 = n.sb(f"i32_{base}_{step}", [P, t.shape[1]], I32)
        k = G.done(nc.gpsimd.iota(i32[:, :], pattern=[[step, t.shape[1]]], base=base, channel_multiplier=0))
        G.wait(k)
        n.t_const = G.done(nc.gpsimd.tensor_copy(t[:, :], i32[:, :]))



HEADS, DH, HID, CHUNK = 4, 32, 64, 256
TPC = CHUNK // P
BASE_LR_INV = float(np.log(np.expm1(0.001)))
NS = ((4.0848, -6.8946, 2.927), (3.9505, -6.3029, 2.6377), (3.7418, -5.5913, 2.3037),
      (2.8769, -3.1427, 1.2046), (2.8366, -3.0525, 1.2012))


def ttt_attention(n, x_all, y_all, stats):
    nc, io, PE, A, V, G, S, ps = n.nc, n.io, n.PE, n.A, n.V, n.G, n.S, n.psum
    NT = x_all.shape[1]
    NC = NT // TPC
    with ExitStack() as mem:
        sb = lambda name, shape, dt=F32: n.sb("t_" + name, shape, dt, mem)
        qT = sb("qT", [P, NT * P])
        kT = sb("kT", [P, NT * P])
        vT = sb("vT", [P, NT * P])
        kl0 = sb("kl0", [P, NT, P])
        kl2 = sb("kl2", [P, NT, P])
        vl1 = sb("vl1", [P, NT, P])
        wT = sb("wT", [P, 384])
        lwT = sb("lwT", [P, 12])
        lr = sb("lr", [P, NT * 12])
        Wc = sb("Wc", [P, 3, HID])
        WB = sb("WB", [P, 3, HEADS, HID])
        W1T = sb("W1T", [P, 2, P])
        N0 = sb("N0", [P, 129])
        aI = sb("aI", [P, len(NS), P])

        wraw = sb("wraw", [P, 3, P])
        lraw = sb("lraw", [12, P])
        w02 = sb("w02", [HID, 2, HEADS, DH])
        nw = sb("nw", [P, 2, P])
        lb = sb("lb", [P, 12])
        d_w = n.book.dma("ttt_weights")
        for dst, src in (
            (wraw[:, :, :], io["L0_attn_qkv_w"].rearrange("(a p) d -> p a d", p=P)),
            (lraw[:, :], io["L0_attn_lr_proj_w"]),
            (w02[:, 0], io["L0_attn_w0"].rearrange("h i d -> i h d")),
            (w02[:, 1], io["L0_attn_w2"].rearrange("h i d -> i h d")),
            (Wc[:, 2, :], io["L0_attn_w1"].rearrange("h o i -> (h o) i")),
            (nw[:, 0, :], io["L0_attn_q_norm_w"].rearrange("(a d) -> a d", a=1).to_broadcast([P, P])),
            (nw[:, 1, :], io["L0_attn_k_norm_w"].rearrange("(a d) -> a d", a=1).to_broadcast([P, P])),
            (lb[:, :], io["L0_attn_lr_proj_b"].rearrange("(a d) -> a d", a=1).to_broadcast([P, 12])),
        ):
            t_w = d_w.mark(nc.sync.dma_start(dst, src))
        PE.wait(t_w, n.t_const)
        for a in range(3):
            nc.tensor.transpose(ps[:, 0, a * P:(a + 1) * P], wraw[:, a, :], n.ident[:, :])
        nc.tensor.transpose(ps[:, 0, 384:396], lraw[:, :], n.ident[0:12, 0:12])
        for a in range(2):
            t = PE.done(nc.tensor.transpose(ps[:, 1, a * HID:(a + 1) * HID],
                                            w02[:, a].rearrange("i h d -> i (h d)"), n.ident[0:HID, 0:HID]))
        A.wait(t)
        A.done(nc.scalar.activation(wT[:, :], ps[:, 0, 0:384], ACT.Copy))
        t_wT = A.done(nc.scalar.activation(lwT[:, :], ps[:, 0, 384:396], ACT.Copy))
        V.wait(t, n.t_const)
        t_Wc = V.done(nc.vector.tensor_copy(Wc[:, 0:2, :], ps[:, 1, 0:2 * HID].rearrange("p (a i) -> p a i", a=2)))
        for k, (a, _, _) in enumerate(NS):
            t_aI = V.done(nc.vector.tensor_scalar(aI[:, k, :], n.ident[:, :], a, None, ALU.mult))
        V.wait(t_w)
        t_lb = V.done(nc.vector.tensor_scalar(lb[:, :], lb[:, :], BASE_LR_INV, None, ALU.add))

        sqw = sb("sqw", [P, 3, HID])
        rs = sb("rs", [P, 129])
        NR = sb("NR", [P, 129])
        Wn = sb("Wn", [P, 3, HID])

        def row_norms(w, t_in, out, t_free):
            A.wait(t_in, t_free)
            t_sq = A.done(nc.scalar.activation(sqw[:, :, :], w[:, :, :], ACT.Square))
            PE.wait(t_sq, n.t_b3)
            t_s = PE.done(nc.tensor.matmul(ps[:, 3, 0:2 * HID], n.blocks[:, :], sqw[:, 0:2, :], start=True, stop=True))
            V.wait(t_sq)
            t_r = V.done(nc.vector.tensor_reduce(rs[:, 0:1], sqw[:, 2, :], AX.X, ALU.add))
            A.wait(t_s, t_r)
            t1 = A.done(nc.scalar.activation(out[:, 0:2 * HID], ps[:, 3, 0:2 * HID], ACT.Sqrt))
            return A.done(nc.scalar.activation(out[:, 128:129], rs[:, 0:1], ACT.Sqrt)), t1

        def blocks_of(t_w, t_free):
            V.wait(t_w, t_free)
            t_wb = V.done(nc.vector.tensor_tensor(
                WB[:, :, :, :], bcast(Wc[:, :, :].unsqueeze(2), [P, 3, HEADS, HID]),
                bcast(n.mask4[:, :, :].unsqueeze(1), [P, 3, HEADS, HID]), ALU.mult))
            PE.wait(t_wb)
            for g in range(2):
                t = PE.done(nc.tensor.transpose(ps[:, 7, g * P:(g + 1) * P],
                                                WB[:, 2, 2 * g:2 * g + 2, :].rearrange("p a b -> p (a b)"), n.ident[:, :]))
            A.wait(t, t_free)
            return t_wb, A.done(nc.scalar.activation(W1T[:, :, :].rearrange("p a b -> p (a b)"), ps[:, 7, 0:256], ACT.Copy))

        n.t_b3 = None
        V.wait(t_Wc)
        A.wait(t_w)
        t_N0, _ = row_norms(Wc, t_Wc, N0, None)
        t_WB, t_W1T = blocks_of(t_Wc, None)

        xs = sb("xs", [P, TPC, P])
        xT = sb("xT", [P, TPC * P])
        sq = sb("sq", [P, TPC, 256])
        qw = sb("qw", [P, TPC, 256])
        vv = sb("vv", [P, TPC, P])
        ss = sb("ss", [P, 4])
        s2 = sb("s2", [P, 16])
        z = sb("z", [P, 24])
        s_ = sb("s_", [P, 24])
        w_ = sb("w_", [P, 24])
        w2_ = sb("w2_", [P, 24])
        ac = sb("ac", [P, 24])
        d_x = n.book.dma("ttt_x")
        x_rows = io["L0_attn_hidden_states"].rearrange("b (t p) d -> p (b t) d", p=P)

        def project(c):
            S.wait(n.prev("x"))
            t_x = d_x.mark(nc.sync.dma_start(xs[:, :, :], x_rows[:, bass.ds(c * TPC, TPC), :]))
            PE.wait(t_x, n.prev("xT"))
            for t in range(TPC):
                k = PE.done(nc.tensor.transpose(ps[:, 0, t * P:(t + 1) * P], xs[:, t, :], n.ident[:, :]))
            n.note("x", k)
            A.wait(k, n.prev("xT_sb"))
            k = A.done(nc.scalar.activation(xT[:, :], ps[:, 0, 0:256], ACT.Copy))
            n.note("xT", k)
            PE.wait(k, n.prev("qk"), n.prev("v"), n.prev("lr"), t_wT)
            for t in range(TPC):
                lhs = xT[:, t * P:(t + 1) * P]
                nc.tensor.matmul(ps[:, 1, t * 256:(t + 1) * 256], lhs, wT[:, 0:256], start=True, stop=True)
                nc.tensor.matmul(ps[:, 2, t * P:(t + 1) * P], lhs, wT[:, 256:384], start=True, stop=True)
                k = PE.done(nc.tensor.matmul(ps[:, 3, t * 12:(t + 1) * 12], lhs, lwT[:, :], start=True, stop=True))
            n.note("xT_sb", k)
            qk = ps[:, 1, :]
            A.wait(k, n.prev("sq2"))
            t_sq = A.done(nc.scalar.activation(sq[:, :, :].rearrange("p a b -> p (a b)"), qk, ACT.Square))
            V.wait(t_sq, n.prev("qkv_t"), n.prev("lrs"))
            t_qw = V.done(nc.vector.tensor_tensor(qw[:, :, :].rearrange("p a (m d) -> p a m d", m=2),
                                                  qk.rearrange("p (a m d) -> p a m d", a=TPC, m=2),
                                                  bcast(nw[:, :, :].unsqueeze(1), [P, TPC, 2, P]), ALU.mult))
            n.note("qk", t_qw)
            t_ss = V.done(nc.vector.tensor_reduce(ss[:, :], sq[:, :, :].rearrange("p a (m d) -> p (a m) d", m=2),
                                                  AX.X, ALU.add))
            A.wait(t_qw, t_ss)
            t_sq2 = A.done(nc.scalar.activation(sq[:, :, :], qw[:, :, :], ACT.Square))
            V.wait(t_sq2)
            t_s2 = V.done(nc.vector.tensor_reduce(s2[:, :], sq[:, :, :].rearrange("p a (h d) -> p (a h) d", d=DH),
                                                  AX.X, ALU.add))
            n.note("sq2", t_s2)
            A.wait(t_s2)
            A.done(nc.scalar.activation(ss[:, :], ss[:, :], ACT.Sqrt, bias=n.eps[:, 0:1], scale=1.0 / P))
            t_n2 = A.done(nc.scalar.activation(s2[:, :], s2[:, :], ACT.Sqrt))
            V.wait(t_n2)
            t = V.done(nc.vector.reciprocal(ss[:, :], ss[:, :]))
            V.wait(t)
            rb = bcast(ss[:, :].unsqueeze(2), [P, 4, 4])
            s2v = s2[:, :].rearrange("p (g h) -> p g h", h=4)
            t = V.done(nc.vector.tensor_tensor(s2v, s2v, rb, ALU.mult))
            V.wait(t)
            t = V.done(nc.vector.tensor_scalar(s2[:, :], s2[:, :], 1e-5, None, ALU.add))
            V.wait(t)
            t = V.done(nc.vector.reciprocal(s2[:, :], s2[:, :]))
            V.wait(t)
            t = V.done(nc.vector.tensor_tensor(s2v, s2v, rb, ALU.mult))
            V.wait(t)
            qwh = qw[:, :, :].rearrange("p a (h d) -> p (a h) d", d=DH)
            t_qk = V.done(nc.vector.tensor_tensor(qwh, qwh, bcast(s2[:, :].unsqueeze(2), [P, 16, DH]), ALU.mult))
            t_z = V.done(nc.vector.tensor_tensor(z[:, :].rearrange("p (a b) -> p a b", a=TPC),
                                                 ps[:, 3, 0:24].rearrange("p (a b) -> p a b", a=TPC),
                                                 bcast(lb[:, :].unsqueeze(1), [P, TPC, 12]), ALU.add))
            n.note("lr", t_z)
            V.wait(t_z)
            t = V.done(nc.vector.scalar_tensor_tensor(s_[:, :], z[:, :], -1.0, z[:, :], ALU.mult, ALU.min))
            A.wait(t)
            t = A.done(nc.scalar.activation(s_[:, :], s_[:, :], ACT.Sigmoid))
            V.wait(t)
            t = V.done(nc.vector.tensor_scalar(w_[:, :], s_[:, :], -1.0, 2.0, ALU.mult, ALU.add))
            V.wait(t)
            t = V.done(nc.vector.reciprocal(w_[:, :], w_[:, :]))
            V.wait(t)
            t = V.done(nc.vector.tensor_tensor(w_[:, :], w_[:, :], s_[:, :], ALU.mult))
            V.wait(t)
            t = V.done(nc.vector.tensor_tensor(w2_[:, :], w_[:, :], w_[:, :], ALU.mult))
            V.wait(t)
            t = V.done(nc.vector.tensor_scalar(ac[:, :], w2_[:, :], 1.0 / 17, None, ALU.mult))
            for k in (15, 13, 11, 9, 7, 5, 3):
                V.wait(t)
                t = V.done(nc.vector.scalar_tensor_tensor(ac[:, :], ac[:, :], 1.0 / k, w2_[:, :], ALU.add, ALU.mult))
            V.wait(t)
            t = V.done(nc.vector.scalar_tensor_tensor(ac[:, :], ac[:, :], 1.0, w_[:, :], ALU.add, ALU.mult))
            V.wait(t)
            t = V.done(nc.vector.tensor_scalar(ac[:, :], ac[:, :], 2.0, None, ALU.mult))
            V.wait(t, n.prev("lrs"))
            lrc = ac[:, :]
            t_lr = V.done(nc.vector.scalar_tensor_tensor(w_[:, :], z[:, :], 0.0, lrc, ALU.max, ALU.add))
            A.wait(n.prev("qkv_t"), n.prev("lrs"))
            t_v = A.done(nc.scalar.activation(vv[:, :, :].rearrange("p a b -> p (a b)"), ps[:, 2, 0:256], ACT.Copy))
            n.note("v", t_v)
            l4 = w_[:, :].rearrange("p (a h j) -> p a h j", a=TPC, j=3)
            G.wait(t_lr, t_qk, t_v)
            for j, src, dst in ((0, qw[:, :, P:256], kl0), (2, qw[:, :, P:256], kl2), (1, vv[:, :, :], vl1)):
                t_g = G.done(nc.gpsimd.tensor_tensor(
                    dst[:, bass.ds(c * TPC, TPC), :].rearrange("p a (h d) -> p a h d", d=DH),
                    src.rearrange("p a (h d) -> p a h d", d=DH),
                    bcast(l4[:, :, :, j:j + 1], [P, TPC, HEADS, DH]), ALU.mult))
            n.note("lrs", t_g)
            PE.wait(t_qk, t_v, n.prev("tr"))
            for m in range(3):
                for t in range(TPC):
                    src = vv[:, t, :] if m == 2 else qw[:, t, m * P:(m + 1) * P]
                    at = (m * TPC + t) * P
                    k = PE.done(nc.tensor.transpose(ps[:, 4 + at // 512, at % 512:at % 512 + P], src, n.ident[:, :]))
            n.note("qkv_t", k)
            A.wait(k)
            A.done(nc.scalar.activation(qT[:, bass.ds(c * CHUNK, CHUNK)], ps[:, 4, 0:256], ACT.Copy))
            A.done(nc.scalar.activation(kT[:, bass.ds(c * CHUNK, CHUNK)], ps[:, 4, 256:512], ACT.Copy))
            n.note("tr", A.done(nc.scalar.activation(vT[:, bass.ds(c * CHUNK, CHUNK)], ps[:, 5, 0:256], ACT.Copy)))

        V.wait(t_lb)
        n.book.run("project", NC, project)

        kTs, vTs = sb("kTs", [P, CHUNK]), sb("vTs", [P, CHUNK])
        k0s, k2s, v1s = (sb(f"{a}s", [P, TPC, P]) for a in ("k0", "k2", "v1"))
        sig, hb, sg, hd, dg, dh, v1, u = (sb(a, [P, 512]) for a in ("sig", "hb", "sg", "hd", "dg", "dh", "v1", "u"))
        sigq, tq, hq = (sb(a, [P, 512]) for a in ("sigq", "tq", "hq"))
        X = sb("X", [P, 3, HID])
        XT = sb("XT", [P, 3, P])
        Ab, T1, Gm = (sb(a, [P, 3, P]) for a in ("Ab", "T1", "Gm"))
        fn = sb("fn", [P, 3])
        d_s = n.book.dma("ttt_stage")
        t_xt0 = V.done(nc.vector.memset(XT[:, :, :], 0.0))

        def stage(c):
            for dst, src in ((kTs[:, :], kT[:, bass.ds(c * CHUNK, CHUNK)]), (vTs[:, :], vT[:, bass.ds(c * CHUNK, CHUNK)]),
                             (k0s[:, :, :], kl0[:, bass.ds(c * TPC, TPC), :]), (k2s[:, :, :], kl2[:, bass.ds(c * TPC, TPC), :]),
                             (v1s[:, :, :], vl1[:, bass.ds(c * TPC, TPC), :])):
                t = d_s.mark(nc.sync.dma_start(dst, src))
            return t

        def forward(c, b, t_free0, t_free1, t_free2):
            PE.wait(t_free0, t_free1, b["WB"])
            for m in range(2):
                for g in range(2):
                    t = PE.done(nc.tensor.matmul(ps[:, m, g * 256:(g + 1) * 256],
                                                 WB[:, m, 2 * g:2 * g + 2, :].rearrange("p a b -> p (a b)"),
                                                 qT[:, bass.ds(c * CHUNK, CHUNK)], start=True, stop=True))
            A.wait(t, b["sigq"])
            t_sq = A.done(nc.scalar.activation(sigq[:, :], ps[:, 0, :], ACT.Sigmoid))
            V.wait(t_sq, b["tq"])
            t_t = V.done(nc.vector.tensor_tensor(tq[:, :], ps[:, 0, :], sigq[:, :], ALU.mult))
            V.wait(t_t, b["hq"])
            t_h = V.done(nc.vector.tensor_tensor(hq[:, :], ps[:, 1, :], tq[:, :], ALU.mult))
            PE.wait(t_h, t_free2, b["W1T"])
            for t in range(TPC):
                for g in range(2):
                    k = PE.done(nc.tensor.matmul(ps[:, 2, t * P:(t + 1) * P], hq[:, g * 256 + t * P:g * 256 + (t + 1) * P],
                                                 W1T[:, g, :], start=(g == 0), stop=(g == 1)))
            V.wait(k)
            yc = y_all[:, bass.ds(c * TPC, TPC), :]
            t_y = V.done(nc.vector.tensor_tensor(yc, ps[:, 2, 0:256].rearrange("p (a b) -> p a b", a=TPC),
                                                 x_all[:, bass.ds(c * TPC, TPC), :], ALU.add))
            V.wait(t_y)
            for t in range(TPC):
                t_st = V.done(nc.vector.bn_stats(stats[:, bass.ds(c * TPC + t, 1), :].rearrange("p a s -> p (a s)"),
                                                 y_all[:, bass.ds(c * TPC + t, 1), :].rearrange("p a d -> p (a d)")))
            return t_h, k, t_st

        def update(c):
            PE.wait(n.prev("stage"), n.prev("hq"), n.prev("y"), n.prev("WB"))
            for m, lhs in ((0, kTs), (1, kTs), (2, vTs)):
                for t in range(TPC):
                    k = nc.tensor.matmul(ps[:, m, t * 256:(t + 1) * 256], lhs[:, t * P:(t + 1) * P],
                                         WB[:, m].rearrange("p h i -> p (h i)"), start=True, stop=True)
                tk = PE.done(k)
                if m == 0:
                    A.wait(tk)
                    t_sig = A.done(nc.scalar.activation(sig[:, :], ps[:, 0, :], ACT.Sigmoid))
                if m == 1:
                    A.wait(tk)
                    t_hb = A.done(nc.scalar.activation(hb[:, :], ps[:, 1, :], ACT.Copy))
            V.wait(t_sig)
            t_sg = V.done(nc.vector.tensor_tensor(sg[:, :], ps[:, 0, :], sig[:, :], ALU.mult))
            G.wait(t_sg, t_hb)
            t_hid = G.done(nc.gpsimd.tensor_tensor(hd[:, :], sg[:, :], hb[:, :], ALU.mult))
            V.wait(t_sg)
            t_v1 = V.done(nc.vector.scalar_tensor_tensor(v1[:, :], sg[:, :], -1.0, sig[:, :], ALU.add, ALU.mult))
            V.wait(tk, t_hb)
            t_dh = V.done(nc.vector.tensor_tensor(dh[:, :], ps[:, 2, :], sg[:, :], ALU.mult))
            t_dg = V.done(nc.vector.tensor_tensor(dg[:, :], ps[:, 2, :], hb[:, :], ALU.mult))
            V.wait(t_v1)
            t_u = V.done(nc.vector.tensor_tensor(u[:, :], sg[:, :], v1[:, :], ALU.subtract))
            V.wait(t_u)
            t_dga = V.done(nc.vector.tensor_tensor(dg[:, :], dg[:, :], u[:, :], ALU.mult))
            fb = {"WB": None, "W1T": n.prev("W1T"), "sigq": n.prev("hq"), "tq": n.prev("hq"), "hq": n.prev("y")}
            t_h, t_o, t_st = forward(c, fb, t_sg, t_hb, t_dg)
            PE.wait(n.prev("X5"))
            for m, lhs, rhs, tr in ((1, k2s, dh, t_dh), (2, v1s, hd, t_hid), (0, k0s, dg, t_dga)):
                PE.wait(tr)
                for h in range(HEADS):
                    for t in range(TPC):
                        k = nc.tensor.matmul(ps[h * DH:(h + 1) * DH, 3, m * HID:(m + 1) * HID],
                                             lhs[:, t, h * DH:(h + 1) * DH], rhs[:, t * 256 + h * HID:t * 256 + (h + 1) * HID],
                                             start=(t == 0), stop=(t == 1), tile_position=(0, h * DH))
            t_gr = PE.done(k)
            grads = ps[:, 3, 0:192].rearrange("p (m i) -> p m i", m=3)
            S.wait(t_gr)
            n.note("stage", stage(c + 1))
            A.wait(t_gr)
            t = A.done(nc.scalar.activation(sqw[:, :, :], grads, ACT.Square))
            V.wait(t)
            t = V.done(nc.vector.tensor_reduce(fn[:, :], sqw[:, :, :], AX.X, ALU.add))
            PE.wait(t)
            t = PE.done(nc.tensor.matmul(ps[:, 3, 256:259], n.blocks[:, :], fn[:, :], start=True, stop=True))
            A.wait(t)
            t = A.done(nc.scalar.activation(fn[:, :], ps[:, 3, 256:259], ACT.Sqrt))
            V.wait(t)
            t = V.done(nc.vector.tensor_scalar(fn[:, :], fn[:, :], 1e-7, None, ALU.add))
            V.wait(t)
            t = V.done(nc.vector.reciprocal(fn[:, :], fn[:, :]))
            V.wait(t)
            t_X = V.done(nc.vector.tensor_tensor(X[:, :, :], grads, bcast(fn[:, :].unsqueeze(2), [P, 3, HID]), ALU.mult))
            n.t_b3 = t_X
            PE.wait(t_X)
            tX, tXT = [t_X] * 3, [None] * 3
            k01 = PE.done(nc.tensor.transpose(ps[:, 4, 0:P], X[:, 0:2, :].rearrange("p a b -> p (a b)"), n.ident[:, :]))
            k2 = PE.done(nc.tensor.transpose(ps[0:HID, 6, 0:P], X[:, 2, :], n.ident[:, :]))
            A.wait(k01)
            for m, rows in ((0, ps[0:HID, 4, 0:P]), (1, ps[HID:P, 4, 0:P]), (2, ps[0:HID, 6, 0:P])):
                if m == 2:
                    A.wait(k2)
                tXT[m] = A.done(nc.scalar.activation(XT[0:HID, m, :], rows, ACT.Copy))
            tXT[0] = tXT[1]
            for it, (_, cb, cc) in enumerate(NS):
                last = it == len(NS) - 1
                tA, tAb, tT, tAA, tG = ([None] * 3 for _ in range(5))
                for m in range(3):
                    PE.wait(tXT[m])
                    tA[m] = PE.done(nc.tensor.matmul(ps[:, 4 + m, 0:P], XT[:, m, :], XT[:, m, :], start=True, stop=True))
                for m in range(3):
                    V.wait(tA[m])
                    tAb[m] = V.done(nc.vector.tensor_tensor(Ab[:, m, :], ps[:, 4 + m, 0:P], n.blocks[:, :], ALU.mult))
                for m in range(3):
                    PE.wait(tAb[m])
                    tAA[m] = PE.done(nc.tensor.matmul(ps[:, 4 + m, P:2 * P], Ab[:, m, :], Ab[:, m, :], start=True, stop=True))
                    V.wait(tAb[m])
                    tT[m] = V.done(nc.vector.scalar_tensor_tensor(T1[:, m, :], Ab[:, m, :], cb, aI[:, it, :], ALU.mult, ALU.add))
                for m in range(3):
                    V.wait(tAA[m], tT[m])
                    tG[m] = V.done(nc.vector.scalar_tensor_tensor(Gm[:, m, :], ps[:, 4 + m, P:2 * P], cc, T1[:, m, :], ALU.mult, ALU.add))
                for m in range(3):
                    PE.wait(tG[m], tX[m])
                    k = nc.tensor.matmul(ps[:, 4 + m, 256:256 + HID], Gm[:, m, :], X[:, m, :], start=True, stop=True)
                    if not last:
                        k = nc.tensor.matmul(ps[0:HID, 4 + m, 384:512], X[:, m, :], Gm[:, m, :], start=True, stop=True)
                    k = PE.done(k)
                    if not last:
                        A.wait(k)
                        tX[m] = A.done(nc.scalar.activation(X[:, m, :], ps[:, 4 + m, 256:256 + HID], ACT.Copy))
                        tXT[m] = A.done(nc.scalar.activation(XT[0:HID, m, :], ps[0:HID, 4 + m, 384:512], ACT.Copy))
            V.wait(k)
            t_Wn = V.done(nc.vector.tensor_tensor(Wn[:, :, :], ps[:, 4:7, 256:256 + HID], Wc[:, :, :], ALU.add))
            n.note("X5", t_Wn)
            t_r, _ = row_norms(Wn, t_Wn, NR, None)
            V.wait(t_r, t_N0)
            t = V.done(nc.vector.tensor_scalar(NR[:, :], NR[:, :], 1e-5, None, ALU.add))
            V.wait(t)
            t = V.done(nc.vector.reciprocal(NR[:, :], NR[:, :]))
            V.wait(t)
            t = V.done(nc.vector.tensor_tensor(NR[:, :], NR[:, :], N0[:, :], ALU.mult))
            V.wait(t)
            V.done(nc.vector.tensor_tensor(Wc[:, 0:2, :], Wn[:, 0:2, :], NR[:, 0:128].rearrange("p (a b) -> p a b", a=2), ALU.mult))
            t = V.done(nc.vector.tensor_scalar(Wc[:, 2, :], Wn[:, 2, :], NR[:, 128:129], None, ALU.mult))
            t_wb, t_w1t = blocks_of(t, t_o)
            for key, tick in (("WB", t_wb), ("W1T", t_w1t), ("hq", t_h), ("y", t_st)):
                n.note(key, tick)

        n.settle()
        t_s0 = stage(0)
        PE.wait(t_s0)
        n.book.run("scan", NC - 1, update)
        last = n.book.events["scan"]
        return forward(NC - 1, {"WB": last["WB"], "W1T": last["W1T"], "sigq": last["hq"], "tq": last["hq"], "hq": last["y"]},
                       last["y"], last["stage"], last["hq"])[2]



def row_stats(n, y_all, stats, t, eng_wait=True):
    n.V.wait(t)
    for i in range(y_all.shape[1]):
        t = n.V.done(n.nc.vector.bn_stats(stats[:, i, :], y_all[:, i, :]))
    return t


def layer_norm(n, y_all, stats, t_stats, out):
    nc, V, A = n.nc, n.V, n.A
    NT = y_all.shape[1]
    mv, sd = n.mv, n.sd
    V.wait(t_stats)
    for i in range(NT):
        t = V.done(nc.vector.bn_aggr(mv[:, i, :], stats[:, i, :]))
    A.wait(t)
    t = A.done(nc.scalar.activation(sd[:, :], mv[:, :, 1:2].rearrange("p a b -> p (a b)"), ACT.Sqrt, bias=n.eps[:, 1:2]))
    V.wait(t)
    t = V.done(nc.vector.reciprocal(sd[:, :], sd[:, :]))
    V.wait(t)
    for i in range(NT):
        t = V.done(nc.vector.tensor_scalar(out[:, i, :], y_all[:, i, :], mv[:, i, 0:1], sd[:, i:i + 1],
                                           ALU.subtract, ALU.mult))
    return t


def transpose_all(n, x_all, xT, t_x, banks=(0, 1)):
    nc, PE, A = n.nc, n.PE, n.A
    PE.wait(t_x)
    free = [None] * len(banks)
    for g in range(x_all.shape[1] // 4):
        k = g % len(banks)
        PE.wait(free[k])
        for i in range(4):
            t = PE.done(nc.tensor.transpose(n.psum[:, banks[k], i * P:(i + 1) * P], x_all[:, 4 * g + i, :], n.ident[:, :]))
        A.wait(t)
        free[k] = A.done(nc.scalar.activation(xT[:, g * 512:(g + 1) * 512], n.psum[:, banks[k], :], ACT.Copy))
    return free[k]


def router(n, xT, rT, t_in, bank):
    nc, PE = n.nc, n.PE
    E = rT.shape[1]
    PE.wait(t_in)
    NT = xT.shape[1] // P
    for i in range(NT):
        t = PE.done(nc.tensor.matmul(n.psum[:, bank, i * E:(i + 1) * E], xT[:, i * P:(i + 1) * P], rT, start=True, stop=True))
    return t, n.psum[:, bank, 0:NT * E].rearrange("p (t e) -> p t e", e=E)


def top_one(n, sb, logits, t_logits):
    nc, V, G = n.nc, n.V, n.G
    NT, E = logits.shape[1:]
    mx = sb("mx", [P, NT])
    hot = sb("hot", [P, NT, E])
    cand = sb("cand", [P, NT, E])
    idx = sb("idx", [P, NT])
    V.wait(t_logits)
    t_mx = V.done(nc.vector.tensor_reduce(mx[:, :], logits, AX.X, ALU.max))
    V.wait(t_mx)
    t = V.done(nc.vector.tensor_tensor(cand[:, :, :], logits, bcast(mx[:, :].unsqueeze(2), [P, NT, E]), ALU.is_ge))
    V.wait(t)
    t = V.done(nc.vector.tensor_tensor(cand[:, :, :], cand[:, :, :], bcast(n.e_less[:, :].unsqueeze(1), [P, NT, E]), ALU.mult))
    V.wait(t)
    t = V.done(nc.vector.tensor_reduce(idx[:, :], cand[:, :, :], AX.X, ALU.min))
    V.wait(t)
    t = V.done(nc.vector.tensor_tensor(hot[:, :, :], bcast(n.e_less[:, :].unsqueeze(1), [P, NT, E]),
                                       bcast(idx[:, :].unsqueeze(2), [P, NT, E]), ALU.is_equal))
    return mx, hot, t_mx, t


def capacity(n, sb, logits, mx, hot, t_mx, t_hot, cap):
    nc, V, A, PE = n.nc, n.V, n.A, n.PE
    NT, E = hot.shape[1:]
    ps = n.psum
    ex = sb("ex", [P, NT, E])
    pr = sb("pr", [P, NT])
    prow = sb("prow", [P, NT * P])
    gt = sb("gt", [P, 2, NT * P], BF16)
    eq = sb("eq", [P, P], BF16)
    tri = sb("tri", [P, P], BF16)
    hotb = sb("hotb", [P, NT, E], BF16)
    rank = sb("rank", [P, NT, E])
    rk = sb("rk", [P, NT])
    V.wait(t_mx)
    t = V.done(nc.vector.tensor_tensor(ex[:, :, :], logits, bcast(mx[:, :].unsqueeze(2), [P, NT, E]), ALU.subtract))
    A.wait(t)
    t = A.done(nc.scalar.activation(ex[:, :, :], ex[:, :, :], ACT.Exp))
    V.wait(t)
    t = V.done(nc.vector.tensor_reduce(pr[:, :], ex[:, :, :], AX.X, ALU.add))
    V.wait(t)
    t_pr = V.done(nc.vector.reciprocal(pr[:, :], pr[:, :]))
    V.wait(t_hot)
    t_hb = V.done(nc.vector.tensor_copy(hotb[:, :, :], hot[:, :, :]))
    V.done(nc.vector.tensor_copy(tri[:, :], n.before[:, :]))
    PE.wait(t_pr)
    for g in range(NT // 4):
        for i in range(4):
            t = PE.done(nc.tensor.transpose(ps[:, 4 + g % 4, i * P:(i + 1) * P],
                                            bcast(pr[:, 4 * g + i:4 * g + i + 1], [P, P]), n.ident[:, :]))
        A.wait(t)
        t_row = A.done(nc.scalar.activation(prow[:, g * 512:(g + 1) * 512], ps[:, 4 + g % 4, :], ACT.Copy))
    V.wait(t_row)
    free = [None, None]
    for i in range(NT):
        s = i % 2
        V.wait(free[s])
        me = slice(i * P, (i + 1) * P)
        if i:
            t = V.done(nc.vector.tensor_scalar(gt[:, s, 0:i * P], prow[:, 0:i * P], pr[:, i:i + 1], None, ALU.is_lt))
        if i < NT - 1:
            t = V.done(nc.vector.tensor_scalar(gt[:, s, (i + 1) * P:], prow[:, (i + 1) * P:], pr[:, i:i + 1], None, ALU.is_le))
        V.wait(t)
        t = V.done(nc.vector.scalar_tensor_tensor(eq[:, :], prow[:, me], pr[:, i:i + 1], tri[:, :], ALU.is_equal, ALU.mult))
        V.wait(t)
        t = V.done(nc.vector.scalar_tensor_tensor(gt[:, s, me], prow[:, me], pr[:, i:i + 1], eq[:, :], ALU.is_lt, ALU.add))
        PE.wait(t, t_hb)
        for j in range(NT):
            k = nc.tensor.matmul(ps[:, 3, j * E:(j + 1) * E], gt[:, s, j * P:(j + 1) * P], hotb[:, i, :],
                                 start=(i == 0 and j == 0), stop=(i == NT - 1), skip_group_check=True)
        free[s] = PE.done(k)
    V.wait(free[s], t_hot)
    t = V.done(nc.vector.tensor_tensor(rank[:, :, :], ps[:, 3, 0:NT * E].rearrange("p (t e) -> p t e", e=E),
                                       hot[:, :, :], ALU.mult))
    V.wait(t)
    t = V.done(nc.vector.tensor_reduce(rk[:, :], rank[:, :, :], AX.X, ALU.add))
    V.wait(t)
    t = V.done(nc.vector.tensor_scalar(rk[:, :], rk[:, :], float(cap), None, ALU.is_lt))
    V.wait(t)
    t = V.done(nc.vector.tensor_tensor(hot[:, :, 1:E], hot[:, :, 1:E], bcast(rk[:, :].unsqueeze(2), [P, NT, E - 1]), ALU.mult))
    V.wait(t)
    t = V.done(nc.vector.tensor_reduce(rk[:, :], hot[:, :, 1:E], AX.X, ALU.add))
    V.wait(t)
    return V.done(nc.vector.tensor_scalar(hot[:, :, 0:1], rk[:, :].unsqueeze(2), -1.0, 1.0, ALU.mult, ALU.add))


def dispatch(n, sb, hot, t_hot, tiles, bank, slots, experts):
    nc, V, PE = n.nc, n.V, n.PE
    NT, E = hot.shape[1:]
    ps = n.psum
    tot = sb("tot", [P, 2, NT + 1, E])
    cnt = sb("cnt", [P, E, NT])
    nt = sb("nt", [P, 2, E + 1])
    te = sb("te", [P, tiles, E])
    tef = sb("tef", [P, tiles])
    pos = sb("pos", [P, NT, E])
    sl = sb("sl", [P, NT])
    hv = hot[:, :, :].rearrange("p t e -> p (t e)")
    PE.wait(t_hot)
    w = NT * E
    nc.tensor.matmul(ps[:, bank, 0:w], n.before[:, :], hv, start=True, stop=True)
    t = PE.done(nc.tensor.matmul(ps[:, bank, w:2 * w], n.ones[:, :], hv, start=True, stop=True))
    within = ps[:, bank, 0:w].rearrange("p (t e) -> p t e", e=E)
    V.wait(t)
    t = V.done(nc.vector.memset(tot[:, :, 0, :], 0.0))
    a = V.done(nc.vector.tensor_copy(tot[:, 0, 1:NT + 1, :], ps[:, bank, w:2 * w].rearrange("p (t e) -> p t e", e=E)))
    src, d = 0, 1
    while d < NT:
        V.wait(a)
        V.done(nc.vector.tensor_copy(tot[:, 1 - src, 1:d + 1, :], tot[:, src, 1:d + 1, :]))
        a = V.done(nc.vector.tensor_tensor(tot[:, 1 - src, d + 1:NT + 1, :], tot[:, src, d + 1:NT + 1, :],
                                           tot[:, src, 1:NT + 1 - d, :], ALU.add))
        src, d = 1 - src, 2 * d
    V.wait(a)
    a = V.done(nc.vector.tensor_tensor(cnt[:, :, :], bcast(tot[:, src, NT, :].unsqueeze(2), [P, E, NT]),
                                       bcast(n.steps[:, :].unsqueeze(1), [P, E, NT]), ALU.is_gt))
    V.wait(a)
    V.done(nc.vector.memset(nt[:, :, 0:1], 0.0))
    a = V.done(nc.vector.tensor_reduce(nt[:, 0, 1:E + 1], cnt[:, :, :], AX.X, ALU.add))
    cur, d = 0, 1
    while d < E:
        V.wait(a)
        V.done(nc.vector.tensor_copy(nt[:, 1 - cur, 1:d + 1], nt[:, cur, 1:d + 1]))
        a = V.done(nc.vector.tensor_tensor(nt[:, 1 - cur, d + 1:E + 1], nt[:, cur, d + 1:E + 1], nt[:, cur, 1:E + 1 - d], ALU.add))
        cur, d = 1 - cur, 2 * d
    V.wait(a)
    a = V.done(nc.vector.tensor_tensor(te[:, :, :], bcast(nt[:, cur, 1:E + 1].unsqueeze(1), [P, tiles, E]),
                                       bcast(n.count[:, 0:tiles].unsqueeze(2), [P, tiles, E]), ALU.is_le))
    V.wait(a)
    a = V.done(nc.vector.tensor_reduce(tef[:, :], te[:, :, :], AX.X, ALU.add))
    V.wait(a)
    t_te = V.done(nc.vector.tensor_scalar(experts[:, :], tef[0:1, :], float(E - 1), None, ALU.min))
    a = V.done(nc.vector.scalar_tensor_tensor(pos[:, :, :], bcast(nt[:, cur, 0:E].unsqueeze(1), [P, NT, E]), float(TILE),
                                              tot[:, src, 0:NT, :], ALU.mult, ALU.add))
    V.wait(a)
    a = V.done(nc.vector.tensor_tensor(pos[:, :, :], within, pos[:, :, :], ALU.add))
    V.wait(a)
    a = V.done(nc.vector.tensor_tensor(pos[:, :, :], pos[:, :, :], hot[:, :, :], ALU.mult))
    V.wait(a)
    a = V.done(nc.vector.tensor_reduce(sl[:, :], pos[:, :, :], AX.X, ALU.add))
    V.wait(a)
    return V.done(nc.vector.tensor_copy(slots[:, :], sl[:, :])), t_te


def scatter(n, rows, x_all, slots, t_in, name):
    n.G.wait(*t_in)
    d = n.book.dma(name, 0)
    for i in range(x_all.shape[1]):
        t = d.mark(n.nc.gpsimd.indirect_dma_start(rows, bass.IndirectOffsetOnAxis(slots[:, i:i + 1], 0), x_all[:, i, :], None))
    return t


def gather_add(n, rows, got, slots, t_in, name, base, y_all, stats):
    n.G.wait(*t_in)
    NT = got.shape[1]
    d = [n.book.dma(f"{name}{g}", 0) for g in range(NT // 4)]
    ticks = [d[i // 4].mark(n.nc.gpsimd.indirect_dma_start(got[:, i, :], None, rows, bass.IndirectOffsetOnAxis(slots[:, i:i + 1], 0)))
             for i in range(NT)]
    for i in range(0, NT, 4):
        n.V.wait(ticks[i + 3])
        t = n.V.done(n.nc.vector.tensor_tensor(y_all[:, i:i + 4, :], base[:, i:i + 4, :], got[:, i:i + 4, :], ALU.add))
        n.V.wait(t)
        for k in range(4):
            t = n.V.done(n.nc.vector.bn_stats(stats[:, i + k, :], y_all[:, i + k, :]))
    return t


class Tiles:

    def __init__(self, n, sb, name, x_rows, y_rows, bank_in, bank_out):
        self.n, self.c = n, Carry(n, name)
        self.x_rows, self.y_rows = (r.rearrange("(t p) d -> p t d", p=P) for r in (x_rows, y_rows))
        self.xt, self.xT, self.yT, self.yt = (sb("tile_" + a, [P, 2, TILE]) for a in ("x", "xT", "yT", "y"))
        self.bank_in, self.bank_out = bank_in, bank_out
        self.d_x = [n.book.dma(f"{name}_x{u}") for u in range(2)]
        self.d_y = [n.book.dma(f"{name}_y{u}") for u in range(2)]

    def load(self, t, u):
        n, c = self.n, self.c
        n.S.wait(c.get(f"in{u}"))
        c.put(f"x{u}", self.d_x[u].mark(n.nc.sync.dma_start(
            self.xt[:, u, :].rearrange("p (a d) -> p a d", a=TP), self.x_rows[:, bass.ds(t * TP, TP), :])))

    def turn_in(self, u):
        n, c = self.n, self.c
        n.PE.wait(c.get(f"x{u}"), c.get("in_free"), c.get("out_free"))
        for a in range(TP):
            k = n.PE.done(n.nc.tensor.transpose(n.psum[:, self.bank_in, a * P:(a + 1) * P], self.xt[:, u, a * P:(a + 1) * P], n.ident[:, :]))
        c.put(f"in{u}", k)
        n.V.wait(k, c.get(f"up{u}"))
        c.put(f"xT{u}", c.put("in_free", n.V.done(n.nc.vector.tensor_copy(self.xT[:, u, :], n.psum[:, self.bank_in, 0:TILE]))))

    def turn_out(self, t, u):
        n, c = self.n, self.c
        n.PE.wait(c.get(f"yT{u}"), c.get("in_free"), c.get("out_free"))
        for a in range(TP):
            k = n.PE.done(n.nc.tensor.transpose(n.psum[:, self.bank_out, TILE + a * P:TILE + (a + 1) * P], self.yT[:, u, a * P:(a + 1) * P],
                                                n.ident[:, :]))
        c.put(f"out{u}", k)
        n.A.wait(k, c.get(f"st{u}"))
        k = n.A.done(n.nc.scalar.activation(self.yt[:, u, :], n.psum[:, self.bank_out, TILE:2 * TILE], ACT.Copy))
        c.put("out_free", k)
        n.S.wait(k)
        c.put(f"st{u}", self.d_y[u].mark(n.nc.sync.dma_start(
            self.y_rows[:, bass.ds(t * TP, TP), :], self.yt[:, u, :].rearrange("p (a d) -> p a d", a=TP))))

    def run(self, tiles, experts, prepare_up, prepare_down, up, down):
        def step(t, s, load=True, prep=True, out=True, dn=True):
            if prep:
                e = expert(t + 1)
                self.turn_in(1 - s)
                prepare_up(e, 1 - s)
            if load:
                self.load(t + 3, 1 - s)
            up(s)
            if out:
                self.turn_out(t - 2, s)
            if dn:
                down(1 - s)
            if prep:
                prepare_down(e, 1 - s)

        def expert(t):
            return self.n.nc.vector.value_load(experts[0:1, bass.ds(t, 1)], min_val=0, max_val=self.n.experts - 1)

        for u in range(2):
            self.load(u, u)
        self.turn_in(0)
        e = expert(0)
        prepare_up(e, 0)
        prepare_down(e, 0)
        self.load(2, 0)
        step(0, 0, out=False, dn=False)
        step(1, 1, out=False)
        pairs = (tiles - 6) // 2
        self.c.loop(pairs, lambda i: [step(2 * i + 2 + u, u) for u in range(2)])
        for t in range(2 * pairs + 2, tiles + 2):
            if t < tiles:
                step(t, t % 2, t + 3 < tiles, t + 1 < tiles)
            else:
                self.turn_out(t - 2, t % 2)
                if t == tiles:
                    down(1 - t % 2)
        return [self.c.get(f"st{u}") for u in range(2)]



def relu_experts(n, x_all, y_all, stats, t_x):
    nc, io, PE, A, V, G, S, ps = n.nc, n.io, n.PE, n.A, n.V, n.G, n.S, n.psum
    E, _, F = io["L0_ffn_W1"].shape
    FC = F // P
    NT = x_all.shape[1]
    cap = -(-NT * P * 5 // (4 * E))
    tiles = n.tiles
    with ExitStack() as mem:
        sb = lambda name, shape, dt=F32: n.sb("r_" + name, shape, dt, mem)
        W1 = sb("W1", [P, E * F])
        W2 = sb("W2", [P, E * FC * P])
        b1 = sb("b1", [P, E * FC])
        b1raw = sb("b1raw", [E, F])
        b2 = sb("b2", [P, E])
        b2raw = sb("b2raw", [E, P])
        rraw = sb("rraw", [E, P])
        rT = sb("rT", [P, E])
        d_s, d_w = n.book.dma("relu_small"), n.book.dma("relu_weights")
        for dst, src in ((rraw[:, :], io["L0_ffn_router_w"]), (b1raw[:, :], io["L0_ffn_b1"]), (b2raw[:, :], io["L0_ffn_b2"])):
            t_s = d_s.mark(nc.sync.dma_start(dst, src))
        for dst, src in ((W1[:, :].rearrange("p (e f) -> p e f", e=E), io["L0_ffn_W1"].rearrange("e p f -> p e f")),
                         (W2[:, :].rearrange("p (g d) -> p g d", d=P), io["L0_ffn_W2"].rearrange("e (c p) d -> p (e c) d", p=P))):
            t_w = d_w.mark(nc.sync.dma_start(dst, src))
        PE.wait(t_s)
        nc.tensor.transpose(ps[:, 2, 0:E], rraw[:, :], n.ident[0:E, 0:E])
        for c in range(FC):
            nc.tensor.transpose(ps[:, 2, (c + 1) * E:(c + 2) * E], b1raw[:, c * P:(c + 1) * P], n.ident[0:E, 0:E])
        t = PE.done(nc.tensor.transpose(ps[:, 2, (FC + 1) * E:(FC + 2) * E], b2raw[:, :], n.ident[0:E, 0:E]))
        V.wait(t)
        t_rT = V.done(nc.vector.tensor_copy(rT[:, :], ps[:, 2, 0:E]))
        t_b1 = V.done(nc.vector.tensor_copy(b1[:, :].rearrange("p (e c) -> p c e", c=FC),
                                            ps[:, 2, E:E + FC * E].rearrange("p (c e) -> p c e", c=FC)))
        t_b2 = V.done(nc.vector.tensor_copy(b2[:, :], ps[:, 2, (FC + 1) * E:(FC + 2) * E]))
        slots, experts = sb("slots", [P, NT], U32), sb("experts", [1, tiles], I32)
        with ExitStack() as tmp:
            tb = lambda name, shape, dt=F32: n.sb("rr_" + name, shape, dt, tmp)
            xT = tb("xT", [P, NT * P])
            t_xT = transpose_all(n, x_all, xT, t_x)
            PE.wait(t_b2)
            t_lg, logits = router(n, xT, rT[:, :], t_xT, 2)
            mx, hot, t_mx, t_hot = top_one(n, tb, logits, t_lg)
            t_hot = capacity(n, tb, logits, mx, hot, t_mx, t_hot, cap)
            t_slots, t_te = dispatch(n, tb, hot, t_hot, tiles, 4, slots, experts)
            n.settle()
        t_sc = scatter(n, n.x_rows[0], x_all, slots, (t_slots, t_x, n.t_zero), "relu_scatter")

        W1s, W2s, h = (sb(a, [P, 2, w]) for a, w in (("W1s", F), ("W2s", F), ("h", FC * TILE)))
        bs = sb("bs", [P, 2, FC + 1])
        tl = Tiles(n, sb, "relu_tiles", n.x_rows[0], n.y_rows[0], 4, 6)
        get, put = tl.c.get, tl.c.put
        S.wait(t_sc)
        V.wait(t_w, t_te)

        def prepare_up(e, u):
            V.wait(get(f"up{u}"))
            put(f"W1{u}", V.done(nc.vector.tensor_copy(W1s[:, u, :], W1[:, bass.ds(e * F, F)])))
            V.wait(get(f"h{u}"))
            put(f"b1{u}", V.done(nc.vector.tensor_copy(bs[:, u, 0:FC], b1[:, bass.ds(e * FC, FC)])))

        def prepare_down(e, u):
            V.wait(get(f"dn{u}"), get(f"yT{u}"))
            put(f"b2{u}", V.done(nc.vector.tensor_copy(bs[:, u, FC:FC + 1], b2[:, bass.ds(e, 1)])))
            put(f"W2{u}", V.done(nc.vector.tensor_copy(W2s[:, u, :], W2[:, bass.ds(e * F, F)])))

        def up(u):
            PE.wait(get(f"xT{u}"), get(f"W1{u}"), get(f"h{u}"))
            hp = ps[:, 2 * u:2 * u + 2, :].rearrange("p b t -> p (b t)")
            for c in range(FC):
                k = PE.done(nc.tensor.matmul(hp[:, c * TILE:(c + 1) * TILE], W1s[:, u, c * P:(c + 1) * P], tl.xT[:, u, :], start=True, stop=True))
                if c % 2:
                    A.wait(k, get(f"b1{u}"), get(f"dn{u}"))
                    for b in (c - 1, c):
                        r = A.done(nc.scalar.activation(h[:, u, b * TILE:(b + 1) * TILE], hp[:, b * TILE:(b + 1) * TILE], ACT.Relu,
                                                        bias=bs[:, u, b:b + 1]))
            put(f"up{u}", k)
            put(f"h{u}", r)

        def down(u):
            PE.wait(get(f"h{u}"), get(f"W2{u}"), get(f"yT{1 - u}"))
            for c in range(FC):
                k = nc.tensor.matmul(ps[:, 5, 0:TILE], W2s[:, u, c * P:(c + 1) * P], h[:, u, c * TILE:(c + 1) * TILE],
                                     start=(c == 0), stop=(c == FC - 1))
            put(f"dn{u}", PE.done(k))
            A.wait(get(f"dn{u}"), get(f"b2{u}"), get(f"out{u}"))
            put(f"yT{u}", A.done(nc.scalar.activation(tl.yT[:, u, :], ps[:, 5, 0:TILE], ACT.Identity, bias=bs[:, u, FC:FC + 1])))

        t_st = tl.run(tiles, experts, prepare_up, prepare_down, up, down)
        got = sb("got", [P, NT, P])
        t = gather_add(n, n.y_rows[0], got, slots, t_st, "relu_gather", x_all, y_all, stats)
        n.settle()
        return t



def softmax_attention(n, x_all, y_all, stats, t_x):
    nc, io, PE, A, V, G, S, ps = n.nc, n.io, n.PE, n.A, n.V, n.G, n.S, n.psum
    NT = x_all.shape[1]
    T = NT * P
    D = 64
    QT = 512
    NU = T // QT
    pairs = io["L1_attn_Wq"].shape[1] // (2 * D)
    scale = 1.0 / float(np.sqrt(D))
    POOL = 704
    SLOT = ((0, 1), (2, 3))
    B_O, B_P, B_M = 4, 5, 6
    with ExitStack() as mem:
        sb = lambda name, shape, dt=F32: n.sb("a_" + name, shape, dt, mem)
        xT = sb("xT", [P, T])
        Wq, Wk = (sb(a, [P, 2, 2, 2, D]) for a in ("Wq", "Wk"))
        Wv, Wo = (sb(a, [P, 2, P]) for a in ("Wv", "Wo"))
        K1, K2 = (sb(a, [P, 2, 2, T], F32R) for a in ("K1", "K2"))
        M1, M2 = (sb(a, [P, 2, 2, QT], F32R) for a in ("M1", "M2"))
        Vb = sb("Vb", [P, 2, NT, P])
        Pb = sb("Pb", [P, 4, 2 * QT])
        acc = sb("acc", [P, 2, 2 * QT])
        Or = sb("Or", [P, 2, QT])
        On = sb("On", [P, QT])
        mx = sb("mx", [P, 2, 4, NU])
        nm = sb("nm", [P, 2, 4])
        rec = sb("rec", [P, QT])
        full = sb("full", [P, QT])
        bo = sb("bo", [P, 1])
        d_q = [n.book.dma(f"att_w{u}") for u in range(2)]
        d_o = [n.book.dma(f"att_wo{u}") for u in range(2)]
        d_b = n.book.dma("att_bo")
        state = {}

        def get(key):
            if key in state:
                return state[key]
            if n.book.loop is not None:
                return n.prev(key)
            return n.book.events.get("heads", {}).get(key)

        def put(key, tick):
            state[key] = tick
            if n.book.loop is not None:
                n.note(key, tick)
            return tick

        def load_qkv(pair, par):
            cols = slice(pair * P, (pair + 1) * P) if isinstance(pair, int) else bass.ds(pair * P, P)
            S.wait(get(f"Wq{par}"), get(f"Wk{par}"), get(f"Wv{par}"))
            for dst, name in ((Wq, "L1_attn_Wq"), (Wk, "L1_attn_Wk")):
                for twice in range(2):
                    d_q[par].mark(nc.sync.dma_start(dst[:, par, :, twice, :],
                                                    io[name][:, cols].rearrange("p (h d) -> p h d", h=2)))
            put(f"dq{par}", d_q[par].mark(nc.sync.dma_start(Wv[:, par, :], io["L1_attn_Wv"][:, cols])))

        def load_o(pair, par):
            rows = slice(pair * P, (pair + 1) * P) if isinstance(pair, int) else bass.ds(pair * P, P)
            S.wait(get(f"Wo{par}"))
            put(f"do{par}", d_o[par].mark(nc.sync.dma_start(Wo[:, par, :], io["L1_attn_Wo"][rows, :])))

        def keys_job(par, qt, h, bank):
            at = slice(qt * QT, (qt + 1) * QT)
            PE.wait(get(f"dq{par}"), get(f"B{bank}"))
            k = PE.done(nc.tensor.matmul(ps[:, bank, :], Wk[:, par, h].rearrange("p a d -> p (a d)"), xT[:, at], start=True, stop=True))
            put(f"Wk{par}", k)
            A.wait(k, get(f"K{par}"))
            A.done(nc.scalar.activation(K1[:, par, h, at], ps[:, bank, :], ACT.Copy))
            A.wait(get("full_read"))
            k = A.done(nc.scalar.activation(full[0:D, :], ps[0:D, bank, :], ACT.Copy))
            put(f"B{bank}", k)
            G.wait(k, get(f"K{par}"), get("pool_last"))
            k = G.done(nc.gpsimd.tensor_tensor(K2[0:D, par, h, at], full[0:D, :], K1[0:D, par, h, at].bitcast(F32), ALU.subtract))
            put("full_read", put("pool_last", k))
            put(f"Kready{par}{h}", k)

        def values_job(par, qt, bank):
            PE.wait(get(f"dq{par}"), get(f"B{bank}"))
            for i in range(4):
                k = nc.tensor.matmul(ps[:, bank, i * P:(i + 1) * P], xT[:, (4 * qt + i) * P:(4 * qt + i + 1) * P], Wv[:, par, :], start=True, stop=True)
            k = PE.done(k)
            put(f"Wv{par}", k)
            A.wait(k, get(f"K{par}"))
            k = A.done(nc.scalar.activation(Vb[:, par, 4 * qt:4 * qt + 4, :].rearrange("p a d -> p (a d)"), ps[:, bank, :], ACT.Copy))
            put(f"B{bank}", k)
            put(f"Vready{par}", k)

        def queries_job(par, u, qt, h, bank):
            PE.wait(get(f"dq{par}"), get(f"B{bank}"))
            k = PE.done(nc.tensor.matmul(ps[:, bank, :], Wq[:, par, h].rearrange("p a d -> p (a d)"), xT[:, qt * QT:(qt + 1) * QT], start=True, stop=True))
            put(f"Wq{par}", k)
            A.wait(k, get(f"M{u}"))
            k1 = A.done(nc.scalar.activation(M1[:, u, h, :], ps[:, bank, :], ACT.Copy))
            k = A.done(nc.scalar.activation(M2[0:D, u, h, :], ps[0:D, bank, :], ACT.Copy))
            A.wait(get("full_read"))
            k = A.done(nc.scalar.activation(full[D:P, :], ps[D:P, bank, :], ACT.Copy))
            put(f"B{bank}", k)
            G.wait(k, get("pool_last"))
            k = G.done(nc.gpsimd.tensor_tensor(M1[D:P, u, h, :], full[D:P, :], M1[D:P, u, h, :].bitcast(F32), ALU.subtract))
            put("full_read", put("pool_last", k))
            put(f"Q{u}{h}", k)

        def max_job(par, u, k, bank):
            h, qc, quarter = k // 16, (k % 16) // 4, k % 4
            PE.wait(get(f"Q{u}{h}"), get(f"Kready{par}{h}"), get(f"B{bank}"))
            t = PE.done(nc.tensor.matmul(ps[:, bank, :], M1[:, u, h, qc * P:(qc + 1) * P],
                                         K1[:, par, h, quarter * QT:(quarter + 1) * QT], start=True, stop=True))
            V.wait(t, get(f"mx_read{h}"))
            put(f"mx{h}", V.done(nc.vector.tensor_reduce(mx[:, h, qc, quarter:quarter + 1], ps[:, bank, :], AX.X, ALU.max)))
            put(f"B{bank}", get(f"mx{h}"))

        def max_row_job(u, h, bank):
            negate_job(h)
            row_job(u, h, bank)

        def negate_job(h):
            V.wait(get(f"mx{h}"), get(f"nm{h}"))
            k = V.done(nc.vector.tensor_reduce(nm[:, h, :], mx[:, h, :, :], AX.X, ALU.max, negate=True))
            put(f"mx_read{h}", k)

        def row_job(u, h, bank):
            PE.wait(get(f"mx_read{h}"), get(f"B{bank}"))
            for qc in range(4):
                k = nc.tensor.matmul(ps[D:D + 1, bank, qc * P:(qc + 1) * P], nm[:, h, qc:qc + 1], n.ident[:, :], start=True, stop=True)
            k = PE.done(k)
            put(f"nm{h}", k)
            A.wait(k)
            k = A.done(nc.scalar.activation(M2[D:D + 1, u, h, :], ps[D:D + 1, bank, :], ACT.Copy))
            put(f"B{bank}", k)
            put(f"M2ready{u}{h}", k)

        def scores(step, par, u, kc):
            b = SLOT[step % 2]
            PE.wait(get(f"slot{step % 2}"), get(f"M2ready{u}0"), get(f"M2ready{u}1"), get(f"Kready{par}1"))
            for h in range(2):
                at = slice(kc * P, (kc + 1) * P)
                nc.tensor.matmul(ps[:, b[h], :], K1[:, par, h, at], M1[:, u, h, :], start=True, stop=False)
                k = nc.tensor.matmul(ps[:, b[h], :], K2[0:D + 1, par, h, at], M2[0:D + 1, u, h, :], start=False, stop=True)
            k = PE.done(k)
            put(f"M{u}", k)
            put(f"Klast{par}", k)
            buf = step % 4
            A.wait(k, get(f"pv{buf}"), get(f"addv{buf}"), get(f"addg{buf}"))
            k = A.done(nc.scalar.activation(Pb[:, buf, :], ps[:, b[0]:b[0] + 2, :].rearrange("p a b -> p (a b)"), ACT.Exp, scale=scale))
            put(f"slot{step % 2}", k)
            put(f"exp{buf}", k)

        def weigh(step, par, u, kc):
            buf = step % 4
            PE.wait(get(f"exp{buf}"), get(f"Vready{par}"))
            if kc == 0:
                PE.wait(get("B_O"))
            for h in range(2):
                k = nc.tensor.matmul(ps[h * D:(h + 1) * D, B_O, :], Vb[:, par, kc, h * D:(h + 1) * D], Pb[:, buf, h * QT:(h + 1) * QT],
                                     start=(kc == 0), stop=(kc == NT - 1))
            k = PE.done(k)
            put(f"pv{buf}", k)
            if kc == NT - 1:
                A.wait(k, get(f"Or{u}"))
                k = A.done(nc.scalar.activation(Or[:, u, :], ps[:, B_O, :], ACT.Copy))
                put("B_O", k)
                put(f"Oraw{u}", k)
            if kc == 0:
                return
            for q, at, key, op in ((V, slice(POOL, 2 * QT), "addv", nc.vector.tensor_tensor),
                                   (G, slice(0, POOL), "addg", nc.gpsimd.tensor_tensor)):
                q.wait(get(f"exp{buf}"), get(f"{key}"), get(f"sums{u}") if kc == 1 else None)
                first = Pb[:, (step - 1) % 4, at] if kc == 1 else acc[:, u, at]
                if q is G:
                    q.wait(get("pool_last"))
                k = q.done(op(acc[:, u, at], first, Pb[:, buf, at], ALU.add))
                if q is G:
                    put("pool_last", k)
                put(key, k)
                put(f"{key}{buf}", k)
                if kc == 1:
                    put(f"{key}{(step - 1) % 4}", k)

        def sums_job(u, bank):
            PE.wait(get("addv"), get("addg"), get(f"B{bank}"))
            for h in range(2):
                k = nc.tensor.matmul(ps[h * D:(h + 1) * D, bank, :], n.ones[:, 0:D], acc[:, u, h * QT:(h + 1) * QT], start=True, stop=True)
            put(f"sums{u}", PE.done(k))

        def reciprocal_job(u, part, bank):
            at = slice(part * P, (part + 1) * P)
            V.wait(get(f"sums{u}"), get("On"))
            put("rec", V.done(nc.vector.reciprocal(rec[:, at], ps[:, bank, at])))
            put(f"B{bank}", get("rec"))

        def normalise_job(u):
            V.wait(get("rec"), get(f"Oraw{u}"), get("On_free"))
            k = V.done(nc.vector.tensor_tensor(On[:, :], rec[:, :], Or[:, u, :], ALU.mult))
            put(f"Or{u}", k)
            put("On", k)

        def output_job(par, qt, bank):
            PE.wait(get("On"), get(f"B{bank}"), get(f"do{par}"))
            k = PE.done(nc.tensor.matmul(ps[:, bank, :], Wo[:, par, :], On[:, :], start=True, stop=True))
            put("On_free", k)
            put(f"Wo{par}", k)
            yq = y_all[:, 4 * qt:4 * qt + 4, :]
            V.wait(k, get(f"y{qt}"))
            k = V.done(nc.vector.tensor_tensor(yq, ps[:, bank, :].rearrange("p (a d) -> p a d", a=4), yq, ALU.add))
            put(f"B{bank}", k)
            put(f"y{qt}", k)

        t_b = d_b.mark(nc.sync.dma_start(bo[:, :], io["L1_attn_bo"].rearrange("(d a) -> d a", a=1)))
        load_qkv(0, 0)
        load_qkv(1, 1)
        load_o(0, 0)
        t_one = G.done(nc.gpsimd.memset(K2[D:D + 1, :, :, :].bitcast(F32), 1.0))
        A.wait(t_b, t_x)
        t_y = A.done(nc.scalar.activation(y_all[:, :, :], bcast(bo[:, :].unsqueeze(2), [P, NT, P]), ACT.Copy))
        t_xT = transpose_all(n, x_all, xT, t_x, (0, 1, 2, 3))
        PE.wait(t_xT)
        for h in range(2):
            queries_job(0, 0, 0, h, 4 + h)
        for h in range(2):
            for qt in range(NU):
                keys_job(0, qt, h, (6, 7, 0, 1)[qt])
        for k in range(8 * NU):
            max_job(0, 0, k, (2, 3, 6, 7)[k % 4])
            if k % 8 == 7:
                values_job(0, k // 8, 4 + k // 8 % 2)
            if k == 20:
                max_row_job(0, 0, 0)
        max_row_job(0, 1, 1)
        n.settle()
        ready = dict(state)
        state.clear()

        STEPS = NT
        MAX_AT = [(kc, point) for kc in range(3, 14) for point in range(3)]

        def body(i, last):
            units = 2 * NU
            for g in range(units):
                a, qt, u = g // NU, g % NU, g % 2
                more_q = not (last and g == units - 1)
                more_k = not (last and a == 1)
                ga, gq = ((g + 1) // NU) % 2, (g + 1) % NU
                pu, pqt, pa = 1 - u, (g - 1) % NU, ((g - 1) % units) // NU
                for kc in range(STEPS):
                    step = g * STEPS + kc

                    def maxima(point):
                        k = 3 * (kc - 3) + point
                        if more_q and 0 <= k < 8 * NU:
                            max_job(ga, 1 - u, k, B_M + k % 2)

                    maxima(0)
                    if more_q and kc == 14:
                        row_job(1 - u, 1, B_P)
                    if kc < STEPS - 1:
                        scores(step + 1, a, u, kc + 1)
                    elif more_q:
                        scores(step + 1, ga, 1 - u, 0)
                    if more_q and kc in (0, 2):
                        queries_job(ga, 1 - u, gq, kc // 2, B_P)
                    if kc == 1:
                        sums_job(pu, B_M + 1)
                    if kc in (1, 2):
                        for part in (2 * kc - 2, 2 * kc - 1):
                            reciprocal_job(pu, part, B_M + 1)
                    if more_k and kc in (3, 7):
                        keys_job(1 - a, qt, kc // 4, B_P)
                    if kc == 4:
                        normalise_job(pu)
                    if kc == 5:
                        output_job(pa, pqt, B_P)
                    if more_k and kc == 9:
                        values_job(1 - a, qt, B_P)
                    maxima(1)
                    if more_q and kc == 9:
                        negate_job(0)
                    if more_q and kc == 13:
                        negate_job(1)
                    if more_q and kc == 11:
                        row_job(1 - u, 0, B_P)
                    weigh(step, a, u, kc)
                    maxima(2)
                if qt == NU - 1:
                    put(f"K{a}", get(f"Klast{a}"))
                    if not last:
                        load_qkv(2 * i + a + 2, a)
                if qt == 0:
                    if not (last and a == 1):
                        load_o(2 * i + a + 1, 1 - a)

        V.done(nc.vector.memset(acc[:, 1, :], 1.0))
        V.done(nc.vector.memset(Or[:, 1, :], 0.0))
        S.wait(ready["dq0"])
        k = d_o[1].mark(nc.sync.dma_start(Wo[:, 1, :], io["L1_attn_Wo"][0:P, :]))
        PE.wait(k)
        n.settle()
        scores(0, 0, 0, 0)
        n.settle()
        state.clear()
        n.book.run("heads", pairs // 2 - 1, lambda i: (state.clear(), body(i, False)))
        state.clear()
        body(pairs // 2 - 1, True)
        sums_job(1, B_M + 1)
        for part in range(4):
            reciprocal_job(1, part, B_M + 1)
        normalise_job(1)
        output_job(1, NU - 1, B_P)
        for qt in range(NU):
            PE.wait(get(f"y{qt}"))
            for i in range(4):
                k = PE.done(nc.tensor.transpose(ps[:, qt, i * P:(i + 1) * P], y_all[:, 4 * qt + i, :], n.ident[:, :]))
            at = slice(4 * qt, 4 * qt + 4)
            V.wait(k)
            t = V.done(nc.vector.tensor_tensor(y_all[:, at, :], ps[:, qt, :].rearrange("p (a d) -> p a d", a=4), x_all[:, at, :], ALU.add))
            V.wait(t)
            for i in range(4 * qt, 4 * qt + 4):
                t = V.done(nc.vector.bn_stats(stats[:, i, :], y_all[:, i, :]))
        n.settle()
        return t



def gated_experts(n, x_all, y_all, stats, t_x):
    nc, io, PE, A, V, G, S, ps = n.nc, n.io, n.PE, n.A, n.V, n.G, n.S, n.psum
    E, _, F = io["L1_ffn_w1_eDF"].shape
    FC = -(-F // P)
    FP, FL = FC * P, F - (FC - 1) * P
    NT = x_all.shape[1]
    tiles = n.tiles
    QT = 512
    with ExitStack() as mem:
        sb = lambda name, shape, dt=F32: n.sb("g_" + name, shape, dt, mem)
        w13 = sb("w13", [P, E, 2, F])
        w2 = sb("w2", [P, E * FC * P])
        w2v = w2[:, :].rearrange("p (e c d) -> p e c d", e=E, c=FC)
        ws13 = sb("ws13", [P, 2, FP])
        ws2 = sb("ws2", [P, FC, P])
        rT = sb("rT", [P, E])
        w13s = sb("w13s", [P, 2, 2, FP])
        w2s = sb("w2s", [P, 2, FP])
        lo = FL // 32 * 32
        for part in (w2v[lo:P, :, FC - 1, :], ws2[lo:P, FC - 1, :], ws13[:, :, F:FP], w13s[:, :, :, F:FP]):
            t_pad = V.done(nc.vector.memset(part, 0.0))
        d_w = [n.book.dma(f"gated_weights{i}") for i in range(3)]
        S.wait(t_pad)
        full = (FC - 1) * P
        t_w = [None] * 3
        for part, dst, src in (
            (0, rT[:, :], io["L1_ffn_router_DE"]),
            (1, ws13[:, 0, 0:F], io["L1_ffn_ws1_DF"]), (1, ws13[:, 1, 0:F], io["L1_ffn_ws3_DF"]),
            (1, ws2[:, 0:FC - 1, :], io["L1_ffn_ws2_FD"][0:full, :].rearrange("(c p) d -> p c d", p=P)),
            (1, ws2[0:FL, FC - 1, :], io["L1_ffn_ws2_FD"][full:F, :]),
            (2, w13[:, :, 0, :], io["L1_ffn_w1_eDF"].rearrange("e p f -> p e f")),
            (2, w13[:, :, 1, :], io["L1_ffn_w3_eDF"].rearrange("e p f -> p e f")),
            (2, w2v[0:FL, :, FC - 1, :], io["L1_ffn_w2_eFD"][:, full:F, :].rearrange("e p d -> p e d")),
            *((2, w2v[:, :, c, :], io["L1_ffn_w2_eFD"][:, c * P:(c + 1) * P, :].rearrange("e p d -> p e d")) for c in range(FC - 1)),
        ):
            t_w[part] = d_w[part].mark(nc.sync.dma_start(dst, src))
        slots, experts = sb("slots", [P, NT], U32), sb("experts", [1, tiles], I32)
        xT = sb("xT", [P, NT * P])
        xg = sb("xg", [P, NT, P])
        with ExitStack() as tmp:
            tb = lambda name, shape, dt=F32: n.sb("gr_" + name, shape, dt, tmp)
            gate = tb("gate", [P, NT])
            t_xT = transpose_all(n, x_all, xT, t_x)
            PE.wait(t_w[0])
            t_lg, logits = router(n, xT, rT[:, :], t_xT, 2)
            mx, hot, t_mx, t_hot = top_one(n, tb, logits, t_lg)
            A.wait(t_mx)
            t = A.done(nc.scalar.activation(gate[:, :], mx[:, :], ACT.Sigmoid))
            G.wait(t)
            t_xg = G.done(nc.gpsimd.tensor_tensor(xg[:, :, :], x_all[:, :, :], bcast(gate[:, :].unsqueeze(2), [P, NT, P]), ALU.mult))
            t_slots, t_te = dispatch(n, tb, hot, t_hot, tiles, 3, slots, experts)
            n.settle()
        t_sc = scatter(n, n.x_rows[1], xg, slots, (t_slots, t_xg, n.t_zero), "gated_scatter")

        sg = sb("sg", [P, FC, QT])
        hh = sb("hh", [P, FC, QT])

        def shared(i):
            PE.wait(n.prev("t"), n.prev("h"))
            ks = []
            for m in range(2):
                for c in range(FC):
                    k = PE.done(nc.tensor.matmul(ps[:, 3 * m + c, :], ws13[:, m, c * P:(c + 1) * P], xT[:, bass.ds(i * QT, QT)], start=True, stop=True))
                    ks.append(k)
            for c in range(FC):
                A.wait(ks[c], n.prev("h"))
                k = A.done(nc.scalar.activation(sg[:, c, :], ps[:, c, :], ACT.Sigmoid))
                V.wait(k)
                k = V.done(nc.vector.tensor_tensor(sg[:, c, :], ps[:, c, :], sg[:, c, :], ALU.mult))
                n.note("t", k)
                V.wait(k, ks[FC + c], n.prev("down"))
                k = V.done(nc.vector.tensor_tensor(hh[:, c, :], ps[:, 3 + c, :], sg[:, c, :], ALU.mult))
            n.note("h", k)
            PE.wait(k, n.prev("y"))
            for t in range(4):
                for c in range(FC):
                    k = nc.tensor.matmul(ps[:, 6, t * P:(t + 1) * P], hh[:, c, t * P:(t + 1) * P], ws2[:, c, :], start=(c == 0), stop=(c == FC - 1))
            k = PE.done(k)
            n.note("down", k)
            V.wait(k)
            at = bass.ds(i * 4, 4)
            n.note("y", V.done(nc.vector.tensor_tensor(y_all[:, at, :], ps[:, 6, :].rearrange("p (a d) -> p a d", a=4),
                                                       x_all[:, at, :], ALU.add)))

        PE.wait(t_w[1])
        n.book.run("shared", NT * P // QT, shared)

        sig = sb("sig", [P, FC * TILE])
        h = sb("h", [P, 2, FC * TILE])
        n.settle()
        tl = Tiles(n, sb, "gated_tiles", n.x_rows[1], n.y_rows[1], 6, 6)
        get, put = tl.c.get, tl.c.put
        S.wait(t_sc)
        V.wait(t_w[2], t_te)

        def prepare_up(e, u):
            V.wait(get(f"up{u}"))
            put(f"w13{u}", V.done(nc.vector.tensor_copy(w13s[:, u, :, 0:F], w13[:, bass.ds(e, 1), :, :].rearrange("p a b f -> p (a b) f"))))

        def prepare_down(e, u):
            V.wait(get(f"dn{u}"))
            put(f"w2{u}", V.done(nc.vector.tensor_copy(w2s[:, u, :], w2[:, bass.ds(e * FP, FP)])))

        def up(u):
            PE.wait(get(f"xT{u}"), get(f"w13{u}"), get("gated"))
            hp = ps[:, 0:6, :].rearrange("p b t -> p (b t)")
            at = [3 * u * 512 + b * TILE for b in range(6)]
            ks = [PE.done(nc.tensor.matmul(hp[:, at[b]:at[b] + TILE], w13s[:, u, b // FC, (b % FC) * P:(b % FC + 1) * P], tl.xT[:, u, :],
                                           start=True, stop=True)) for b in range(2 * FC)]
            put(f"up{u}", ks[-1])
            up1, up3 = hp[:, at[0]:at[0] + FC * TILE], hp[:, at[FC]:at[FC] + FC * TILE]
            A.wait(ks[-1], get("gated"))
            k = A.done(nc.scalar.activation(sig[:, :], up1, ACT.Sigmoid))
            V.wait(k)
            k = V.done(nc.vector.tensor_tensor(sig[:, :], up1, sig[:, :], ALU.mult))
            V.wait(k, get(f"dn{u}"))
            put("gated", put(f"h{u}", V.done(nc.vector.tensor_tensor(h[:, u, :], up3, sig[:, :], ALU.mult))))

        def down(u):
            PE.wait(get(f"h{u}"), get(f"w2{u}"), get(f"yT{1 - u}"))
            for c in range(FC):
                k = nc.tensor.matmul(ps[:, 7, 0:TILE], w2s[:, u, c * P:(c + 1) * P], h[:, u, c * TILE:(c + 1) * TILE],
                                     start=(c == 0), stop=(c == FC - 1))
            put(f"dn{u}", PE.done(k))
            A.wait(get(f"dn{u}"), get(f"out{u}"))
            put(f"yT{u}", A.done(nc.scalar.activation(tl.yT[:, u, :], ps[:, 7, 0:TILE], ACT.Copy)))

        t_st = tl.run(tiles, experts, prepare_up, prepare_down, up, down)
        t = gather_add(n, n.y_rows[1], xg, slots, (*t_st, t_sc), "gated_gather", y_all, y_all, stats)
        n.settle()
        return t


def program(nc, known, io, out, debug=None, start=0):
    with ExitStack() as ctx:
        n = Net(nc, ctx, known, io)
        NT = io["L0_attn_hidden_states"].shape[1] // P
        E = io["L0_ffn_W1"].shape[0]
        n.tiles = NT * P // TILE + E
        n.experts = E
        constants(n)
        x_all = n.sb("x_all", [P, NT, P])
        y_all = n.sb("y_all", [P, NT, P])
        stats = n.sb("stats", [P, NT, 6])
        n.mv = n.sb("mv", [P, NT, 2])
        n.sd = n.sb("sd", [P, NT])
        n.x_rows = [nc.dram_tensor(f"x_rows{i}", (n.tiles * TILE, P), F32, kind="Internal").ap() for i in range(2)]
        n.y_rows = [nc.dram_tensor(f"y_rows{i}", (n.tiles * TILE, P), F32, kind="Internal").ap() for i in range(2)]
        n.G.wait(n.t_const)
        zero = n.sb("zero", [P, P])
        t = n.G.done(nc.gpsimd.memset(zero[:, :], 0.0))
        d_z = n.book.dma("zero_rows")
        n.A.wait(t)
        for i in range(2):
            n.t_zero = d_z.mark(nc.scalar.dma_start(n.x_rows[i].rearrange("(t p) d -> p t d", p=P),
                                                    bcast(zero[:, :].unsqueeze(1), [P, n.tiles * TP, P])))
        d_in = n.book.dma("x_in")
        src = io["L0_attn_hidden_states"] if not start else debug["x"]
        t_in = d_in.mark(nc.sync.dma_start(x_all[:, :, :], src.rearrange("b (t p) d -> p (b t) d", p=P)))
        n.V.wait(t_in)
        d = n.book.dma("dbg")

        def dump(name, src, t):
            if debug and name in debug:
                n.S.wait(t)
                n.S.wait(d.mark(nc.sync.dma_start(debug[name].rearrange("(t p) d -> p t d", p=P), src[:, :, :])))
        if start < 1:
            t = ttt_attention(n, x_all, y_all, stats)
            dump("y1", y_all, t)
            t_in = layer_norm(n, y_all, stats, t, x_all)
            dump("x1", x_all, t_in)
        n.settle()
        if start < 2:
            t = relu_experts(n, x_all, y_all, stats, t_in)
            t_in = layer_norm(n, y_all, stats, t, x_all)
            dump("x2", x_all, t_in)
        if start < 3:
            t = softmax_attention(n, x_all, y_all, stats, t_in)
            t_in = layer_norm(n, y_all, stats, t, x_all)
            dump("x3", x_all, t_in)
        t = gated_experts(n, x_all, y_all, stats, t_in)
        t_in = layer_norm(n, y_all, stats, t, x_all)
        n.S.wait(t_in, n.t_zero)
        n.S.wait(d.mark(nc.sync.dma_start(out.rearrange("b (t p) d -> p (b t) d", p=P), x_all[:, :, :])))
        return n.book.found


_INS = ['L0_attn_hidden_states', 'L0_attn_qkv_w', 'L0_attn_q_norm_w', 'L0_attn_k_norm_w', 'L0_attn_lr_proj_w',
        'L0_attn_lr_proj_b', 'L0_attn_w0', 'L0_attn_w1', 'L0_attn_w2', 'L0_ffn_router_w', 'L0_ffn_W1', 'L0_ffn_b1',
        'L0_ffn_W2', 'L0_ffn_b2', 'L1_attn_Wq', 'L1_attn_Wk', 'L1_attn_Wv', 'L1_attn_Wo', 'L1_attn_bo',
        'L1_ffn_router_DE', 'L1_ffn_w1_eDF', 'L1_ffn_w3_eDF', 'L1_ffn_w2_eFD', 'L1_ffn_ws1_DF', 'L1_ffn_ws3_DF',
        'L1_ffn_ws2_FD']


def kernel(**inputs):
    import concourse.bacc as _bacc
    from concourse.bass_utils import run_bass_kernel_spmd as _run

    arrays = {f"in_{name}_dram": np.ascontiguousarray(inputs[name]) for name in _INS}
    known = {}
    for _ in range(2):
        nc = _bacc.Bacc("TRN2", target_bir_lowering=False, num_devices=1)
        io = {name: nc.dram_tensor(f"in_{name}_dram", arrays[f"in_{name}_dram"].shape, F32, kind="ExternalInput").ap()
              for name in _INS}
        out = nc.dram_tensor("out_0_dram", (1, 2048, 128), F32, kind="ExternalOutput").ap()
        known = program(nc, known, io, out)
    r = _run(nc, [arrays], core_ids=[0])
    return r.results[0]["out_0_dram"]
```

```python
from contextlib import ExitStack

import numpy as np

import concourse.bass as bass
import concourse.mybir as mybir

F32 = mybir.dt.float32
F32R = mybir.dt.float32r
BF16 = mybir.dt.bfloat16
I32 = mybir.dt.int32
U32 = mybir.dt.uint32
ALU = mybir.AluOpType
ACT = mybir.ActivationFunctionType
AX = mybir.AxisListType

P = 128
LN_EPS = 1e-5
TILE = 256
TP = TILE // P
CREDIT = 1000


class Tick:

    def __init__(self, counter, value, loop=None):
        self.counter, self.value, self.loop = counter, value, loop

    def back(self, n=1):
        t = Tick(self.counter, self.value, self.loop)
        t.value -= n * self.loop.per(self.counter)
        return t


class Loop:

    def __init__(self, book, name, n):
        self.book, self.name, self.n = book, name, n
        self.open = True
        self.start = {c: c.count for c in book.counters}
        self.index = None

    def per(self, counter):
        return self.book.known.get((self.name, counter.name), 0)

    def close(self):
        self.open = False
        for c in self.book.counters:
            raised = c.count - self.start[c]
            self.book.found[(self.name, c.name)] = raised
            c.count = self.start[c] + self.n * raised


class Counter:

    def __init__(self, book, name, step, credit=CREDIT):
        self.book, self.name, self.step = book, name, step
        self.sem = book.ctx.enter_context(book.nc.semaphore(name))
        self.count = credit
        book.counters.append(self)
        if credit:
            book.nc.sync.sem_inc(self.sem, credit)

    def mark(self, instruction):
        instruction.then_inc(self.sem, self.step)
        self.count += self.step
        return Tick(self, self.count, self.book.loop)


class Queue:

    def __init__(self, book, name, engine):
        self.book, self.name, self.engine = book, name, engine
        self.counter = Counter(book, f"done_{name}", 1)
        self.seen = {}

    def wait(self, *ticks):
        for t in ticks:
            if t is None:
                continue
            loop, value = t.loop, t.value
            if loop is not None and not loop.open:
                value += (loop.n - 1) * loop.per(t.counter)
                loop = None
            key = (t.counter, loop)
            if self.seen.get(key, -1) >= value:
                continue
            self.seen[key] = value
            if loop is None:
                self.engine.wait_ge(t.counter.sem, value)
            else:
                self.engine.wait_ge(t.counter.sem, loop.index * loop.per(t.counter) + value)

    def done(self, instruction):
        return self.counter.mark(instruction)


class Book:

    def __init__(self, nc, ctx, known):
        self.nc, self.ctx, self.known, self.found = nc, ctx, known, {}
        self.counters, self.loop, self.events = [], None, {}
        self.queues = [Queue(self, n, e) for n, e in (
            ("pe", nc.tensor), ("act", nc.scalar), ("dve", nc.vector), ("pool", nc.gpsimd), ("sp", nc.sync))]

    def dma(self, name, credit=CREDIT):
        return Counter(self, name, 16, credit)

    def run(self, name, n, body):
        loop = Loop(self, name, n)
        for q in self.queues:
            q.seen = {k: v for k, v in q.seen.items() if k[1] is None}
        with self.nc.Fori(0, n, 1) as i:
            loop.index, self.loop = i, loop
            self.events[name] = {}
            body(i)
        self.loop = None
        loop.close()
        for q in self.queues:
            q.seen = {k: v for k, v in q.seen.items() if k[1] is None}


def bcast(ap, shape):
    return ap.to_broadcast(list(shape))


class Net:

    def __init__(self, nc, ctx, known, io):
        self.nc, self.ctx, self.io = nc, ctx, io
        self.book = Book(nc, ctx, known)
        self.PE, self.A, self.V, self.G, self.S = self.book.queues
        self.psum = ctx.enter_context(nc.psum_tensor("psum", [P, 8, 512], F32))

    def note(self, key, tick):
        book = self.book
        book.events[book.loop.name][key] = tick
        book.found[("event", book.loop.name, key)] = (tick.counter.name, tick.value - tick.loop.start[tick.counter])

    def prev(self, key):
        book, loop = self.book, self.book.loop
        if ("event", loop.name, key) not in book.known:
            return None
        name, offset = book.known[("event", loop.name, key)]
        counter = next(c for c in book.counters if c.name == name)
        return Tick(counter, loop.start[counter] + offset - loop.per(counter), loop)

    def settle(self, *dmas):
        ticks = [Tick(q.counter, q.counter.count) for q in self.book.queues]
        for q in self.book.queues:
            q.wait(*ticks, *dmas)

    def sb(self, name, shape, dt=F32, ctx=None):
        return (ctx or self.ctx).enter_context(self.nc.sbuf_tensor(name, shape, dt))


class Carry:

    def __init__(self, n, name):
        self.n, self.name, self.now = n, name, {}

    def get(self, key):
        if key in self.now:
            return self.now[key]
        if self.n.book.loop is not None:
            return self.n.prev(key)
        return self.n.book.events.get(self.name, {}).get(key)

    def put(self, key, tick):
        self.now[key] = tick
        if self.n.book.loop is not None:
            self.n.note(key, tick)
        return tick

    def loop(self, count, body):
        self.n.settle()
        self.now = {}

        def fresh(i):
            self.now = {}
            body(i)

        self.n.book.run(self.name, count, fresh)
        self.now = {}


def constants(n):
    nc, G = n.nc, n.G
    n.ident = n.sb("ident", [P, P])
    n.ones = n.sb("ones", [P, P])
    n.blocks = n.sb("blocks", [P, P])
    n.mask4 = n.sb("mask4", [P, 4, 64])
    n.before = n.sb("before", [P, P])
    n.eps = n.sb("eps", [P, 4])
    ts = [G.done(nc.gpsimd.memset(t, v)) for t, v in (
        (n.ident[:, :], 0.0), (n.ones[:, :], 1.0), (n.blocks[:, :], 1.0), (n.mask4[:, :, :], 1.0),
        (n.before[:, :], 1.0), (n.eps[:, 0:1], 1e-6), (n.eps[:, 1:2], LN_EPS), (n.eps[:, 2:3], 1e-7),
        (n.eps[:, 3:4], 0.0))]
    G.wait(ts[-1])

    def keep(t, pattern, base, mult, op=ALU.is_ge, fill=0.0):
        k = G.done(nc.gpsimd.affine_select(out=t, in_=t, pattern=pattern, compare_op=op, fill=fill, base=base,
                                           channel_multiplier=mult))
        G.wait(k)
        return k

    keep(n.ident[:, :], [[-1, P]], 0, 1, ALU.not_equal, 1.0)
    b = n.blocks[:, :].rearrange("p (h x) -> p h x", h=4)
    keep(b, [[-32, 4], [0, 32]], 0, 1)
    keep(b, [[32, 4], [0, 32]], 31, -1)
    keep(n.mask4[:, :, :], [[-32, 4], [0, 64]], 0, 1)
    keep(n.mask4[:, :, :], [[32, 4], [0, 64]], 31, -1)
    keep(n.before[:, :], [[1, P]], -1, -1)
    n.e_less = n.sb("e_less", [P, 8])
    n.steps = n.sb("steps", [P, 16])
    n.count = n.sb("count", [P, 24])
    for t, step, base in ((n.e_less, 1, -8), (n.steps, TILE, 0), (n.count, 1, 0)):
        i32 = n.sb(f"i32_{base}_{step}", [P, t.shape[1]], I32)
        k = G.done(nc.gpsimd.iota(i32[:, :], pattern=[[step, t.shape[1]]], base=base, channel_multiplier=0))
        G.wait(k)
        n.t_const = G.done(nc.gpsimd.tensor_copy(t[:, :], i32[:, :]))



HEADS, DH, HID, CHUNK = 4, 32, 64, 256
TPC = CHUNK // P
BASE_LR_INV = float(np.log(np.expm1(0.001)))
NS = ((4.0848, -6.8946, 2.927), (3.9505, -6.3029, 2.6377), (3.7418, -5.5913, 2.3037),
      (2.8769, -3.1427, 1.2046), (2.8366, -3.0525, 1.2012))


def ttt_attention(n, x_all, y_all, stats, t_x):
    nc, io, PE, A, V, G, S, ps = n.nc, n.io, n.PE, n.A, n.V, n.G, n.S, n.psum
    NT = x_all.shape[1]
    NC = NT // TPC
    with ExitStack() as mem:
        sb = lambda name, shape, dt=F32: n.sb("t_" + name, shape, dt, mem)
        xT = sb("xT", [P, NT * P])
        wT = sb("wT", [P, 384])
        lwT = sb("lwT", [P, 12])
        Wc = sb("Wc", [P, 3, HID])
        WB = sb("WB", [P, 3, HEADS, HID])
        W1T = sb("W1T", [P, 2, P])
        N0 = sb("N0", [P, 129])
        aI = sb("aI", [P, len(NS), P])

        wraw = sb("wraw", [P, 3, P])
        lraw = sb("lraw", [12, P])
        w02 = sb("w02", [HID, 2, HEADS, DH])
        nw = sb("nw", [P, 2, P])
        lb = sb("lb", [P, 12])
        d_w = n.book.dma("ttt_weights")
        for dst, src in (
            (wraw[:, :, :], io["L0_attn_qkv_w"].rearrange("(a p) d -> p a d", p=P)),
            (lraw[:, :], io["L0_attn_lr_proj_w"]),
            (w02[:, 0], io["L0_attn_w0"].rearrange("h i d -> i h d")),
            (w02[:, 1], io["L0_attn_w2"].rearrange("h i d -> i h d")),
            (Wc[:, 2, :], io["L0_attn_w1"].rearrange("h o i -> (h o) i")),
            (nw[:, 0, :], io["L0_attn_q_norm_w"].rearrange("(a d) -> a d", a=1).to_broadcast([P, P])),
            (nw[:, 1, :], io["L0_attn_k_norm_w"].rearrange("(a d) -> a d", a=1).to_broadcast([P, P])),
            (lb[:, :], io["L0_attn_lr_proj_b"].rearrange("(a d) -> a d", a=1).to_broadcast([P, 12])),
        ):
            t_w = d_w.mark(nc.sync.dma_start(dst, src))
        n.prefetch()
        PE.wait(t_w, n.t_const)
        for a in range(3):
            nc.tensor.transpose(ps[:, 0, a * P:(a + 1) * P], wraw[:, a, :], n.ident[:, :])
        nc.tensor.transpose(ps[:, 0, 384:396], lraw[:, :], n.ident[0:12, 0:12])
        for a in range(2):
            t = PE.done(nc.tensor.transpose(ps[:, 1, a * HID:(a + 1) * HID],
                                            w02[:, a].rearrange("i h d -> i (h d)"), n.ident[0:HID, 0:HID]))
        A.wait(t)
        A.done(nc.scalar.activation(wT[:, :], ps[:, 0, 0:384], ACT.Copy))
        t_wT = A.done(nc.scalar.activation(lwT[:, :], ps[:, 0, 384:396], ACT.Copy))
        V.wait(t, n.t_const)
        t_Wc = V.done(nc.vector.tensor_copy(Wc[:, 0:2, :], ps[:, 1, 0:2 * HID].rearrange("p (a i) -> p a i", a=2)))
        for k, (a, b, _) in enumerate(NS):
            t_aI = V.done(nc.vector.tensor_scalar(aI[:, k, :], n.ident[:, :], a / b, None, ALU.mult))
        V.wait(t_w)
        t_lb = V.done(nc.vector.tensor_scalar(lb[:, :], lb[:, :], BASE_LR_INV, None, ALU.add))

        sqw = sb("sqw", [P, 3, HID])
        rs = sb("rs", [P, 129])
        NR = sb("NR", [P, 129])
        Wn = sb("Wn", [P, 3, HID])

        def row_norms(w, t_in, out, t_bank):
            A.wait(t_in)
            t_sq = A.done(nc.scalar.activation(sqw[:, :, :], w[:, :, :], ACT.Square))
            PE.wait(t_sq, t_bank)
            t_s = PE.done(nc.tensor.matmul(ps[:, 3, 0:2 * HID], n.blocks[:, :], sqw[:, 0:2, :], start=True, stop=True))
            V.wait(t_sq)
            t_r = V.done(nc.vector.tensor_reduce(rs[:, 0:1], sqw[:, 2, :], AX.X, ALU.add))
            A.wait(t_s, t_r)
            A.done(nc.scalar.activation(out[:, 0:2 * HID], ps[:, 3, 0:2 * HID], ACT.Sqrt))
            return A.done(nc.scalar.activation(out[:, 2 * HID:2 * HID + 1], rs[:, 0:1], ACT.Sqrt))

        def blocks_of(m, t_w, *t_free):
            V.wait(t_w, *t_free)
            return V.done(nc.vector.tensor_tensor(WB[:, m, :, :], bcast(Wc[:, m, :].unsqueeze(1), [P, HEADS, HID]), n.mask4[:, :, :], ALU.mult))

        V.wait(t_Wc)
        A.wait(t_w)
        t_N0 = row_norms(Wc, t_Wc, N0, None)
        V.wait(t_w)
        for m in range(3):
            blocks_of(m, t_Wc)

        t_xT = transpose_all(n, x_all, xT, t_x, (4, 5, 6))
        PE.wait(*t_xT, t_wT)
        xTs = sb("xTs", [P, CHUNK])
        sq = sb("sq", [P, TPC, 256])
        qw = sb("qw", [P, TPC, 256])
        vv = sb("vv", [P, TPC, P])
        ss = sb("ss", [P, 4])
        s2 = sb("s2", [P, 16])
        qTs, kTs, vTs = (sb(a, [P, CHUNK]) for a in ("qTs", "kTs", "vTs"))
        k0s, k2s, v1s = (sb(f"{a}s", [P, TPC, P]) for a in ("k0", "k2", "v1"))

        def project(c, ev, prev, t_bank, t_used):
            def turn():
                G.wait(prev("used_xT"), t_xT[-1])
                ev["xTs"] = G.done(nc.gpsimd.tensor_copy(xTs[:, :], xT[:, bass.ds(c * CHUNK, CHUNK)]))

            def product(t):
                PE.wait(ev["xTs"], t_wT, *t_bank())
                lhs = xTs[:, t * P:(t + 1) * P]
                ev["p_qk"] = PE.done(nc.tensor.matmul(ps[:, 1, t * 256:(t + 1) * 256], lhs, wT[:, 0:256], start=True, stop=True))
                ev["used_xT"] = PE.done(nc.tensor.matmul(ps[:, 2, t * P:(t + 1) * P], lhs, wT[:, 256:384], start=True, stop=True))

            def weigh():
                k1, k2 = ev["p_qk"], ev["used_xT"]
                A.wait(k1, prev("s2"))
                ev["sq"] = A.done(nc.scalar.activation(sq[:, :, :].rearrange("p a b -> p (a b)"), ps[:, 1, :], ACT.Square))
                A.wait(k2, prev("turned"), prev("scaled"))
                ev["vv"] = A.done(nc.scalar.activation(vv[:, :, :].rearrange("p a b -> p (a b)"), ps[:, 2, 0:256], ACT.Copy))
                V.wait(ev["sq"], prev("turned"), prev("scaled"))
                ev["qw"] = V.done(nc.vector.tensor_tensor(qw[:, :, :].rearrange("p a (m d) -> p a m d", m=2),
                                                          ps[:, 1, :].rearrange("p (a m d) -> p a m d", a=TPC, m=2),
                                                          bcast(nw[:, :, :].unsqueeze(1), [P, TPC, 2, P]), ALU.mult))

            def squares():
                ev["ss"] = V.done(nc.vector.tensor_reduce(ss[:, :], sq[:, :, :].rearrange("p a (m d) -> p (a m) d", m=2), AX.X, ALU.add))
                A.wait(ev["qw"], ev["ss"])
                ev["sq2"] = A.done(nc.scalar.activation(sq[:, :, :], qw[:, :, :], ACT.Square))

            def roots():
                V.wait(ev["sq2"])
                ev["s2"] = V.done(nc.vector.tensor_reduce(s2[:, :], sq[:, :, :].rearrange("p a (h d) -> p (a h) d", d=DH), AX.X, ALU.add))
                A.wait(ev["s2"])
                A.done(nc.scalar.activation(ss[:, :], ss[:, :], ACT.Sqrt, bias=n.eps[:, 0:1], scale=1.0 / P))
                ev["n2"] = A.done(nc.scalar.activation(s2[:, :], s2[:, :], ACT.Sqrt))

            def scales():
                V.wait(ev["n2"])
                t = V.done(nc.vector.reciprocal(ss[:, :], ss[:, :]))
                V.wait(t)
                rb = bcast(ss[:, :].unsqueeze(2), [P, 4, 4])
                s2v = s2[:, :].rearrange("p (g h) -> p g h", h=4)
                t = V.done(nc.vector.tensor_tensor(s2v, s2v, rb, ALU.mult))
                V.wait(t)
                t = V.done(nc.vector.tensor_scalar(s2[:, :], s2[:, :], 1e-5, None, ALU.add))
                V.wait(t)
                t = V.done(nc.vector.reciprocal(s2[:, :], s2[:, :]))
                V.wait(t)
                t = V.done(nc.vector.tensor_tensor(s2v, s2v, rb, ALU.mult))
                G.wait(t)
                qwh = qw[:, :, :].rearrange("p a (h d) -> p (a h) d", d=DH)
                ev["qk"] = G.done(nc.gpsimd.tensor_tensor(qwh, qwh, bcast(s2[:, :].unsqueeze(2), [P, 16, DH]), ALU.mult))

            def rates():
                l4 = lr[:, bass.ds(c * (TPC * 12), TPC * 12)].rearrange("p (a h j) -> p a h j", a=TPC, j=3)
                G.wait(t_lr, ev["qk"], ev["vv"], *t_used())
                for j, src, dst in ((0, qw[:, :, P:256], k0s), (2, qw[:, :, P:256], k2s), (1, vv[:, :, :], v1s)):
                    t_g = G.done(nc.gpsimd.tensor_tensor(
                        dst[:, :, :].rearrange("p a (h d) -> p a h d", d=DH), src.rearrange("p a (h d) -> p a h d", d=DH),
                        bcast(l4[:, :, :, j:j + 1], [P, TPC, HEADS, DH]), ALU.mult))
                ev["scaled"] = t_g

            def transposes():
                PE.wait(ev["qk"], ev["vv"], *t_bank())
                for m in range(3):
                    for t in range(TPC):
                        src = vv[:, t, :] if m == 2 else qw[:, t, m * P:(m + 1) * P]
                        bank, at = ((0, 0), (0, 256), (2, 256))[m]
                        k = PE.done(nc.tensor.transpose(ps[:, bank, at + t * P:at + (t + 1) * P], src, n.ident[:, :]))
                ev["turned"] = k

            def features():
                A.wait(ev["turned"], *t_used())
                A.done(nc.scalar.activation(qTs[:, :], ps[:, 0, 0:256], ACT.Copy))
                A.done(nc.scalar.activation(kTs[:, :], ps[:, 0, 256:512], ACT.Copy))
                ev["ready"] = A.done(nc.scalar.activation(vTs[:, :], ps[:, 2, 256:512], ACT.Copy))

            return turn, lambda: product(0), lambda: product(1), weigh, squares, roots, scales, rates, transposes, features

        sig, hb, db, sg, hd, dg, dh, v1, u = (sb(a, [P, 512]) for a in ("sig", "hb", "db", "sg", "hd", "dg", "dh", "v1", "u"))
        sigq, gq, uq, hq = (sb(a, [P, 512]) for a in ("sigq", "gq", "uq", "hq"))
        X = sb("X", [P, 3, HID])
        XT = sb("XT", [P, 3, P])
        Ab, T1, Gm = (sb(a, [P, 3, P]) for a in ("Ab", "T1", "Gm"))
        fn = sb("fn", [P, 3])
        V.done(nc.vector.memset(XT[:, :, :], 0.0))

        def prev(key):
            return n.prev(key) if n.book.loop is not None else n.book.events.get("scan", {}).get(key)

        def turn_w1():
            PE.wait(prev("WB2"), prev("y"))
            for g in range(2):
                t = PE.done(nc.tensor.transpose(ps[:, 7, g * P:(g + 1) * P],
                                                WB[:, 2, 2 * g:2 * g + 2, :].rearrange("p a b -> p (a b)"), n.ident[:, :]))
            return t

        def keep_w1(t):
            V.wait(t, prev("o"))
            return V.done(nc.vector.tensor_copy(W1T[:, :, :].rearrange("p a b -> p (a b)"), ps[:, 7, 0:256]))

        def forward_products(t_ready):
            PE.wait(prev("WB1"), t_ready, prev("X5"))
            for m in range(2):
                for g in range(2):
                    t = PE.done(nc.tensor.matmul(ps[:, 5 + m, g * 256:(g + 1) * 256],
                                                 WB[:, m, 2 * g:2 * g + 2, :].rearrange("p a b -> p (a b)"),
                                                 qTs[:, :], start=True, stop=True))
            A.wait(t, prev("hq"))
            A.done(nc.scalar.activation(sigq[:, :], ps[:, 5, :], ACT.Sigmoid))
            A.done(nc.scalar.activation(gq[:, :], ps[:, 5, :], ACT.Copy))
            t_q = A.done(nc.scalar.activation(uq[:, :], ps[:, 6, :], ACT.Copy))
            return t, t_q

        def gate_job(t_q):
            G.wait(t_q, prev("o"))
            t = G.done(nc.gpsimd.tensor_tensor(gq[:, :], gq[:, :], sigq[:, :], ALU.mult))
            G.wait(t)
            return G.done(nc.gpsimd.tensor_tensor(hq[:, :], uq[:, :], gq[:, :], ALU.mult))

        def forward_output(t_h, t_w1t):
            PE.wait(t_h, t_w1t)
            for t in range(TPC):
                for g in range(2):
                    k = PE.done(nc.tensor.matmul(ps[:, 7, t * P:(t + 1) * P], hq[:, g * 256 + t * P:g * 256 + (t + 1) * P],
                                                 W1T[:, g, :], start=(g == 0), stop=(g == 1)))
            return k

        def residual(c, k):
            V.wait(k)
            yc = y_all[:, bass.ds(c * TPC, TPC), :]
            t_y = V.done(nc.vector.tensor_tensor(yc, ps[:, 7, 0:256].rearrange("p (a b) -> p a b", a=TPC),
                                                 x_all[:, bass.ds(c * TPC, TPC), :], ALU.add))
            V.wait(t_y)
            for t in range(TPC):
                t_st = V.done(nc.vector.bn_stats(stats[:, bass.ds(c * TPC + t, 1), :].rearrange("p a s -> p (a s)"),
                                                 y_all[:, bass.ds(c * TPC + t, 1), :].rearrange("p a d -> p (a d)")))
            return t_y, t_st

        def update(c):
            ev = {}
            parts = list(project(c + 1, ev, prev, lambda: (t_sg, t_hb, t_db), lambda: (t_gr, t_q)))
            part = lambda: parts.pop(0)()
            part()
            PE.wait(prev("ready"))
            tk = [None] * 3
            for m, lhs in ((0, kTs), (1, kTs), (2, vTs)):
                PE.wait(prev(f"WB{m}"))
                for t in range(TPC):
                    k = nc.tensor.matmul(ps[:, m, t * 256:(t + 1) * 256], lhs[:, t * P:(t + 1) * P],
                                         WB[:, m].rearrange("p h i -> p (h i)"), start=True, stop=True)
                tk[m] = PE.done(k)
            A.wait(tk[0])
            t_sig = A.done(nc.scalar.activation(sig[:, :], ps[:, 0, :], ACT.Sigmoid))
            A.wait(tk[1])
            t_hb = A.done(nc.scalar.activation(hb[:, :], ps[:, 1, :], ACT.Copy))
            A.wait(tk[2])
            t_db = A.done(nc.scalar.activation(db[:, :], ps[:, 2, :], ACT.Copy))
            V.wait(t_sig)
            t_sg = V.done(nc.vector.tensor_tensor(sg[:, :], ps[:, 0, :], sig[:, :], ALU.mult))
            V.wait(t_sg)
            t_v1 = V.done(nc.vector.scalar_tensor_tensor(v1[:, :], sg[:, :], -1.0, sig[:, :], ALU.add, ALU.mult))
            V.wait(t_v1)
            t_u = V.done(nc.vector.tensor_tensor(u[:, :], sg[:, :], v1[:, :], ALU.subtract))
            V.wait(t_hb, t_db)
            t_dg = V.done(nc.vector.tensor_tensor(dg[:, :], db[:, :], hb[:, :], ALU.mult))
            V.wait(t_dg)
            t_dga = V.done(nc.vector.tensor_tensor(dg[:, :], dg[:, :], u[:, :], ALU.mult))
            G.wait(t_sg, t_hb, t_db, t_aI)
            t_dh = G.done(nc.gpsimd.tensor_tensor(dh[:, :], db[:, :], sg[:, :], ALU.mult))
            t_hid = G.done(nc.gpsimd.tensor_tensor(hd[:, :], sg[:, :], hb[:, :], ALU.mult))
            t_q, t_qa = forward_products(None)
            t_h = gate_job(t_qa)
            t_w1t = keep_w1(turn_w1())
            PE.wait(prev("X5"))
            for m, lhs, rhs, tr in ((1, k2s, dh, t_dh), (2, v1s, hd, t_hid), (0, k0s, dg, t_dga)):
                PE.wait(tr)
                for h in range(HEADS):
                    for t in range(TPC):
                        k = nc.tensor.matmul(ps[h * DH:(h + 1) * DH, 3, m * HID:(m + 1) * HID],
                                             lhs[:, t, h * DH:(h + 1) * DH], rhs[:, t * 256 + h * HID:t * 256 + (h + 1) * HID],
                                             start=(t == 0), stop=(t == 1), tile_position=(0, h * DH))
            t_gr = PE.done(k)
            grads = ps[:, 3, 0:192].rearrange("p (m i) -> p m i", m=3)
            part()
            A.wait(t_gr)
            t = A.done(nc.scalar.activation(sqw[:, :, :], grads, ACT.Square))
            V.wait(t)
            t = V.done(nc.vector.tensor_reduce(fn[:, :], sqw[:, :, :], AX.X, ALU.add))
            PE.wait(t)
            t = PE.done(nc.tensor.matmul(ps[:, 3, 256:259], n.blocks[:, :], fn[:, :], start=True, stop=True))
            part()
            A.wait(t)
            t = A.done(nc.scalar.activation(fn[:, :], ps[:, 3, 256:259], ACT.Sqrt))
            V.wait(t)
            t = V.done(nc.vector.tensor_scalar(fn[:, :], fn[:, :], 1e-7, None, ALU.add))
            V.wait(t)
            t = V.done(nc.vector.reciprocal(fn[:, :], fn[:, :]))
            V.wait(t)
            t_X = V.done(nc.vector.tensor_tensor(X[:, :, :], grads, bcast(fn[:, :].unsqueeze(2), [P, 3, HID]), ALU.mult))
            part()
            PE.wait(t_X, t_qa)
            tX, tXT = [t_X] * 3, [None] * 3
            k01 = PE.done(nc.tensor.transpose(ps[:, 4, 0:P], X[:, 0:2, :].rearrange("p a b -> p (a b)"), n.ident[:, :]))
            k2 = PE.done(nc.tensor.transpose(ps[0:HID, 6, 0:P], X[:, 2, :], n.ident[:, :]))
            A.wait(k01)
            for m, rows in ((0, ps[0:HID, 4, 0:P]), (1, ps[HID:P, 4, 0:P]), (2, ps[0:HID, 6, 0:P])):
                if m == 2:
                    A.wait(k2)
                tXT[m] = A.done(nc.scalar.activation(XT[0:HID, m, :], rows, ACT.Copy))
            tXT[0] = tXT[1]
            for it, (_, cb, cc) in enumerate(NS):
                last = it == len(NS) - 1
                tA, tAb, tT, tAA, tG = ([None] * 3 for _ in range(5))
                for m in range(3):
                    PE.wait(tXT[m])
                    tA[m] = PE.done(nc.tensor.matmul(ps[:, 4 + m, 0:P], XT[:, m, :], XT[:, m, :], start=True, stop=True))
                for m in range(3):
                    V.wait(tA[m])
                    tAb[m] = V.done(nc.vector.tensor_tensor(Ab[:, m, :], ps[:, 4 + m, 0:P], n.blocks[:, :], ALU.mult))
                for m in range(3):
                    PE.wait(tAb[m])
                    tAA[m] = PE.done(nc.tensor.matmul(ps[:, 4 + m, P:2 * P], Ab[:, m, :], Ab[:, m, :], start=True, stop=True))
                    G.wait(tAb[m], prev("X5"))
                    tT[m] = G.done(nc.gpsimd.tensor_tensor(T1[:, m, :], Ab[:, m, :], aI[:, it, :], ALU.add))
                for m in range(3):
                    V.wait(tAA[m], tT[m])
                    tG[m] = V.done(nc.vector.scalar_tensor_tensor(Gm[:, m, :], ps[:, 4 + m, P:2 * P], cc / cb, T1[:, m, :], ALU.mult, ALU.add))
                for m in range(3):
                    PE.wait(tG[m], tX[m])
                    k = nc.tensor.matmul(ps[:, 4 + m, 256:256 + HID], Gm[:, m, :], X[:, m, :], start=True, stop=True)
                    if not last:
                        k = nc.tensor.matmul(ps[0:HID, 4 + m, 384:512], X[:, m, :], Gm[:, m, :], start=True, stop=True)
                    k = PE.done(k)
                    if not last:
                        A.wait(k)
                        tX[m] = A.done(nc.scalar.activation(X[:, m, :], ps[:, 4 + m, 256:256 + HID], ACT.Copy, scale=cb))
                        tXT[m] = A.done(nc.scalar.activation(XT[0:HID, m, :], ps[0:HID, 4 + m, 384:512], ACT.Copy, scale=cb))
                if it < len(NS) - 1:
                    part()
            V.wait(k)
            t_Wn = V.done(nc.vector.scalar_tensor_tensor(Wn[:, :, :], ps[:, 4:7, 256:256 + HID], NS[-1][1], Wc[:, :, :], ALU.mult, ALU.add))
            n.note("X5", t_Wn)
            t_r = row_norms(Wn, t_Wn, NR, t_X)
            k_o = forward_output(t_h, t_w1t)
            part()
            part()
            t_wb = {}
            for m, at in ((0, slice(0, HID)), (1, slice(HID, 2 * HID + 1))):
                V.wait(t_r, t_N0)
                t = V.done(nc.vector.tensor_scalar(NR[:, at], NR[:, at], 1e-5, None, ALU.add))
                V.wait(t)
                t = V.done(nc.vector.reciprocal(NR[:, at], NR[:, at]))
                V.wait(t)
                t = V.done(nc.vector.tensor_tensor(NR[:, at], NR[:, at], N0[:, at], ALU.mult))
                V.wait(t)
                t = V.done(nc.vector.tensor_tensor(Wc[:, m, :], Wn[:, m, :], NR[:, m * HID:(m + 1) * HID], ALU.mult))
                t_wb[f"WB{m}"] = blocks_of(m, t, t_q)
                if m == 1:
                    t = V.done(nc.vector.tensor_scalar(Wc[:, 2, :], Wn[:, 2, :], NR[:, 128:129], None, ALU.mult))
                    t_wb["WB2"] = blocks_of(2, t, t_w1t)
            t_y, t_st = residual(c, k_o)
            assert not parts
            ev.update(t_wb, hq=t_h, y=t_y, o=k_o)
            for key, tick in ev.items():
                n.note(key, tick)

        ev = {}
        parts = project(0, ev, lambda key: None, lambda: (), lambda: ())
        for part in parts[:7]:
            part()

        PE.wait(t_N0)
        for i in range(NT):
            k = PE.done(nc.tensor.matmul(ps[:, 3, i * 12:(i + 1) * 12], xT[:, i * P:(i + 1) * P], lwT[:, :], start=True, stop=True))
        z, s_, w_, w2_, ac, lr = (sb(a, [P, NT * 12]) for a in ("z", "s_", "w_", "w2_", "ac", "lr"))
        V.wait(k, t_lb)
        t_z = V.done(nc.vector.tensor_tensor(z[:, :].rearrange("p (a b) -> p a b", a=NT),
                                             ps[:, 3, 0:NT * 12].rearrange("p (a b) -> p a b", a=NT),
                                             bcast(lb[:, :].unsqueeze(1), [P, NT, 12]), ALU.add))
        V.wait(t_z)
        t = V.done(nc.vector.scalar_tensor_tensor(s_[:, :], z[:, :], -1.0, z[:, :], ALU.mult, ALU.min))
        A.wait(t)
        t = A.done(nc.scalar.activation(s_[:, :], s_[:, :], ACT.Sigmoid))
        V.wait(t)
        t = V.done(nc.vector.tensor_scalar(w_[:, :], s_[:, :], -1.0, 2.0, ALU.mult, ALU.add))
        V.wait(t)
        t = V.done(nc.vector.reciprocal(w_[:, :], w_[:, :]))
        V.wait(t)
        t = V.done(nc.vector.tensor_tensor(w_[:, :], w_[:, :], s_[:, :], ALU.mult))
        V.wait(t)
        t = V.done(nc.vector.tensor_tensor(w2_[:, :], w_[:, :], w_[:, :], ALU.mult))
        V.wait(t)
        t = V.done(nc.vector.tensor_scalar(ac[:, :], w2_[:, :], 1.0 / 17, None, ALU.mult))
        for k in (15, 13, 11, 9, 7, 5, 3):
            V.wait(t)
            t = V.done(nc.vector.scalar_tensor_tensor(ac[:, :], ac[:, :], 1.0 / k, w2_[:, :], ALU.add, ALU.mult))
        V.wait(t)
        t = V.done(nc.vector.scalar_tensor_tensor(ac[:, :], ac[:, :], 1.0, w_[:, :], ALU.add, ALU.mult))
        V.wait(t)
        t = V.done(nc.vector.tensor_scalar(ac[:, :], ac[:, :], 2.0, None, ALU.mult))
        V.wait(t)
        t_lr = V.done(nc.vector.scalar_tensor_tensor(lr[:, :], z[:, :], 0.0, ac[:, :], ALU.max, ALU.add))

        for part in parts[7:]:
            part()
        n.settle()
        n.book.run("scan", NC - 1, update)
        t_q, t_qa = forward_products(prev("ready"))
        t_h = gate_job(t_qa)
        t = residual(NC - 1, forward_output(t_h, keep_w1(turn_w1())))[1]
        n.settle()
        return lambda: [norm_group(n, g, y_all, stats, t, x_all, True) for g in range(NT // GROUP)]



GROUP = 4


def norm_group(n, g, y_all, stats, t, out, have_stats=False):
    nc, V, A = n.nc, n.V, n.A
    tiles = range(g * GROUP, (g + 1) * GROUP)
    at = slice(g * GROUP, (g + 1) * GROUP)
    mv, sd = n.mv, n.sd
    V.wait(t)
    if not have_stats:
        for i in tiles:
            t = V.done(nc.vector.bn_stats(stats[:, i, :], y_all[:, i, :]))
        V.wait(t)
    for i in tiles:
        t = V.done(nc.vector.bn_aggr(mv[:, i, :], stats[:, i, :]))
    A.wait(t)
    t = A.done(nc.scalar.activation(sd[:, at], mv[:, at, 1:2].rearrange("p a b -> p (a b)"), ACT.Sqrt, bias=n.eps[:, 1:2]))
    V.wait(t)
    t = V.done(nc.vector.reciprocal(sd[:, at], sd[:, at]))
    V.wait(t)
    for i in tiles:
        t = V.done(nc.vector.tensor_scalar(out[:, i, :], y_all[:, i, :], mv[:, i, 0:1], sd[:, i:i + 1], ALU.subtract, ALU.mult))
    return t


def transpose_all(n, x_all, xT, t_x, banks=(0, 1), after=None):
    nc, PE, A = n.nc, n.PE, n.A
    free = [None] * len(banks)
    ticks = []
    for g in range(x_all.shape[1] // GROUP):
        k = g % len(banks)
        PE.wait(t_x[g], free[k])
        for i in range(GROUP):
            t = PE.done(nc.tensor.transpose(n.psum[:, banks[k], i * P:(i + 1) * P], x_all[:, GROUP * g + i, :], n.ident[:, :]))
        A.wait(t)
        free[k] = A.done(nc.scalar.activation(xT[:, g * 512:(g + 1) * 512], n.psum[:, banks[k], :], ACT.Copy))
        ticks.append(free[k])
        if after and g:
            after(g - 1, ticks[g - 1])
    if after:
        after(g, ticks[g])
    return ticks


def route(n, x_all, xT, rT, t_x, bank):
    nc, PE = n.nc, n.PE
    E, NT = rT.shape[1], x_all.shape[1]
    last = []

    def logits(g, t):
        PE.wait(t)
        for i in range(g * GROUP, (g + 1) * GROUP):
            k = PE.done(nc.tensor.matmul(n.psum[:, bank, i * E:(i + 1) * E], xT[:, i * P:(i + 1) * P], rT, start=True, stop=True))
        last.append(k)

    transpose_all(n, x_all, xT, t_x, after=logits)
    return last[-1], n.psum[:, bank, 0:NT * E].rearrange("p (t e) -> p t e", e=E)


def top_one(n, sb, logits, t_logits):
    nc, V, G = n.nc, n.V, n.G
    NT, E = logits.shape[1:]
    mx = sb("mx", [P, NT])
    hot = sb("hot", [P, NT, E])
    cand = sb("cand", [P, NT, E])
    idx = sb("idx", [P, NT])
    V.wait(t_logits)
    t_mx = V.done(nc.vector.tensor_reduce(mx[:, :], logits, AX.X, ALU.max))
    V.wait(t_mx)
    t = V.done(nc.vector.tensor_tensor(cand[:, :, :], logits, bcast(mx[:, :].unsqueeze(2), [P, NT, E]), ALU.is_ge))
    V.wait(t)
    t = V.done(nc.vector.tensor_tensor(cand[:, :, :], cand[:, :, :], bcast(n.e_less[:, :].unsqueeze(1), [P, NT, E]), ALU.mult))
    V.wait(t)
    t = V.done(nc.vector.tensor_reduce(idx[:, :], cand[:, :, :], AX.X, ALU.min))
    V.wait(t)
    t = V.done(nc.vector.tensor_tensor(hot[:, :, :], bcast(n.e_less[:, :].unsqueeze(1), [P, NT, E]),
                                       bcast(idx[:, :].unsqueeze(2), [P, NT, E]), ALU.is_equal))
    return mx, hot, t_mx, t


def capacity(n, sb, logits, mx, hot, t_mx, t_hot, cap):
    nc, V, A, PE = n.nc, n.V, n.A, n.PE
    NT, E = hot.shape[1:]
    ps = n.psum
    ex = sb("ex", [P, NT, E])
    pr = sb("pr", [P, NT])
    prow = sb("prow", [P, NT * P])
    gt = sb("gt", [P, 2, NT * P], BF16)
    eq = sb("eq", [P, 2, P], BF16)
    hotb = sb("hotb", [P, NT, E], BF16)
    rank = sb("rank", [P, NT, E])
    rk = sb("rk", [P, NT])
    V.wait(t_mx)
    t = V.done(nc.vector.tensor_tensor(ex[:, :, :], logits, bcast(mx[:, :].unsqueeze(2), [P, NT, E]), ALU.subtract))
    A.wait(t)
    t = A.done(nc.scalar.activation(ex[:, :, :], ex[:, :, :], ACT.Exp))
    V.wait(t)
    t = V.done(nc.vector.tensor_reduce(pr[:, :], ex[:, :, :], AX.X, ALU.add))
    V.wait(t)
    t_pr = V.done(nc.vector.reciprocal(pr[:, :], pr[:, :]))
    V.wait(t_hot)
    t_hb = V.done(nc.vector.tensor_copy(hotb[:, :, :], hot[:, :, :]))
    PE.wait(t_pr)
    for g in range(NT // 4):
        for i in range(4):
            t = PE.done(nc.tensor.transpose(ps[:, 4 + g % 4, i * P:(i + 1) * P],
                                            bcast(pr[:, 4 * g + i:4 * g + i + 1], [P, P]), n.ident[:, :]))
        A.wait(t)
        t_row = A.done(nc.scalar.activation(prow[:, g * 512:(g + 1) * 512], ps[:, 4 + g % 4, :], ACT.Copy))
    V.wait(t_row)
    free = [None, None]
    for i in range(NT):
        s = i % 2
        V.wait(free[s])
        me = slice(i * P, (i + 1) * P)
        V.done(nc.vector.tensor_scalar(gt[:, s, 0:(i + 1) * P], prow[:, 0:(i + 1) * P], pr[:, i:i + 1], None, ALU.is_lt))
        if i < NT - 1:
            V.done(nc.vector.tensor_scalar(gt[:, s, (i + 1) * P:], prow[:, (i + 1) * P:], pr[:, i:i + 1], None, ALU.is_le))
        t = V.done(nc.vector.scalar_tensor_tensor(eq[:, s, :], prow[:, me], pr[:, i:i + 1], n.before[:, :], ALU.is_equal, ALU.mult))
        PE.wait(t, t_hb)
        for j in range(NT):
            k = nc.tensor.matmul(ps[:, 3, j * E:(j + 1) * E], gt[:, s, j * P:(j + 1) * P], hotb[:, i, :],
                                 start=(i == 0 and j == 0), stop=False, skip_group_check=True)
        k = nc.tensor.matmul(ps[:, 3, i * E:(i + 1) * E], eq[:, s, :], hotb[:, i, :], start=False, stop=(i == NT - 1),
                             skip_group_check=True)
        free[s] = PE.done(k)
    V.wait(free[s], t_hot)
    t = V.done(nc.vector.tensor_tensor(rank[:, :, :], ps[:, 3, 0:NT * E].rearrange("p (t e) -> p t e", e=E),
                                       hot[:, :, :], ALU.mult))
    V.wait(t)
    t = V.done(nc.vector.tensor_reduce(rk[:, :], rank[:, :, :], AX.X, ALU.add))
    V.wait(t)
    t = V.done(nc.vector.tensor_scalar(rk[:, :], rk[:, :], float(cap), None, ALU.is_lt))
    V.wait(t)
    t = V.done(nc.vector.tensor_tensor(hot[:, :, 1:E], hot[:, :, 1:E], bcast(rk[:, :].unsqueeze(2), [P, NT, E - 1]), ALU.mult))
    V.wait(t)
    t = V.done(nc.vector.tensor_reduce(rk[:, :], hot[:, :, 1:E], AX.X, ALU.add))
    V.wait(t)
    return V.done(nc.vector.tensor_scalar(hot[:, :, 0:1], rk[:, :].unsqueeze(2), -1.0, 1.0, ALU.mult, ALU.add))


def dispatch(n, sb, hot, t_hot, tiles, bank, slots, experts):
    nc, V, PE = n.nc, n.V, n.PE
    NT, E = hot.shape[1:]
    ps = n.psum
    tot = sb("tot", [P, 2, NT + 1, E])
    cnt = sb("cnt", [P, E, NT])
    nt = sb("nt", [P, 2, E + 1])
    te = sb("te", [P, tiles, E])
    tef = sb("tef", [P, tiles])
    pos = sb("pos", [P, NT, E])
    sl = sb("sl", [P, NT])
    hv = hot[:, :, :].rearrange("p t e -> p (t e)")
    PE.wait(t_hot)
    w = NT * E
    nc.tensor.matmul(ps[:, bank, 0:w], n.before[:, :], hv, start=True, stop=True)
    t = PE.done(nc.tensor.matmul(ps[:, bank, w:2 * w], n.ones[:, :], hv, start=True, stop=True))
    within = ps[:, bank, 0:w].rearrange("p (t e) -> p t e", e=E)
    V.wait(t)
    t = V.done(nc.vector.memset(tot[:, :, 0, :], 0.0))
    a = V.done(nc.vector.tensor_copy(tot[:, 0, 1:NT + 1, :], ps[:, bank, w:2 * w].rearrange("p (t e) -> p t e", e=E)))
    src, d = 0, 1
    while d < NT:
        V.wait(a)
        V.done(nc.vector.tensor_copy(tot[:, 1 - src, 1:d + 1, :], tot[:, src, 1:d + 1, :]))
        a = V.done(nc.vector.tensor_tensor(tot[:, 1 - src, d + 1:NT + 1, :], tot[:, src, d + 1:NT + 1, :],
                                           tot[:, src, 1:NT + 1 - d, :], ALU.add))
        src, d = 1 - src, 2 * d
    V.wait(a)
    a = V.done(nc.vector.tensor_tensor(cnt[:, :, :], bcast(tot[:, src, NT, :].unsqueeze(2), [P, E, NT]),
                                       bcast(n.steps[:, :].unsqueeze(1), [P, E, NT]), ALU.is_gt))
    V.wait(a)
    V.done(nc.vector.memset(nt[:, :, 0:1], 0.0))
    a = V.done(nc.vector.tensor_reduce(nt[:, 0, 1:E + 1], cnt[:, :, :], AX.X, ALU.add))
    cur, d = 0, 1
    while d < E:
        V.wait(a)
        V.done(nc.vector.tensor_copy(nt[:, 1 - cur, 1:d + 1], nt[:, cur, 1:d + 1]))
        a = V.done(nc.vector.tensor_tensor(nt[:, 1 - cur, d + 1:E + 1], nt[:, cur, d + 1:E + 1], nt[:, cur, 1:E + 1 - d], ALU.add))
        cur, d = 1 - cur, 2 * d
    V.wait(a)
    a = V.done(nc.vector.tensor_tensor(te[:, :, :], bcast(nt[:, cur, 1:E + 1].unsqueeze(1), [P, tiles, E]),
                                       bcast(n.count[:, 0:tiles].unsqueeze(2), [P, tiles, E]), ALU.is_le))
    V.wait(a)
    a = V.done(nc.vector.tensor_reduce(tef[:, :], te[:, :, :], AX.X, ALU.add))
    V.wait(a)
    t_te = V.done(nc.vector.tensor_scalar(experts[:, :], tef[0:1, :], float(E - 1), None, ALU.min))
    a = V.done(nc.vector.scalar_tensor_tensor(pos[:, :, :], bcast(nt[:, cur, 0:E].unsqueeze(1), [P, NT, E]), float(TILE),
                                              tot[:, src, 0:NT, :], ALU.mult, ALU.add))
    V.wait(a)
    a = V.done(nc.vector.tensor_tensor(pos[:, :, :], within, pos[:, :, :], ALU.add))
    V.wait(a)
    a = V.done(nc.vector.tensor_tensor(pos[:, :, :], pos[:, :, :], hot[:, :, :], ALU.mult))
    V.wait(a)
    a = V.done(nc.vector.tensor_reduce(sl[:, :], pos[:, :, :], AX.X, ALU.add))
    V.wait(a)
    return V.done(nc.vector.tensor_copy(slots[:, :], sl[:, :])), t_te


def scatter(n, rows, x_all, slots, t_in, name):
    n.G.wait(*t_in)
    d = n.book.dma(name, 0)
    for i in range(x_all.shape[1]):
        t = d.mark(n.nc.gpsimd.indirect_dma_start(rows, bass.IndirectOffsetOnAxis(slots[:, i:i + 1], 0), x_all[:, i, :], None))
    return t


def gather_norm(n, rows, got, slots, t_in, name, base, y_all, stats, out):
    n.G.wait(*t_in)
    n.A.done(n.nc.scalar.activation(n.warm[:, :], n.eps[:, 0:1], ACT.Sqrt))
    NT = got.shape[1]
    d = [n.book.dma(f"{name}{g}", 0) for g in range(NT // GROUP)]
    ticks = [d[i // GROUP].mark(n.nc.gpsimd.indirect_dma_start(got[:, i, :], None, rows, bass.IndirectOffsetOnAxis(slots[:, i:i + 1], 0)))
             for i in range(NT)]
    t_out = []
    for g in range(NT // GROUP):
        at = slice(g * GROUP, (g + 1) * GROUP)
        n.V.wait(ticks[g * GROUP + GROUP - 1])
        t = n.V.done(n.nc.vector.tensor_tensor(y_all[:, at, :], base[:, at, :], got[:, at, :], ALU.add))
        t_out.append(norm_group(n, g, y_all, stats, t, out))
    return t_out


class Tiles:

    def __init__(self, n, sb, name, x_rows, y_rows, bank_in, bank_out):
        self.n, self.c = n, Carry(n, name)
        self.x_rows, self.y_rows = (r.rearrange("(t p) d -> p t d", p=P) for r in (x_rows, y_rows))
        self.xt, self.xT, self.yT, self.yt = (sb("tile_" + a, [P, 2, TILE]) for a in ("x", "xT", "yT", "y"))
        self.bank_in, self.bank_out = bank_in, bank_out
        self.d_x = [n.book.dma(f"{name}_x{u}") for u in range(2)]
        self.d_y = [n.book.dma(f"{name}_y{u}") for u in range(2)]

    def load(self, t, u):
        n, c = self.n, self.c
        n.S.wait(c.get(f"in{u}"))
        c.put(f"x{u}", self.d_x[u].mark(n.nc.sync.dma_start(
            self.xt[:, u, :].rearrange("p (a d) -> p a d", a=TP), self.x_rows[:, bass.ds(t * TP, TP), :])))

    def turn_in(self, u):
        n, c = self.n, self.c
        n.PE.wait(c.get(f"x{u}"), c.get("in_free"), c.get("out_free"))
        for a in range(TP):
            k = n.PE.done(n.nc.tensor.transpose(n.psum[:, self.bank_in, a * P:(a + 1) * P], self.xt[:, u, a * P:(a + 1) * P], n.ident[:, :]))
        c.put(f"in{u}", k)
        n.V.wait(k, c.get(f"up{u}"))
        c.put(f"xT{u}", c.put("in_free", n.V.done(n.nc.vector.tensor_copy(self.xT[:, u, :], n.psum[:, self.bank_in, 0:TILE]))))

    def turn_out(self, t, u):
        n, c = self.n, self.c
        n.PE.wait(c.get(f"yT{u}"), c.get("in_free"), c.get("out_free"))
        for a in range(TP):
            k = n.PE.done(n.nc.tensor.transpose(n.psum[:, self.bank_out, TILE + a * P:TILE + (a + 1) * P], self.yT[:, u, a * P:(a + 1) * P],
                                                n.ident[:, :]))
        c.put(f"out{u}", k)
        n.A.wait(k, c.get(f"st{u}"))
        k = n.A.done(n.nc.scalar.activation(self.yt[:, u, :], n.psum[:, self.bank_out, TILE:2 * TILE], ACT.Copy))
        c.put("out_free", k)
        n.S.wait(k)
        c.put(f"st{u}", self.d_y[u].mark(n.nc.sync.dma_start(
            self.y_rows[:, bass.ds(t * TP, TP), :], self.yt[:, u, :].rearrange("p (a d) -> p a d", a=TP))))

    def run(self, tiles, experts, prepare_up, prepare_down, up, down):
        def step(t, s, load=True, prep=True, out=True, dn=True):
            if prep:
                e = expert(t + 1)
                self.turn_in(1 - s)
                prepare_up(e, 1 - s)
            if load:
                self.load(t + 3, 1 - s)
            up(s)
            if out:
                self.turn_out(t - 2, s)
            if dn:
                down(1 - s)
            if prep:
                prepare_down(e, 1 - s)

        def expert(t):
            return self.n.nc.vector.value_load(experts[0:1, bass.ds(t, 1)], min_val=0, max_val=self.n.experts - 1)

        for u in range(2):
            self.load(u, u)
        self.turn_in(0)
        e = expert(0)
        prepare_up(e, 0)
        prepare_down(e, 0)
        self.load(2, 0)
        step(0, 0, out=False, dn=False)
        step(1, 1, out=False)
        pairs = (tiles - 6) // 2
        self.c.loop(pairs, lambda i: [step(2 * i + 2 + u, u) for u in range(2)])
        for t in range(2 * pairs + 2, tiles + 2):
            if t < tiles:
                step(t, t % 2, t + 3 < tiles, t + 1 < tiles)
            else:
                self.turn_out(t - 2, t % 2)
                if t == tiles:
                    down(1 - t % 2)
        return [self.c.get(f"st{u}") for u in range(2)]



def relu_weights(n, mem):
    io = n.io
    E, _, F = io["L0_ffn_W1"].shape
    n.relu_w = [n.sb("r_" + a, shape, F32, mem) for a, shape in (
        ("W1", [P, E * F]), ("W2", [P, E * F]), ("b1raw", [E, F]), ("b2raw", [E, P]), ("rraw", [E, P]))]


def relu_loads(n):
    nc, io = n.nc, n.io
    E = io["L0_ffn_W1"].shape[0]
    W1, W2, b1raw, b2raw, rraw = n.relu_w
    d_s, d_w = n.book.dma("relu_small"), n.book.dma("relu_weights")
    for dst, src in ((rraw[:, :], io["L0_ffn_router_w"]), (b1raw[:, :], io["L0_ffn_b1"]), (b2raw[:, :], io["L0_ffn_b2"])):
        t_s = d_s.mark(nc.sync.dma_start(dst, src))
    for dst, src in ((W1[:, :].rearrange("p (e f) -> p e f", e=E), io["L0_ffn_W1"].rearrange("e p f -> p e f")),
                     (W2[:, :].rearrange("p (g d) -> p g d", d=P), io["L0_ffn_W2"].rearrange("e (c p) d -> p (e c) d", p=P))):
        t_w = d_w.mark(nc.sync.dma_start(dst, src))
    n.relu_ready = t_s, t_w


def relu_experts(n, x_all, y_all, stats, finish):
    nc, io, PE, A, V, G, S, ps = n.nc, n.io, n.PE, n.A, n.V, n.G, n.S, n.psum
    E, _, F = io["L0_ffn_W1"].shape
    FC = F // P
    NT = x_all.shape[1]
    cap = -(-NT * P * 5 // (4 * E))
    tiles = n.tiles
    with ExitStack() as mem:
        sb = lambda name, shape, dt=F32: n.sb("r_" + name, shape, dt, mem)
        W1, W2, b1raw, b2raw, rraw = n.relu_w
        t_s, t_w = n.relu_ready
        t_x = finish()
        b1 = sb("b1", [P, E * FC])
        b2 = sb("b2", [P, E])
        rT = sb("rT", [P, E])
        PE.wait(t_s)
        nc.tensor.transpose(ps[:, 2, 0:E], rraw[:, :], n.ident[0:E, 0:E])
        for c in range(FC):
            nc.tensor.transpose(ps[:, 2, (c + 1) * E:(c + 2) * E], b1raw[:, c * P:(c + 1) * P], n.ident[0:E, 0:E])
        t = PE.done(nc.tensor.transpose(ps[:, 2, (FC + 1) * E:(FC + 2) * E], b2raw[:, :], n.ident[0:E, 0:E]))
        V.wait(t)
        V.done(nc.vector.tensor_copy(rT[:, :], ps[:, 2, 0:E]))
        V.done(nc.vector.tensor_copy(b1[:, :].rearrange("p (e c) -> p c e", c=FC),
                                            ps[:, 2, E:E + FC * E].rearrange("p (c e) -> p c e", c=FC)))
        t_b2 = V.done(nc.vector.tensor_copy(b2[:, :], ps[:, 2, (FC + 1) * E:(FC + 2) * E]))
        slots, experts = n.slots, sb("experts", [1, tiles], I32)
        with ExitStack() as tmp:
            tb = lambda name, shape, dt=F32: n.sb("rr_" + name, shape, dt, tmp)
            xT = tb("xT", [P, NT * P])
            PE.wait(t_b2)
            t_lg, logits = route(n, x_all, xT, rT[:, :], t_x, 2)
            mx, hot, t_mx, t_hot = top_one(n, tb, logits, t_lg)
            t_hot = capacity(n, tb, logits, mx, hot, t_mx, t_hot, cap)
            t_slots, t_te = dispatch(n, tb, hot, t_hot, tiles, 4, slots, experts)
            n.settle()
        t_sc = scatter(n, n.x_rows[0], x_all, slots, (t_slots, *t_x, n.t_zero), "relu_scatter")

        W1s, W2s, h = (sb(a, [P, 2, w]) for a, w in (("W1s", F), ("W2s", F), ("h", FC * TILE)))
        bs = sb("bs", [P, 2, FC + 1])
        tl = Tiles(n, sb, "relu_tiles", n.x_rows[0], n.y_rows[0], 4, 6)
        get, put = tl.c.get, tl.c.put
        S.wait(t_sc)
        V.wait(t_w, t_te)

        def prepare_up(e, u):
            V.wait(get(f"up{u}"))
            put(f"W1{u}", V.done(nc.vector.tensor_copy(W1s[:, u, :], W1[:, bass.ds(e * F, F)])))
            V.wait(get(f"h{u}"))
            put(f"b1{u}", V.done(nc.vector.tensor_copy(bs[:, u, 0:FC], b1[:, bass.ds(e * FC, FC)])))

        def prepare_down(e, u):
            V.wait(get(f"dn{u}"), get(f"yT{u}"))
            put(f"b2{u}", V.done(nc.vector.tensor_copy(bs[:, u, FC:FC + 1], b2[:, bass.ds(e, 1)])))
            put(f"W2{u}", V.done(nc.vector.tensor_copy(W2s[:, u, :], W2[:, bass.ds(e * F, F)])))

        def up(u):
            PE.wait(get(f"xT{u}"), get(f"W1{u}"), get(f"h{u}"))
            hp = ps[:, 2 * u:2 * u + 2, :].rearrange("p b t -> p (b t)")
            for c in range(FC):
                k = PE.done(nc.tensor.matmul(hp[:, c * TILE:(c + 1) * TILE], W1s[:, u, c * P:(c + 1) * P], tl.xT[:, u, :], start=True, stop=True))
                if c % 2:
                    A.wait(k, get(f"b1{u}"), get(f"dn{u}"))
                    for b in (c - 1, c):
                        r = A.done(nc.scalar.activation(h[:, u, b * TILE:(b + 1) * TILE], hp[:, b * TILE:(b + 1) * TILE], ACT.Relu,
                                                        bias=bs[:, u, b:b + 1]))
            put(f"up{u}", k)
            put(f"h{u}", r)

        def down(u):
            PE.wait(get(f"h{u}"), get(f"W2{u}"), get(f"yT{1 - u}"))
            for c in range(FC):
                k = nc.tensor.matmul(ps[:, 5, 0:TILE], W2s[:, u, c * P:(c + 1) * P], h[:, u, c * TILE:(c + 1) * TILE],
                                     start=(c == 0), stop=(c == FC - 1))
            put(f"dn{u}", PE.done(k))
            A.wait(get(f"dn{u}"), get(f"b2{u}"), get(f"out{u}"))
            put(f"yT{u}", A.done(nc.scalar.activation(tl.yT[:, u, :], ps[:, 5, 0:TILE], ACT.Identity, bias=bs[:, u, FC:FC + 1])))

        t_st = tl.run(tiles, experts, prepare_up, prepare_down, up, down)
        n.settle(*t_st)
        return lambda: gather_norm(n, n.y_rows[0], y_all, slots, t_st, "relu_gather", x_all, y_all, stats, x_all)



def att_load_qkv(n, pair, par):
    cols = slice(pair * P, (pair + 1) * P) if isinstance(pair, int) else bass.ds(pair * P, P)
    d = n.att_d[0][par]
    for m, name in enumerate(("L1_attn_Wq", "L1_attn_Wk", "L1_attn_Wv")):
        t = d.mark(n.nc.sync.dma_start(n.att_w[0][:, par, m, :], n.io[name][:, cols]))
    return t


def att_load_o(n, pair, par):
    rows = slice(pair * P, (pair + 1) * P) if isinstance(pair, int) else bass.ds(pair * P, P)
    return n.att_d[1][par].mark(n.nc.sync.dma_start(n.att_w[1][:, par, :], n.io["L1_attn_Wo"][rows, :]))


def attention_weights(n):
    n.att_w = n.sb("att_Wqkv", [P, 2, 3, P]), n.sb("att_Wo", [P, 2, P]), n.sb("att_b", [P, 1])
    n.att_d = [[n.book.dma(f"att_{a}{u}") for u in range(2)] for a in ("w", "wo")]


def attention_loads(n):
    n.t_bo = n.book.dma("att_bo").mark(n.nc.sync.dma_start(n.att_w[2][:, :], n.io["L1_attn_bo"].rearrange("(d a) -> d a", a=1)))
    n.att_ready = {"dq0": att_load_qkv(n, 0, 0), "dq1": att_load_qkv(n, 1, 1), "do0": att_load_o(n, 0, 0), "do1": att_load_o(n, 0, 1)}


def softmax_attention(n, x_all, y_all, stats, finish):
    nc, io, PE, A, V, G, S, ps = n.nc, n.io, n.PE, n.A, n.V, n.G, n.S, n.psum
    NT = x_all.shape[1]
    T = NT * P
    D = 64
    QT = 512
    NU = T // QT
    pairs = io["L1_attn_Wq"].shape[1] // (2 * D)
    scale = 1.0 / float(np.sqrt(D))
    POOL = 704
    SLOT = ((0, 1), (2, 3))
    B_O, B_P, B_M = 4, 5, 6
    with ExitStack() as mem:
        sb = lambda name, shape, dt=F32: n.sb("a_" + name, shape, dt, mem)
        xh, xl = (sb(a, [P, T], F32R) for a in ("xh", "xl"))
        Wqkv, Wo, bo = n.att_w
        Wq, Wk = (sb(a, [P, 2, 2, 2, 2, D], F32R) for a in ("Wq", "Wk"))
        Wv = sb("Wv", [P, 2, 2, P], F32R)
        K1, K2 = (sb(a, [P, 2, 2, T], F32R) for a in ("K1", "K2"))
        M1, M2 = (sb(a, [P, 2, 2, QT], F32R) for a in ("M1", "M2"))
        Vb = sb("Vb", [P, 2, NT, P])
        Pb = sb("Pb", [P, 4, 2 * QT])
        acc = sb("acc", [P, 2, 2 * QT])
        Or = sb("Or", [P, 2, QT])
        On = sb("On", [P, QT])
        mx = sb("mx", [P, 2, 4, NU])
        nm = sb("nm", [P, 2, 4])
        rec = sb("rec", [P, QT])
        full = sb("full", [P, QT])
        state = dict(n.att_ready)

        def get(key):
            if key in state:
                return state[key]
            if n.book.loop is not None:
                return n.prev(key)
            return n.book.events.get("heads", {}).get(key)

        def put(key, tick):
            state[key] = tick
            if n.book.loop is not None:
                n.note(key, tick)
            return tick

        def load_qkv(pair, par):
            S.wait(get(f"Wsplit{par}"))
            put(f"dq{par}", att_load_qkv(n, pair, par))

        def split_job(par, E=G):
            A.wait(get(f"dq{par}"), get(f"Wq{par}"), get(f"Wk{par}"), get(f"Wv{par}"))
            E.wait(get(f"dq{par}"), get("pool_last") if E is G else None)
            for m, W in enumerate((Wq, Wk, Wv)):
                if W is Wv:
                    src, hi, lo = Wqkv[:, par, m, :], Wv[:, par, 0, :], Wv[:, par, 1, :]
                else:
                    src = bcast(Wqkv[:, par, m, :].rearrange("p (h d) -> p h d", h=2).unsqueeze(2), [P, 2, 2, D])
                    hi, lo = W[:, par, 0], W[:, par, 1]
                k = A.done(nc.scalar.activation(hi, src, ACT.Copy))
                E.wait(k)
                k = E.done(E.engine.tensor_tensor(lo, src, hi.bitcast(F32), ALU.subtract))
            put(f"Wsplit{par}", k)
            if E is G:
                put("pool_last", k)

        def project(out, W, x, lhs_is_x=False):
            for k, (a, b) in enumerate(((0, 0), (1, 0), (0, 1))):
                lhs, rhs = (x[a], W[b]) if lhs_is_x else (W[a], x[b])
                t = nc.tensor.matmul(out, lhs, rhs, start=(k == 0), stop=(k == 2))
            return t

        def load_o(pair, par):
            S.wait(get(f"Wo{par}"))
            put(f"do{par}", att_load_o(n, pair, par))

        def low_part(out, rows, hi, bank, E, free):
            src = ps[rows, bank, :]
            if E is G:
                A.wait(get("full_read"))
                k = A.done(nc.scalar.activation(full[rows, :], src, ACT.Copy))
                put(f"B{bank}", k)
                src = full[rows, :]
            else:
                k = Tick(A.counter, A.counter.count, n.book.loop)
            E.wait(k, free, get("pool_last") if E is G else None)
            k = E.done(E.engine.tensor_tensor(out, src, hi.bitcast(F32), ALU.subtract))
            if E is G:
                put("full_read", put("pool_last", k))
            else:
                put(f"B{bank}", k)
            return k

        def keys_job(par, qt, h, bank, E=G):
            at = slice(qt * QT, (qt + 1) * QT)
            PE.wait(get(f"Wsplit{par}"), get(f"B{bank}"))
            k = PE.done(project(ps[:, bank, :], [Wk[:, par, s, h].rearrange("p a d -> p (a d)") for s in range(2)], (xh[:, at], xl[:, at])))
            put(f"Wk{par}", k)
            A.wait(k, get(f"K{par}"))
            put(f"Khigh{par}{h}", A.done(nc.scalar.activation(K1[:, par, h, at], ps[:, bank, :], ACT.Copy)))
            put(f"Kready{par}{h}", low_part(K2[0:D, par, h, at], slice(0, D), K1[0:D, par, h, at], bank, E, get(f"K{par}")))

        def values_job(par, qt, bank):
            PE.wait(get(f"Wsplit{par}"), get(f"B{bank}"))
            for i in range(4):
                k = project(ps[:, bank, i * P:(i + 1) * P], [Wv[:, par, s, :] for s in range(2)],
                            [x[:, (4 * qt + i) * P:(4 * qt + i + 1) * P] for x in (xh, xl)], True)
            k = PE.done(k)
            put(f"Wv{par}", k)
            A.wait(k, get(f"K{par}"))
            k = A.done(nc.scalar.activation(Vb[:, par, 4 * qt:4 * qt + 4, :].rearrange("p a d -> p (a d)"), ps[:, bank, :], ACT.Copy))
            put(f"B{bank}", k)
            put(f"Vready{par}", k)

        def queries_job(par, u, qt, h, bank, E=G):
            PE.wait(get(f"Wsplit{par}"), get(f"B{bank}"))
            k = PE.done(project(ps[:, bank, :], [Wq[:, par, s, h].rearrange("p a d -> p (a d)") for s in range(2)],
                                [x[:, qt * QT:(qt + 1) * QT] for x in (xh, xl)]))
            put(f"Wq{par}", k)
            A.wait(k, get(f"M{u}"))
            A.done(nc.scalar.activation(M1[:, u, h, :], ps[:, bank, :], ACT.Copy))
            A.done(nc.scalar.activation(M2[0:D, u, h, :], ps[0:D, bank, :], ACT.Copy))
            put(f"Q{u}{h}", low_part(M1[D:P, u, h, :], slice(D, P), M1[D:P, u, h, :], bank, E, None))

        def max_job(par, u, k, bank):
            h, qc, quarter = k // 16, (k % 16) // 4, k % 4
            PE.wait(get(f"Q{u}{h}"), get(f"Khigh{par}{h}"), get(f"B{bank}"))
            t = PE.done(nc.tensor.matmul(ps[:, bank, :], M1[:, u, h, qc * P:(qc + 1) * P],
                                         K1[:, par, h, quarter * QT:(quarter + 1) * QT], start=True, stop=True))
            V.wait(t, get(f"mx_read{h}"))
            put(f"mx{h}", V.done(nc.vector.tensor_reduce(mx[:, h, qc, quarter:quarter + 1], ps[:, bank, :], AX.X, ALU.max)))
            put(f"B{bank}", get(f"mx{h}"))

        def max_row_job(u, h, bank):
            negate_job(h)
            row_job(u, h, bank)

        def negate_job(h):
            V.wait(get(f"mx{h}"), get(f"nm{h}"))
            k = V.done(nc.vector.tensor_reduce(nm[:, h, :], mx[:, h, :, :], AX.X, ALU.max, negate=True))
            put(f"mx_read{h}", k)

        def row_job(u, h, bank):
            PE.wait(get(f"mx_read{h}"), get(f"B{bank}"))
            for qc in range(4):
                k = nc.tensor.matmul(ps[D:D + 1, bank, qc * P:(qc + 1) * P], nm[:, h, qc:qc + 1], n.ident[:, :], start=True, stop=True)
            k = PE.done(k)
            put(f"nm{h}", k)
            A.wait(k)
            k = A.done(nc.scalar.activation(M2[D:D + 1, u, h, :], ps[D:D + 1, bank, :], ACT.Copy))
            put(f"B{bank}", k)
            put(f"M2ready{u}{h}", k)

        def scores(step, par, u, kc):
            b = SLOT[step % 2]
            PE.wait(get(f"slot{step % 2}"), get(f"M2ready{u}0"), get(f"M2ready{u}1"), get(f"Kready{par}0"), get(f"Kready{par}1"))
            for h in range(2):
                at = slice(kc * P, (kc + 1) * P)
                nc.tensor.matmul(ps[:, b[h], :], K1[:, par, h, at], M1[:, u, h, :], start=True, stop=False)
                k = nc.tensor.matmul(ps[:, b[h], :], K2[0:D + 1, par, h, at], M2[0:D + 1, u, h, :], start=False, stop=True)
            k = PE.done(k)
            put(f"M{u}", k)
            put(f"Klast{par}", k)
            buf = step % 4
            A.wait(k, get(f"pv{buf}"), get(f"addv{buf}"), get(f"addg{buf}"))
            k = A.done(nc.scalar.activation(Pb[:, buf, :], ps[:, b[0]:b[0] + 2, :].rearrange("p a b -> p (a b)"), ACT.Exp, scale=scale))
            put(f"slot{step % 2}", k)
            put(f"exp{buf}", k)

        def weigh(step, par, u, kc):
            buf = step % 4
            PE.wait(get(f"exp{buf}"), get(f"Vready{par}"))
            if kc == 0:
                PE.wait(get("B_O"))
            for h in range(2):
                k = nc.tensor.matmul(ps[h * D:(h + 1) * D, B_O, :], Vb[:, par, kc, h * D:(h + 1) * D], Pb[:, buf, h * QT:(h + 1) * QT],
                                     start=(kc == 0), stop=(kc == NT - 1))
            k = PE.done(k)
            put(f"pv{buf}", k)
            if kc == NT - 1:
                A.wait(k, get(f"Or{u}"))
                k = A.done(nc.scalar.activation(Or[:, u, :], ps[:, B_O, :], ACT.Copy))
                put("B_O", k)
                put(f"Oraw{u}", k)
            if kc == 0:
                return
            for q, at, key, op in ((V, slice(POOL, 2 * QT), "addv", nc.vector.tensor_tensor),
                                   (G, slice(0, POOL), "addg", nc.gpsimd.tensor_tensor)):
                q.wait(get(f"exp{buf}"), get(f"{key}"), get(f"sums{u}") if kc == 1 else None)
                first = Pb[:, (step - 1) % 4, at] if kc == 1 else acc[:, u, at]
                if q is G:
                    q.wait(get("pool_last"))
                k = q.done(op(acc[:, u, at], first, Pb[:, buf, at], ALU.add))
                if q is G:
                    put("pool_last", k)
                put(key, k)
                put(f"{key}{buf}", k)
                if kc == 1:
                    put(f"{key}{(step - 1) % 4}", k)

        def sums_job(u, bank):
            PE.wait(get("addv"), get("addg"), get(f"B{bank}"))
            for h in range(2):
                k = nc.tensor.matmul(ps[h * D:(h + 1) * D, bank, :], n.ones[:, 0:D], acc[:, u, h * QT:(h + 1) * QT], start=True, stop=True)
            put(f"sums{u}", PE.done(k))

        def reciprocal_job(u, part, bank):
            at = slice(part * P, (part + 1) * P)
            V.wait(get(f"sums{u}"), get("On"))
            put("rec", V.done(nc.vector.reciprocal(rec[:, at], ps[:, bank, at])))
            put(f"B{bank}", get("rec"))

        def normalise_job(u):
            V.wait(get("rec"), get(f"Oraw{u}"), get("On_free"))
            k = V.done(nc.vector.tensor_tensor(On[:, :], rec[:, :], Or[:, u, :], ALU.mult))
            put(f"Or{u}", k)
            put("On", k)

        def output_job(par, qt, bank):
            PE.wait(get("On"), get(f"B{bank}"), get(f"do{par}"))
            k = PE.done(nc.tensor.matmul(ps[:, bank, :], Wo[:, par, :], On[:, :], start=True, stop=True))
            put("On_free", k)
            put(f"Wo{par}", k)
            yq = y_all[:, 4 * qt:4 * qt + 4, :]
            V.wait(k, get(f"y{qt}"))
            k = V.done(nc.vector.tensor_tensor(yq, ps[:, bank, :].rearrange("p (a d) -> p a d", a=4), yq, ALU.add))
            put(f"B{bank}", k)
            put(f"y{qt}", k)

        t_one = (V.done(nc.vector.memset(K2[D:D + 1, 0].bitcast(F32), 1.0)),
                 A.done(nc.scalar.activation(K2[D:D + 1, 1], bcast(n.ones[D:D + 1, 0:1].unsqueeze(2), [1, 2, T]), ACT.Copy)))
        split_job(0, V)
        V.done(nc.vector.memset(acc[:, 1, :], 1.0))
        V.done(nc.vector.memset(Or[:, 1, :], 0.0))
        t_x = finish()
        V.wait(n.t_bo, *t_x)
        V.done(nc.vector.tensor_copy(y_all[:, :, :], bcast(bo[:, :].unsqueeze(2), [P, NT, P])))
        for g in range(NU):
            PE.wait(t_x[g], n.t_const)
            for i in range(GROUP):
                k = PE.done(nc.tensor.transpose(ps[:, g, i * P:(i + 1) * P], x_all[:, GROUP * g + i, :], n.ident[:, :]))
            at = slice(g * QT, (g + 1) * QT)
            A.wait(k)
            k = A.done(nc.scalar.activation(xh[:, at], ps[:, g, :], ACT.Copy))
            V.wait(k)
            put(f"B{g}", V.done(nc.vector.tensor_tensor(xl[:, at], ps[:, g, :], xh[:, at].bitcast(F32), ALU.subtract)))
        split_job(1)
        PE.wait(*t_one, *(get(f"B{g}") for g in range(NU)))
        for h in range(2):
            queries_job(0, 0, 0, h, 4 + h, V)
        for h in range(2):
            for qt in range(NU):
                keys_job(0, qt, h, (6, 7, 0, 1)[qt], V)
        for k in range(8 * NU):
            max_job(0, 0, k, (2, 3, 6, 7)[k % 4])
            if k % 8 == 7:
                values_job(0, k // 8, 4 + k // 8 % 2)
            if k == 20:
                max_row_job(0, 0, 0)
        max_row_job(0, 1, 1)
        STEPS = NT

        def body(i, last):
            units = 2 * NU
            for g in range(units):
                a, qt, u = g // NU, g % NU, g % 2
                more_q = not (last and g == units - 1)
                more_k = not (last and a == 1)
                ga, gq = ((g + 1) // NU) % 2, (g + 1) % NU
                pu, pqt, pa = 1 - u, (g - 1) % NU, ((g - 1) % units) // NU
                for kc in range(STEPS):
                    step = g * STEPS + kc

                    def maxima(point):
                        k = 3 * (kc - 3) + point
                        if more_q and 0 <= k < 8 * NU:
                            max_job(ga, 1 - u, k, B_M + k % 2)

                    maxima(0)
                    if more_q and kc == 14:
                        row_job(1 - u, 1, B_P)
                    if kc < STEPS - 1:
                        scores(step + 1, a, u, kc + 1)
                    elif more_q:
                        scores(step + 1, ga, 1 - u, 0)
                    if more_q and kc in (0, 2):
                        queries_job(ga, 1 - u, gq, kc // 2, B_P)
                    if kc == 1:
                        sums_job(pu, B_M + 1)
                    if kc in (1, 2):
                        for part in (2 * kc - 2, 2 * kc - 1):
                            reciprocal_job(pu, part, B_M + 1)
                    if more_k and kc in (3, 7):
                        keys_job(1 - a, qt, kc // 4, B_P)
                    if kc == 4:
                        normalise_job(pu)
                    if kc == 5:
                        output_job(pa, pqt, B_P)
                    if more_k and kc == 9:
                        values_job(1 - a, qt, B_P)
                    if not last and qt == NU - 1 and kc == 12:
                        split_job(a)
                    maxima(1)
                    if more_q and kc == 9:
                        negate_job(0)
                    if more_q and kc == 13:
                        negate_job(1)
                    if more_q and kc == 11:
                        row_job(1 - u, 0, B_P)
                    weigh(step, a, u, kc)
                    maxima(2)
                if qt == NU - 1:
                    put(f"K{a}", get(f"Klast{a}"))
                if qt == 0:
                    if not last:
                        load_qkv(2 * i + a + 2, a)
                    if not (last and a == 1):
                        load_o(2 * i + a + 1, 1 - a)

        PE.wait(get("do1"))
        n.settle()
        scores(0, 0, 0, 0)
        n.settle()
        state.clear()
        n.book.run("heads", pairs // 2 - 1, lambda i: (state.clear(), body(i, False)))
        state.clear()
        body(pairs // 2 - 1, True)
        sums_job(1, B_M + 1)
        for part in range(4):
            reciprocal_job(1, part, B_M + 1)
        normalise_job(1)
        output_job(1, NU - 1, B_P)
        ready = [get(f"y{qt}") for qt in range(NU)]
        n.settle()
        return lambda: attention_norm(n, x_all, y_all, stats, ready)


def attention_norm(n, x_all, y_all, stats, ready):
    nc, PE, V, ps = n.nc, n.PE, n.V, n.psum
    t_out = []
    for qt, t_y in enumerate(ready):
        PE.wait(t_y)
        for i in range(GROUP):
            k = PE.done(nc.tensor.transpose(ps[:, qt, i * P:(i + 1) * P], y_all[:, GROUP * qt + i, :], n.ident[:, :]))
        at = slice(GROUP * qt, GROUP * qt + GROUP)
        V.wait(k)
        t = V.done(nc.vector.tensor_tensor(y_all[:, at, :], ps[:, qt, :].rearrange("p (a d) -> p a d", a=GROUP), x_all[:, at, :], ALU.add))
        t_out.append(norm_group(n, qt, y_all, stats, t, x_all))
    return t_out



def gated_experts(n, x_all, y_all, stats, finish):
    nc, io, PE, A, V, G, S, ps = n.nc, n.io, n.PE, n.A, n.V, n.G, n.S, n.psum
    E, _, F = io["L1_ffn_w1_eDF"].shape
    FC = -(-F // P)
    FP, FL = FC * P, F - (FC - 1) * P
    NT = x_all.shape[1]
    tiles = n.tiles
    QT = 512
    with ExitStack() as mem:
        sb = lambda name, shape, dt=F32: n.sb("g_" + name, shape, dt, mem)
        w13 = sb("w13", [P, E, 2, F])
        w2 = sb("w2", [P, E * FC * P])
        w2v = w2[:, :].rearrange("p (e c d) -> p e c d", e=E, c=FC)
        ws13 = sb("ws13", [P, 2, FP])
        ws2 = sb("ws2", [P, FC, P])
        rT = sb("rT", [P, E])
        w13s = sb("w13s", [P, 2, 2, FP])
        w2s = sb("w2s", [P, 2, FP])
        lo = FL // 32 * 32
        for part in (w2v[lo:P, :, FC - 1, :], ws2[lo:P, FC - 1, :], ws13[:, :, F:FP], w13s[:, :, :, F:FP]):
            t_pad = V.done(nc.vector.memset(part, 0.0))
        d_w = [n.book.dma(f"gated_weights{i}") for i in range(3)]
        S.wait(t_pad)
        full = (FC - 1) * P
        t_w = [None] * 3
        for part, dst, src in (
            (0, rT[:, :], io["L1_ffn_router_DE"]),
            (1, ws13[:, 0, 0:F], io["L1_ffn_ws1_DF"]), (1, ws13[:, 1, 0:F], io["L1_ffn_ws3_DF"]),
            (1, ws2[:, 0:FC - 1, :], io["L1_ffn_ws2_FD"][0:full, :].rearrange("(c p) d -> p c d", p=P)),
            (1, ws2[0:FL, FC - 1, :], io["L1_ffn_ws2_FD"][full:F, :]),
            (2, w13[:, :, 0, :], io["L1_ffn_w1_eDF"].rearrange("e p f -> p e f")),
            (2, w13[:, :, 1, :], io["L1_ffn_w3_eDF"].rearrange("e p f -> p e f")),
            (2, w2v[0:FL, :, FC - 1, :], io["L1_ffn_w2_eFD"][:, full:F, :].rearrange("e p d -> p e d")),
            *((2, w2v[:, :, c, :], io["L1_ffn_w2_eFD"][:, c * P:(c + 1) * P, :].rearrange("e p d -> p e d")) for c in range(FC - 1)),
        ):
            t_w[part] = d_w[part].mark(nc.sync.dma_start(dst, src))
        t_x = finish()
        slots, experts = n.slots, sb("experts", [1, tiles], I32)
        xT = sb("xT", [P, NT * P])
        xg = sb("xg", [P, NT, P])
        with ExitStack() as tmp:
            tb = lambda name, shape, dt=F32: n.sb("gr_" + name, shape, dt, tmp)
            gate = tb("gate", [P, NT])
            PE.wait(t_w[0])
            t_lg, logits = route(n, x_all, xT, rT[:, :], t_x, 2)
            mx, hot, t_mx, t_hot = top_one(n, tb, logits, t_lg)
            A.wait(t_mx)
            t = A.done(nc.scalar.activation(gate[:, :], mx[:, :], ACT.Sigmoid))
            G.wait(t)
            t_xg = G.done(nc.gpsimd.tensor_tensor(xg[:, :, :], x_all[:, :, :], bcast(gate[:, :].unsqueeze(2), [P, NT, P]), ALU.mult))
            t_slots, t_te = dispatch(n, tb, hot, t_hot, tiles, 3, slots, experts)
            n.settle()
        t_sc = scatter(n, n.x_rows[1], xg, slots, (t_slots, t_xg, n.t_zero), "gated_scatter")

        sg = sb("sg", [P, FC, QT])
        hh = sb("hh", [P, 2, FC, QT])
        yTs = sb("yTs", [P, 2, QT])
        chunks = NT * P // QT
        t_hh, t_dn, t_yT, t_tr, t_y = ([None] * chunks for _ in range(5))
        read1, read3 = [None] * FC, [None] * FC

        def shared_up(i):
            u = i % 2
            at = slice(i * QT, (i + 1) * QT)
            ks = []
            for m, read in ((0, read1), (1, read3)):
                for c in range(FC):
                    PE.wait(read[c])
                    ks.append(PE.done(nc.tensor.matmul(ps[:, FC * m + c, :], ws13[:, m, c * P:(c + 1) * P], xT[:, at], start=True, stop=True)))
            for c in range(FC):
                A.wait(ks[c], read3[c])
                k = A.done(nc.scalar.activation(sg[:, c, :], ps[:, c, :], ACT.Sigmoid))
                V.wait(k)
                read1[c] = V.done(nc.vector.tensor_tensor(sg[:, c, :], ps[:, c, :], sg[:, c, :], ALU.mult))
                V.wait(read1[c], ks[FC + c], t_dn[i - 2] if i > 1 else None)
                read3[c] = V.done(nc.vector.tensor_tensor(hh[:, u, c, :], ps[:, FC + c, :], sg[:, c, :], ALU.mult))
            t_hh[i] = read3[FC - 1]

        def shared_down(i):
            u = i % 2
            PE.wait(t_hh[i], t_yT[i - 1] if i else None)
            for c in range(FC):
                k = nc.tensor.matmul(ps[:, 6, :], ws2[:, c, :], hh[:, u, c, :], start=(c == 0), stop=(c == FC - 1))
            t_dn[i] = PE.done(k)
            A.wait(t_dn[i], t_tr[i - 2] if i > 1 else None)
            t_yT[i] = A.done(nc.scalar.activation(yTs[:, u, :], ps[:, 6, :], ACT.Copy))

        def shared_out(i):
            u = i % 2
            PE.wait(t_yT[i], t_y[i - 1] if i else None)
            for t in range(GROUP):
                k = PE.done(nc.tensor.transpose(ps[:, 7, t * P:(t + 1) * P], yTs[:, u, t * P:(t + 1) * P], n.ident[:, :]))
            t_tr[i] = k
            V.wait(k)
            at = slice(i * GROUP, (i + 1) * GROUP)
            t_y[i] = V.done(nc.vector.tensor_tensor(y_all[:, at, :], ps[:, 7, :].rearrange("p (a d) -> p a d", a=GROUP), x_all[:, at, :], ALU.add))

        PE.wait(t_w[1])
        shared_up(0)
        for i in range(chunks):
            if i + 1 < chunks:
                shared_up(i + 1)
            if i:
                shared_out(i - 1)
            shared_down(i)
        shared_out(chunks - 1)

        sig = sb("sig", [P, FC * TILE])
        h = sb("h", [P, 2, FC * TILE])
        n.settle()
        tl = Tiles(n, sb, "gated_tiles", n.x_rows[1], n.y_rows[1], 6, 6)
        get, put = tl.c.get, tl.c.put
        S.wait(t_sc)
        V.wait(t_w[2], t_te)

        def prepare_up(e, u):
            V.wait(get(f"up{u}"))
            put(f"w13{u}", V.done(nc.vector.tensor_copy(w13s[:, u, :, 0:F], w13[:, bass.ds(e, 1), :, :].rearrange("p a b f -> p (a b) f"))))

        def prepare_down(e, u):
            V.wait(get(f"dn{u}"))
            put(f"w2{u}", V.done(nc.vector.tensor_copy(w2s[:, u, :], w2[:, bass.ds(e * FP, FP)])))

        def up(u):
            PE.wait(get(f"xT{u}"), get(f"w13{u}"), get("gated"))
            hp = ps[:, 0:6, :].rearrange("p b t -> p (b t)")
            at = [3 * u * 512 + b * TILE for b in range(6)]
            ks = [PE.done(nc.tensor.matmul(hp[:, at[b]:at[b] + TILE], w13s[:, u, b // FC, (b % FC) * P:(b % FC + 1) * P], tl.xT[:, u, :],
                                           start=True, stop=True)) for b in range(2 * FC)]
            put(f"up{u}", ks[-1])
            up1, up3 = hp[:, at[0]:at[0] + FC * TILE], hp[:, at[FC]:at[FC] + FC * TILE]
            A.wait(ks[-1], get("gated"))
            k = A.done(nc.scalar.activation(sig[:, :], up1, ACT.Sigmoid))
            V.wait(k)
            k = V.done(nc.vector.tensor_tensor(sig[:, :], up1, sig[:, :], ALU.mult))
            V.wait(k, get(f"dn{u}"))
            put("gated", put(f"h{u}", V.done(nc.vector.tensor_tensor(h[:, u, :], up3, sig[:, :], ALU.mult))))

        def down(u):
            PE.wait(get(f"h{u}"), get(f"w2{u}"), get(f"yT{1 - u}"))
            for c in range(FC):
                k = nc.tensor.matmul(ps[:, 7, 0:TILE], w2s[:, u, c * P:(c + 1) * P], h[:, u, c * TILE:(c + 1) * TILE],
                                     start=(c == 0), stop=(c == FC - 1))
            put(f"dn{u}", PE.done(k))
            A.wait(get(f"dn{u}"), get(f"out{u}"))
            put(f"yT{u}", A.done(nc.scalar.activation(tl.yT[:, u, :], ps[:, 7, 0:TILE], ACT.Copy)))

        t_st = tl.run(tiles, experts, prepare_up, prepare_down, up, down)
        t = gather_norm(n, n.y_rows[1], xg, slots, (*t_st, t_sc), "gated_gather", y_all, y_all, stats, x_all)
        n.settle()
        return t


def program(nc, known, io, out):
    with ExitStack() as ctx:
        n = Net(nc, ctx, known, io)
        NT = io["L0_attn_hidden_states"].shape[1] // P
        E = io["L0_ffn_W1"].shape[0]
        n.tiles = NT * P // TILE + E
        n.experts = E
        constants(n)
        x_all = n.sb("x_all", [P, NT, P])
        y_all = n.sb("y_all", [P, NT, P])
        stats = n.sb("stats", [P, NT, 6])
        n.mv = n.sb("mv", [P, NT, 2])
        n.sd = n.sb("sd", [P, NT])
        n.warm = n.sb("warm", [P, 1])
        n.x_rows = [nc.dram_tensor(f"x_rows{i}", (n.tiles * TILE, P), F32, kind="Internal").ap() for i in range(2)]
        n.y_rows = [nc.dram_tensor(f"y_rows{i}", (n.tiles * TILE, P), F32, kind="Internal").ap() for i in range(2)]
        n.G.wait(n.t_const)
        zero = n.sb("zero", [P, P])
        t = n.G.done(nc.gpsimd.memset(zero[:, :], 0.0))
        d_z = n.book.dma("zero_rows")
        n.A.wait(t)
        for i in range(2):
            n.t_zero = d_z.mark(nc.scalar.dma_start(n.x_rows[i].rearrange("(t p) d -> p t d", p=P),
                                                    bcast(zero[:, :].unsqueeze(1), [P, n.tiles * TP, P])))
        d_in = n.book.dma("x_in")
        t_in = d_in.mark(nc.sync.dma_start(x_all[:, :, :], io["L0_attn_hidden_states"].rearrange("b (t p) d -> p (b t) d", p=P)))
        n.V.wait(t_in)
        n.slots = n.sb("slots", [P, NT], U32)
        attention_weights(n)
        n.prefetch = lambda: (relu_loads(n), attention_loads(n))
        groups = range(NT // GROUP)
        with ExitStack() as relu_mem:
            relu_weights(n, relu_mem)
            finish = ttt_attention(n, x_all, y_all, stats, [t_in] * len(groups))
            finish = relu_experts(n, x_all, y_all, stats, finish)
        finish = softmax_attention(n, x_all, y_all, stats, finish)
        t = gated_experts(n, x_all, y_all, stats, finish)
        d_out = n.book.dma("out")
        for g in groups:
            n.S.wait(t[g], n.t_zero)
            t_out = d_out.mark(nc.sync.dma_start(out.rearrange("b (g a p) d -> g p (b a) d", p=P, a=GROUP)[g],
                                                 x_all[:, g * GROUP:(g + 1) * GROUP, :]))
        n.S.wait(t_out)
        return n.book.found


_INS = ['L0_attn_hidden_states', 'L0_attn_qkv_w', 'L0_attn_q_norm_w', 'L0_attn_k_norm_w', 'L0_attn_lr_proj_w',
        'L0_attn_lr_proj_b', 'L0_attn_w0', 'L0_attn_w1', 'L0_attn_w2', 'L0_ffn_router_w', 'L0_ffn_W1', 'L0_ffn_b1',
        'L0_ffn_W2', 'L0_ffn_b2', 'L1_attn_Wq', 'L1_attn_Wk', 'L1_attn_Wv', 'L1_attn_Wo', 'L1_attn_bo',
        'L1_ffn_router_DE', 'L1_ffn_w1_eDF', 'L1_ffn_w3_eDF', 'L1_ffn_w2_eFD', 'L1_ffn_ws1_DF', 'L1_ffn_ws3_DF',
        'L1_ffn_ws2_FD']


def kernel(**inputs):
    import concourse.bacc as _bacc
    from concourse.bass_utils import run_bass_kernel_spmd as _run

    arrays = {f"in_{name}_dram": np.ascontiguousarray(inputs[name]) for name in _INS}
    known = {}
    for _ in range(2):
        nc = _bacc.Bacc("TRN2", target_bir_lowering=False, num_devices=1)
        io = {name: nc.dram_tensor(f"in_{name}_dram", arrays[f"in_{name}_dram"].shape, F32, kind="ExternalInput").ap()
              for name in _INS}
        out = nc.dram_tensor("out_0_dram", (1, 2048, 128), F32, kind="ExternalOutput").ap()
        known = program(nc, known, io, out)
    r = _run(nc, [arrays], core_ids=[0])
    return r.results[0]["out_0_dram"]
```
